# Optimizing a Trainium2 kernel written in Bass

```python
import numpy as np
import jax
import jax.numpy as jnp

def _softmax(x, axis=-1):
    return jax.nn.softmax(x, axis=axis)

def _gelu(x):
    return jax.nn.gelu(x, approximate=True)

def _silu(x):
    return jax.nn.silu(x)

def _sigmoid(x):
    return jax.nn.sigmoid(x)

def _layernorm(x, axis=-1, eps=1e-05):
    m = jnp.mean(x, axis=axis, keepdims=True)
    v = jnp.var(x, axis=axis, keepdims=True)
    return (x - m) / jnp.sqrt(v + eps)

def _scatter_add(tgt, idx, src, axis=0):
    return tgt.at[idx].add(src)

def _segment_sum(src, seg, n):
    return jax.ops.segment_sum(src, seg, n)
kernel_name = 'mk_hybrid_d2_jaxref_r8_9fd0dd'

def setup_inputs(seed: int=0):
    np.random.seed(seed)
    _w = jnp.asarray

    def _L0_attn_a_setup():
        import jax, jax.numpy as jnp
        import numpy as np
        LN_EPS = 1e-05
        key = jax.random.key(seed)
        ks = jax.random.split(key, 8)
        B, L, d_model = (2, 256, 128)
        d_inner, d_state, dt_rank, d_conv = (256, 16, 64, 4)
        f32 = jnp.float32
        A_init = jnp.broadcast_to(jnp.arange(1, d_state + 1, dtype=f32), (d_inner, d_state))
        return {'x': jax.random.normal(ks[0], (B, L, d_model), f32), 'norm_g': jnp.ones((d_model,), f32), 'norm_b': jnp.zeros((d_model,), f32), 'in_w': jax.random.normal(ks[1], (2 * d_inner, d_model), f32) / np.sqrt(d_model), 'conv_w': jax.random.normal(ks[2], (d_inner, 1, d_conv), f32) / np.sqrt(d_conv), 'conv_b': jnp.zeros((d_inner,), f32), 'xproj_w': jax.random.normal(ks[3], (dt_rank + 2 * d_state, d_inner), f32) / np.sqrt(d_inner), 'dt_w': jax.random.normal(ks[4], (d_inner, dt_rank), f32) / np.sqrt(dt_rank), 'dt_b': jax.random.uniform(ks[5], (d_inner,), f32, np.log(0.0001), np.log(0.1)), 'A_log': jnp.log(A_init), 'D': jnp.ones((d_inner,), f32), 'out_w': jax.random.normal(ks[6], (d_model, d_inner), f32) / np.sqrt(d_inner)}
    _L0_attn_a_in = _L0_attn_a_setup()

    def _L0_attn_b_setup():
        import jax, jax.numpy as jnp
        import numpy as np
        DIM = 128
        DIM_HEAD = 128
        HEADS = 8
        DIM_INNER = DIM_HEAD * HEADS
        key = jax.random.key(seed)
        k_x, k_qkv, k_out = jax.random.split(key, 3)
        x = jax.random.normal(k_x, (2, 256, DIM), dtype=jnp.float32)
        gamma = jnp.ones((DIM,), dtype=jnp.float32)
        w_qkv = jax.random.uniform(k_qkv, (DIM_INNER * 3, DIM), dtype=jnp.float32, minval=-1.0, maxval=1.0) / np.sqrt(DIM)
        w_out = jax.random.uniform(k_out, (DIM, DIM_INNER), dtype=jnp.float32, minval=-1.0, maxval=1.0) / np.sqrt(DIM_INNER)
        return {'x': x, 'gamma': gamma, 'w_qkv': w_qkv, 'w_out': w_out}
    _L0_attn_b_in = _L0_attn_b_setup()

    def _L0_ffn_setup():
        import jax, jax.numpy as jnp
        import numpy as np
        B, S, D, F, E = (1, 128, 128, 512, 8)
        EPS = 1e-05

        def _sublayer(xs, g, b, W1e, b1e, W2e, b2e):
            mu = jnp.mean(xs, axis=-1, keepdims=True)
            var = jnp.mean(jnp.square(xs - mu), axis=-1, keepdims=True)
            h = (xs - mu) * jax.lax.rsqrt(var + EPS) * g + b
            return xs + jax.nn.relu(h @ W1e.T + b1e) @ W2e.T + b2e
        key = jax.random.key(seed)
        ks = jax.random.split(key, 4)
        x = jax.random.normal(ks[0], (B, S, D), jnp.float32)
        centroids = jax.random.normal(ks[1], (E, D), jnp.float32) * 0.1
        gamma = jnp.ones((E, D), jnp.float32)
        beta = jnp.zeros((E, D), jnp.float32)
        W1 = jax.random.normal(ks[2], (E, F, D), jnp.float32) * 0.02
        b1 = jnp.zeros((E, F), jnp.float32)
        W2 = jax.random.normal(ks[3], (E, D, F), jnp.float32) * 0.02
        b2 = jnp.zeros((E, D), jnp.float32)
        return {'x': x, 'centroids': centroids, 'gamma': gamma, 'beta': beta, 'W1': W1, 'b1': b1, 'W2': W2, 'b2': b2}
    _L0_ffn_in = _L0_ffn_setup()

    def _L1_attn_a_setup():
        import jax, jax.numpy as jnp
        import numpy as np
        N_HEAD = 16
        EPS = 1e-06

        def _rotate_half(x):
            d = x.shape[-1] // 2
            return jnp.concatenate((-x[..., d:], x[..., :d]), axis=-1)

        def _rms_norm(x, w, eps=EPS):
            d = x.shape[-1]
            rms = jnp.linalg.norm(x, axis=-1, keepdims=True) * d ** (-0.5)
            return w * (x / (rms + eps))
        key = jax.random.key(seed)
        ks = jax.random.split(key, 3)
        B, T, C = (4, 256, 128)
        x = jax.random.normal(ks[0], (B, T, C), dtype=jnp.float32)
        W_kqv = jax.random.normal(ks[1], (3 * C, C), dtype=jnp.float32) * C ** (-0.5)
        W_proj = jax.random.normal(ks[2], (C, C), dtype=jnp.float32) * C ** (-0.5)
        D = C // N_HEAD
        q_norm_w = jnp.ones((D,), dtype=jnp.float32)
        k_norm_w = jnp.ones((D,), dtype=jnp.float32)
        return {'x': x, 'W_kqv': W_kqv, 'W_proj': W_proj, 'q_norm_w': q_norm_w, 'k_norm_w': k_norm_w}
    _L1_attn_a_in = _L1_attn_a_setup()

    def _L1_attn_b_setup():
        import jax, jax.numpy as jnp
        import numpy as np
        D_MODEL = 128
        D_STATE = 64
        D_CONV = 4
        EXPAND = 2
        INNER = EXPAND * D_STATE
        PROJ = D_STATE + 2 * INNER
        B, L = (8, 512)
        EPS = 0.0001

        def _ssm_forward(x, conv_w, conv_b, in_proj_w, in_proj_b, A_log, out_proj_w, out_proj_b):
            bsz, L_in, _ = x.shape
            pad = (D_CONV - 1) // 2
            xc = jnp.transpose(x, (0, 2, 1))
            xc = jax.lax.conv_general_dilated(xc, conv_w, window_strides=(1,), padding=[(pad, pad)], dimension_numbers=('NCH', 'OIH', 'NCH'), feature_group_count=D_MODEL)
            xc = xc + conv_b[None, :, None]
            Lc = xc.shape[2]
            if Lc < L_in:
                xc = jnp.pad(xc, ((0, 0), (0, 0), (0, L_in - Lc)))
            elif Lc > L_in:
                xc = xc[:, :, :L_in]
            xc = jnp.transpose(xc, (0, 2, 1))
            proj = xc @ in_proj_w.T + in_proj_b
            delta = proj[..., :D_STATE]
            B_in = proj[..., D_STATE:D_STATE + INNER]
            C = proj[..., D_STATE + INNER:]
            n_groups = INNER // D_STATE
            B_in = B_in.reshape(bsz, L_in, D_STATE, n_groups).mean(axis=-1)
            C = C.reshape(bsz, L_in, D_STATE, n_groups).mean(axis=-1)
            A = -jnp.exp(A_log)[None, None, :]
            delta = jax.nn.softplus(delta)
            dA = delta * A
            A_bar = jnp.exp(dA)
            A_safe = jnp.where(jnp.abs(A) < EPS, EPS * jnp.sign(A) + EPS, A)
            scale = (A_bar - 1.0) / A_safe
            taylor = 1.0 + dA / 2.0 + dA * dA / 6.0
            scale = jnp.where(jnp.abs(A) < EPS, taylor, scale)
            B_bar = scale * B_in

            def comb(e1, e2):
                a1, b1 = e1
                a2, b2 = e2
                return (a1 * a2, a2 * b1 + b2)
            _, h = jax.lax.associative_scan(comb, (A_bar, B_bar), axis=1)
            y_state = C * h
            return y_state @ out_proj_w.T + out_proj_b
        key = jax.random.key(seed)
        ks = jax.random.split(key, 6)
        x = jax.random.normal(ks[0], (B, L, D_MODEL), dtype=jnp.float32)
        conv_w = jax.random.normal(ks[1], (D_MODEL, 1, D_CONV), dtype=jnp.float32) / np.sqrt(D_CONV)
        conv_b = jnp.zeros((D_MODEL,), dtype=jnp.float32)
        in_proj_w = jax.random.normal(ks[2], (PROJ, D_MODEL), dtype=jnp.float32) / np.sqrt(D_MODEL)
        in_proj_b = jnp.zeros((PROJ,), dtype=jnp.float32)
        A_log = jax.random.normal(ks[3], (D_STATE,), dtype=jnp.float32) * 0.1
        out_proj_w = jax.random.normal(ks[4], (D_MODEL, D_STATE), dtype=jnp.float32) / np.sqrt(D_STATE)
        out_proj_b = jnp.zeros((D_MODEL,), dtype=jnp.float32)
        return {'x': x, 'conv_w': conv_w, 'conv_b': conv_b, 'in_proj_w': in_proj_w, 'in_proj_b': in_proj_b, 'A_log': A_log, 'out_proj_w': out_proj_w, 'out_proj_b': out_proj_b}
    _L1_attn_b_in = _L1_attn_b_setup()

    def _L1_ffn_setup():
        import jax, jax.numpy as jnp
        import numpy as np
        B, T, D = (2, 128, 128)
        H, DK, K = (8, 128, 8)
        NKEYS = 32
        NEXP = NKEYS * NKEYS

        def _rmsnorm(x, w, eps=1e-06):
            inv = jax.lax.rsqrt(jnp.mean(x * x, axis=-1, keepdims=True) + eps)
            return x * inv * w
        key = jax.random.key(seed)
        ks = jax.random.split(key, 5)
        return {'x': jax.random.normal(ks[0], (B, T, D), jnp.float32), 'w_q': jax.random.normal(ks[1], (H * 2 * DK, D), jnp.float32) * 0.02, 'keys': jax.random.normal(ks[2], (H, NKEYS, 2, DK), jnp.float32) * 0.02, 'expert_down': jax.random.normal(ks[3], (NEXP, D), jnp.float32) * 0.02, 'expert_up': jax.random.normal(ks[4], (NEXP, D), jnp.float32) * 0.02, 'norm_w': jnp.ones((D,), jnp.float32)}
    _L1_ffn_in = _L1_ffn_setup()
    _d = {'L0_attn_a_x': _L0_attn_a_in['x'], 'L0_attn_a_norm_g': _L0_attn_a_in['norm_g'], 'L0_attn_a_norm_b': _L0_attn_a_in['norm_b'], 'L0_attn_a_in_w': _L0_attn_a_in['in_w'], 'L0_attn_a_conv_w': _L0_attn_a_in['conv_w'], 'L0_attn_a_conv_b': _L0_attn_a_in['conv_b'], 'L0_attn_a_xproj_w': _L0_attn_a_in['xproj_w'], 'L0_attn_a_dt_w': _L0_attn_a_in['dt_w'], 'L0_attn_a_dt_b': _L0_attn_a_in['dt_b'], 'L0_attn_a_A_log': _L0_attn_a_in['A_log'], 'L0_attn_a_D': _L0_attn_a_in['D'], 'L0_attn_a_out_w': _L0_attn_a_in['out_w'], 'L0_attn_b_gamma': _L0_attn_b_in['gamma'], 'L0_attn_b_w_qkv': _L0_attn_b_in['w_qkv'], 'L0_attn_b_w_out': _L0_attn_b_in['w_out'], 'L0_ffn_centroids': _L0_ffn_in['centroids'], 'L0_ffn_gamma': _L0_ffn_in['gamma'], 'L0_ffn_beta': _L0_ffn_in['beta'], 'L0_ffn_W1': _L0_ffn_in['W1'], 'L0_ffn_b1': _L0_ffn_in['b1'], 'L0_ffn_W2': _L0_ffn_in['W2'], 'L0_ffn_b2': _L0_ffn_in['b2'], 'L1_attn_a_W_kqv': _L1_attn_a_in['W_kqv'], 'L1_attn_a_W_proj': _L1_attn_a_in['W_proj'], 'L1_attn_a_q_norm_w': _L1_attn_a_in['q_norm_w'], 'L1_attn_a_k_norm_w': _L1_attn_a_in['k_norm_w'], 'L1_attn_b_conv_w': _L1_attn_b_in['conv_w'], 'L1_attn_b_conv_b': _L1_attn_b_in['conv_b'], 'L1_attn_b_in_proj_w': _L1_attn_b_in['in_proj_w'], 'L1_attn_b_in_proj_b': _L1_attn_b_in['in_proj_b'], 'L1_attn_b_A_log': _L1_attn_b_in['A_log'], 'L1_attn_b_out_proj_w': _L1_attn_b_in['out_proj_w'], 'L1_attn_b_out_proj_b': _L1_attn_b_in['out_proj_b'], 'L1_ffn_w_q': _L1_ffn_in['w_q'], 'L1_ffn_keys': _L1_ffn_in['keys'], 'L1_ffn_expert_down': _L1_ffn_in['expert_down'], 'L1_ffn_expert_up': _L1_ffn_in['expert_up'], 'L1_ffn_norm_w': _L1_ffn_in['norm_w']}
    _x0 = _d['L0_attn_a_x']
    _d['L0_attn_a_x'] = jax.random.normal(jax.random.fold_in(jax.random.key(seed), 1), (16, 256, 128), dtype=_x0.dtype)
    del _x0
    return _d

def reference(L0_attn_a_x, L0_attn_a_norm_g, L0_attn_a_norm_b, L0_attn_a_in_w, L0_attn_a_conv_w, L0_attn_a_conv_b, L0_attn_a_xproj_w, L0_attn_a_dt_w, L0_attn_a_dt_b, L0_attn_a_A_log, L0_attn_a_D, L0_attn_a_out_w, L0_attn_b_gamma, L0_attn_b_w_qkv, L0_attn_b_w_out, L0_ffn_centroids, L0_ffn_gamma, L0_ffn_beta, L0_ffn_W1, L0_ffn_b1, L0_ffn_W2, L0_ffn_b2, L1_attn_a_W_kqv, L1_attn_a_W_proj, L1_attn_a_q_norm_w, L1_attn_a_k_norm_w, L1_attn_b_conv_w, L1_attn_b_conv_b, L1_attn_b_in_proj_w, L1_attn_b_in_proj_b, L1_attn_b_A_log, L1_attn_b_out_proj_w, L1_attn_b_out_proj_b, L1_ffn_w_q, L1_ffn_keys, L1_ffn_expert_down, L1_ffn_expert_up, L1_ffn_norm_w):

    def _L0_attn_a_ref(x, norm_g, norm_b, in_w, conv_w, conv_b, xproj_w, dt_w, dt_b, A_log, D, out_w):
        import jax, jax.numpy as jnp
        import numpy as np
        LN_EPS = 1e-05
        Bsz, L, d_model = x.shape
        d_inner, d_state = A_log.shape
        dt_rank = dt_w.shape[1]
        d_conv = conv_w.shape[-1]
        residual = x
        mu = jnp.mean(x, axis=-1, keepdims=True)
        var = jnp.var(x, axis=-1, keepdims=True)
        xn = (x - mu) * jax.lax.rsqrt(var + LN_EPS) * norm_g + norm_b
        xz = xn @ in_w.T
        x_, z = (xz[..., :d_inner], xz[..., d_inner:])
        xp = jnp.pad(x_, ((0, 0), (d_conv - 1, 0), (0, 0)))
        w = conv_w[:, 0, :]
        xc = conv_b + sum((xp[:, k:k + L, :] * w[:, k] for k in range(d_conv)))
        u = jax.nn.silu(xc)
        dbc = u @ xproj_w.T
        delta_raw = dbc[..., :dt_rank]
        Bm = dbc[..., dt_rank:dt_rank + d_state]
        Cm = dbc[..., dt_rank + d_state:]
        delta = jax.nn.softplus(delta_raw @ dt_w.T + dt_b)
        A = -jnp.exp(A_log)

        def step(h, ins):
            d_t, B_t, C_t, u_t = ins
            dA = jnp.exp(d_t[..., None] * A)
            dB = d_t[..., None] * B_t[:, None, :]
            h = dA * h + dB * u_t[..., None]
            y_t = jnp.einsum('bdn,bn->bd', h, C_t)
            return (h, y_t)
        h0 = jnp.zeros((Bsz, d_inner, d_state), x.dtype)
        xs = (jnp.swapaxes(delta, 0, 1), jnp.swapaxes(Bm, 0, 1), jnp.swapaxes(Cm, 0, 1), jnp.swapaxes(u, 0, 1))
        _, ys = jax.lax.scan(step, h0, xs)
        y = jnp.swapaxes(ys, 0, 1) + u * D
        y = y * jax.nn.silu(z)
        return y @ out_w.T + residual

    def _L0_attn_b_ref(x, gamma, w_qkv, w_out):
        import jax, jax.numpy as jnp
        import numpy as np
        DIM = 128
        DIM_HEAD = 128
        HEADS = 8
        DIM_INNER = DIM_HEAD * HEADS
        scale_norm = DIM ** 0.5
        scale_attn = DIM_HEAD ** (-0.5)
        l2 = jnp.sqrt(jnp.sum(x * x, axis=-1, keepdims=True))
        xn = x / jnp.maximum(l2, 1e-12) * scale_norm * gamma
        qkv = jnp.einsum('bnc,fc->bnf', xn, w_qkv)
        b, n, _ = qkv.shape
        qkv = qkv.reshape(b, n, 3, HEADS, DIM_HEAD)
        q, k, v = (qkv[:, :, 0], qkv[:, :, 1], qkv[:, :, 2])
        q = q * scale_attn
        sim = jnp.einsum('bihd,bjhd->bhij', q, k)
        causal_mask = jnp.triu(jnp.ones((n, n), dtype=bool), k=1)
        neg = -jnp.finfo(sim.dtype).max
        sim = jnp.where(causal_mask, neg, sim)
        attn = jax.nn.softmax(sim, axis=-1)
        out = jnp.einsum('bhij,bjhd->bihd', attn, v)
        out = out.reshape(b, n, DIM_INNER)
        return jnp.einsum('bnf,cf->bnc', out, w_out)

    def _L0_ffn_ref(x, centroids, gamma, beta, W1, b1, W2, b2):
        import jax, jax.numpy as jnp
        import numpy as np
        B, S, D, F, E = (1, 128, 128, 512, 8)
        EPS = 1e-05

        def _sublayer(xs, g, b, W1e, b1e, W2e, b2e):
            mu = jnp.mean(xs, axis=-1, keepdims=True)
            var = jnp.mean(jnp.square(xs - mu), axis=-1, keepdims=True)
            h = (xs - mu) * jax.lax.rsqrt(var + EPS) * g + b
            return xs + jax.nn.relu(h @ W1e.T + b1e) @ W2e.T + b2e
        feats = x.reshape(-1, x.shape[-1])
        scores = jax.lax.stop_gradient(feats @ centroids.T)
        expert = jnp.argmax(scores, axis=1)
        onehot = jax.nn.one_hot(expert, E, dtype=feats.dtype)
        alpha = jax.nn.sigmoid(jnp.sum(feats * centroids[expert], axis=-1, keepdims=True))
        ys = jax.vmap(_sublayer, in_axes=(None, 0, 0, 0, 0, 0, 0))(feats, gamma, beta, W1, b1, W2, b2)
        y = jnp.einsum('te,etd->td', onehot, ys)
        out = alpha * y + (1.0 - alpha) * feats
        return out.reshape(x.shape)

    def _L1_attn_a_ref(x, W_kqv, W_proj, q_norm_w, k_norm_w):
        import jax, jax.numpy as jnp
        import numpy as np
        N_HEAD = 16
        EPS = 1e-06

        def _rotate_half(x):
            d = x.shape[-1] // 2
            return jnp.concatenate((-x[..., d:], x[..., :d]), axis=-1)

        def _rms_norm(x, w, eps=EPS):
            d = x.shape[-1]
            rms = jnp.linalg.norm(x, axis=-1, keepdims=True) * d ** (-0.5)
            return w * (x / (rms + eps))
        B, T, C = x.shape
        H = N_HEAD
        D = C // H
        kqv = x @ W_kqv.T
        k, q, v = jnp.split(kqv, 3, axis=2)

        def to_heads(t):
            return t.reshape(B, T, H, D).transpose(0, 2, 1, 3)
        k, q, v = (to_heads(k), to_heads(q), to_heads(v))
        inv_freq = 1.0 / 10000.0 ** (jnp.arange(0, D, 2, dtype=jnp.float32) / D)
        t_pos = jnp.arange(T, dtype=jnp.float32)
        freqs = t_pos[:, None] * inv_freq[None, :]
        freqs = jnp.concatenate((freqs, freqs), axis=-1)
        cos = jnp.cos(freqs)[None, None]
        sin = jnp.sin(freqs)[None, None]
        q = q * cos + _rotate_half(q) * sin
        k = k * cos + _rotate_half(k) * sin
        q = _rms_norm(q, q_norm_w)
        k = _rms_norm(k, k_norm_w)
        scores = jnp.einsum('bhtd,bhsd->bhts', q, k) / jnp.sqrt(jnp.float32(D))
        causal = jnp.triu(jnp.ones((T, T), dtype=bool), k=1)
        scores = jnp.where(causal[None, None], -jnp.inf, scores)
        att = jax.nn.softmax(scores, axis=-1)
        y = jnp.einsum('bhts,bhsd->bhtd', att, v)
        y = y.transpose(0, 2, 1, 3).reshape(B, T, C)
        return y @ W_proj.T

    def _L1_attn_b_ref(x, conv_w, conv_b, in_proj_w, in_proj_b, A_log, out_proj_w, out_proj_b):
        import jax, jax.numpy as jnp
        import numpy as np
        D_MODEL = 128
        D_STATE = 64
        D_CONV = 4
        EXPAND = 2
        INNER = EXPAND * D_STATE
        PROJ = D_STATE + 2 * INNER
        B, L = (8, 512)
        EPS = 0.0001

        def _ssm_forward(x, conv_w, conv_b, in_proj_w, in_proj_b, A_log, out_proj_w, out_proj_b):
            bsz, L_in, _ = x.shape
            pad = (D_CONV - 1) // 2
            xc = jnp.transpose(x, (0, 2, 1))
            xc = jax.lax.conv_general_dilated(xc, conv_w, window_strides=(1,), padding=[(pad, pad)], dimension_numbers=('NCH', 'OIH', 'NCH'), feature_group_count=D_MODEL)
            xc = xc + conv_b[None, :, None]
            Lc = xc.shape[2]
            if Lc < L_in:
                xc = jnp.pad(xc, ((0, 0), (0, 0), (0, L_in - Lc)))
            elif Lc > L_in:
                xc = xc[:, :, :L_in]
            xc = jnp.transpose(xc, (0, 2, 1))
            proj = xc @ in_proj_w.T + in_proj_b
            delta = proj[..., :D_STATE]
            B_in = proj[..., D_STATE:D_STATE + INNER]
            C = proj[..., D_STATE + INNER:]
            n_groups = INNER // D_STATE
            B_in = B_in.reshape(bsz, L_in, D_STATE, n_groups).mean(axis=-1)
            C = C.reshape(bsz, L_in, D_STATE, n_groups).mean(axis=-1)
            A = -jnp.exp(A_log)[None, None, :]
            delta = jax.nn.softplus(delta)
            dA = delta * A
            A_bar = jnp.exp(dA)
            A_safe = jnp.where(jnp.abs(A) < EPS, EPS * jnp.sign(A) + EPS, A)
            scale = (A_bar - 1.0) / A_safe
            taylor = 1.0 + dA / 2.0 + dA * dA / 6.0
            scale = jnp.where(jnp.abs(A) < EPS, taylor, scale)
            B_bar = scale * B_in

            def comb(e1, e2):
                a1, b1 = e1
                a2, b2 = e2
                return (a1 * a2, a2 * b1 + b2)
            _, h = jax.lax.associative_scan(comb, (A_bar, B_bar), axis=1)
            y_state = C * h
            return y_state @ out_proj_w.T + out_proj_b
        return _ssm_forward(x, conv_w, conv_b, in_proj_w, in_proj_b, A_log, out_proj_w, out_proj_b)

    def _L1_ffn_ref(x, w_q, keys, expert_down, expert_up, norm_w):
        import jax, jax.numpy as jnp
        import numpy as np
        B, T, D = (2, 128, 128)
        H, DK, K = (8, 128, 8)
        NKEYS = 32
        NEXP = NKEYS * NKEYS

        def _rmsnorm(x, w, eps=1e-06):
            inv = jax.lax.rsqrt(jnp.mean(x * x, axis=-1, keepdims=True) + eps)
            return x * inv * w
        b, t, d = x.shape
        xn = _rmsnorm(x, norm_w)
        q = (xn @ w_q.T).reshape(b, t, H, 2, DK)
        sim1 = jnp.einsum('bthd,hkd->bthk', q[..., 0, :], keys[:, :, 0, :])
        sim2 = jnp.einsum('bthd,hkd->bthk', q[..., 1, :], keys[:, :, 1, :])
        s1, i1 = jax.lax.top_k(sim1, K)
        s2, i2 = jax.lax.top_k(sim2, K)
        all_idx = (i1[..., :, None] * NKEYS + i2[..., None, :]).reshape(b, t, H, K * K)
        all_sc = (s1[..., :, None] + s2[..., None, :]).reshape(b, t, H, K * K)
        fs, pk = jax.lax.top_k(all_sc, K)
        fi = jnp.take_along_axis(all_idx, pk, axis=-1)
        wd = expert_down[fi]
        wu = expert_up[fi]
        hidden = jax.nn.gelu(jnp.einsum('btd,bthkd->bthk', xn, wd), approximate=False)
        hidden = hidden * jax.nn.relu(fs)
        return jnp.einsum('bthk,bthkd->btd', hidden, wu)
    x = L0_attn_a_x
    x = x + _L0_attn_a_ref(_layernorm(x, axis=-1), L0_attn_a_norm_g, L0_attn_a_norm_b, L0_attn_a_in_w, L0_attn_a_conv_w, L0_attn_a_conv_b, L0_attn_a_xproj_w, L0_attn_a_dt_w, L0_attn_a_dt_b, L0_attn_a_A_log, L0_attn_a_D, L0_attn_a_out_w)
    x = x + _L0_ffn_ref(_layernorm(x, axis=-1), L0_ffn_centroids, L0_ffn_gamma, L0_ffn_beta, L0_ffn_W1, L0_ffn_b1, L0_ffn_W2, L0_ffn_b2)
    x = x + _L0_attn_b_ref(_layernorm(x, axis=-1), L0_attn_b_gamma, L0_attn_b_w_qkv, L0_attn_b_w_out)
    x = x + _L0_ffn_ref(_layernorm(x, axis=-1), L0_ffn_centroids, L0_ffn_gamma, L0_ffn_beta, L0_ffn_W1, L0_ffn_b1, L0_ffn_W2, L0_ffn_b2)
    x = x + _L1_attn_a_ref(_layernorm(x, axis=-1), L1_attn_a_W_kqv, L1_attn_a_W_proj, L1_attn_a_q_norm_w, L1_attn_a_k_norm_w)
    x = x + _L1_ffn_ref(_layernorm(x, axis=-1), L1_ffn_w_q, L1_ffn_keys, L1_ffn_expert_down, L1_ffn_expert_up, L1_ffn_norm_w)
    x = x + _L1_attn_b_ref(_layernorm(x, axis=-1), L1_attn_b_conv_w, L1_attn_b_conv_b, L1_attn_b_in_proj_w, L1_attn_b_in_proj_b, L1_attn_b_A_log, L1_attn_b_out_proj_w, L1_attn_b_out_proj_b)
    x = x + _L1_ffn_ref(_layernorm(x, axis=-1), L1_ffn_w_q, L1_ffn_keys, L1_ffn_expert_down, L1_ffn_expert_up, L1_ffn_norm_w)
    return x

_drawn_inputs = setup_inputs


def setup_inputs(seed=0):
    import zlib

    import numpy as np

    out = dict(_drawn_inputs(seed))
    spreads = {'L0_attn_a_norm_g': (1.0, 0.2),
     'L0_attn_a_norm_b': (0.0, 0.1),
     'L0_attn_a_conv_b': (0.0, 0.396),
     'L0_attn_a_D': (1.0, 0.2),
     'L0_attn_b_gamma': (1.0, 0.6),
     'L0_ffn_gamma': (1.0, 0.6),
     'L0_ffn_beta': (0.0, 0.8),
     'L0_ffn_b1': (0.0, 0.528),
     'L0_ffn_b2': (0.0, 0.1),
     'L1_attn_a_q_norm_w': (1.0, 0.6),
     'L1_attn_a_k_norm_w': (1.0, 0.6),
     'L1_attn_b_conv_b': (0.0, 0.554),
     'L1_attn_b_in_proj_b': (0.0, 0.454),
     'L1_attn_b_out_proj_b': (0.0, 0.317),
     'L1_ffn_norm_w': (1.0, 0.6)}
    factors = {'L0_attn_a_dt_w': 3.635,
     'L0_attn_a_dt_b': 2.995,
     'L0_attn_a_A_log': 4.461,
     'L0_attn_b_w_qkv': 2.933,
     'L0_attn_b_w_out': 2.94,
     'L1_attn_b_A_log': 6.459,
     'L1_ffn_w_q': 8.0,
     'L1_ffn_keys': 8.0,
     'L1_ffn_expert_down': 8.0,
     'L1_ffn_expert_up': 8.0}
    for name, (base, spread) in spreads.items():
        noise = np.random.default_rng([zlib.crc32(name.encode()), seed]).standard_normal(out[name].shape)
        drawn = base * np.exp(spread * noise) if base else spread * noise
        out[name] = jnp.asarray(drawn.astype(out[name].dtype))
    for name, factor in factors.items():
        out[name] = (out[name] * factor).astype(out[name].dtype)
    return out
```

```python
from contextlib import ExitStack

import numpy as np

import concourse.bass as bass
from concourse import mybir

P = 128
TPC = 4
CH = TPC * P
SEQ = 256
SPC = CH // SEQ

F32 = mybir.dt.float32
BF16 = mybir.dt.bfloat16
ALU = mybir.AluOpType
ACT = mybir.ActivationFunctionType
AX = mybir.AxisListType.X


class Env:
    pass


class Lent:
    handles = []


def sweep(nc):
    nc.clear_and_free_semaphores(Lent.handles)
    Lent.handles = []
    nc.all_engine_barrier()


class Link:

    def __init__(self, eng, sem, base=0):
        self.eng, self.sem, self.base, self.n = eng, sem, base, 0

    def __call__(self, ins):
        ins.then_inc(self.sem, 1)
        self.n += 1
        self.eng.wait_ge(self.sem, self.base + self.n)

    def inc(self, ins):
        ins.then_inc(self.sem, 1)
        self.n += 1

    def wait(self, back=0):
        self.eng.wait_ge(self.sem, self.base + self.n - back)


def hold(eng, sem, value):
    eng.wait_ge(sem, value)
    eng.nop(nofuse=True)


def scope(nc, ctx, tag):
    def sb(name, shape, dt=F32):
        return ctx.enter_context(nc.sbuf_tensor(f"{tag}_{name}", shape, dt))

    def ps(name, shape, dt=F32):
        return ctx.enter_context(nc.psum_tensor(f"{tag}_{name}", shape, dt))

    def sem(name):
        handle = nc.alloc_semaphore(name=f"{tag}_{name}")
        Lent.handles.append(handle)
        return handle

    return sb, ps, sem


def turn_weights(nc, env, tag, loads, turns, extra=None):
    with ExitStack() as ctx:
        sb, ps, sem = scope(nc, ctx, tag)
        turned = ps("turned", [P, 8, 512])
        loaded, placed, evacuated = sem("loaded"), sem("placed"), sem("evacuated")
        block = ctx.enter_context(nc.Block())

        @block.sync
        def _(sp):
            for dst, src in loads:
                sp.dma_start(dst, src, allow_slow_non_contiguous=True).then_inc(loaded, 16)
            sp.wait_ge(loaded, 16 * len(loads))

        if turns:
            @block.tensor
            def _(pe):
                pe.wait_ge(loaded, 16 * len(loads))
                for j, (src, dst) in enumerate(turns):
                    p, f = src.shape[0], dst.shape[0]
                    if j >= 8:
                        pe.wait_ge(evacuated, j - 7)
                    nc.tensor.transpose(turned[0:f, j % 8, 0:p], src, env.ident[0:p, 0:p]).then_inc(placed, 1)

            @block.vector
            def _(dve):
                for j, (src, dst) in enumerate(turns):
                    p, f = src.shape[0], dst.shape[0]
                    dve.wait_ge(placed, j + 1)
                    nc.vector.tensor_copy(dst, turned[0:f, j % 8, 0:p]).then_inc(evacuated, 1)
                dve.wait_ge(evacuated, len(turns))


def row_scales(nc, env, tag, second):
    NT = env.NT
    with ExitStack() as ctx:
        sb, ps, sem = scope(nc, ctx, tag)
        tmp = sb("tmp", [P, 5, NT])
        rooted, vec = sem("rooted"), sem("vec")
        block = ctx.enter_context(nc.Block())
        st, t0, t1, t2, t3, t4 = env.stats, tmp[:, 0, :], tmp[:, 1, :], tmp[:, 2, :], tmp[:, 3, :], tmp[:, 4, :]

        @block.vector
        def _(dve):
            link = Link(dve, vec)
            link.inc(nc.vector.tensor_tensor(t0, st[:, :, 1], st[:, :, 4], ALU.add))
            link.inc(nc.vector.tensor_tensor(t1, st[:, :, 1], st[:, :, 4], ALU.subtract))
            link.inc(nc.vector.tensor_tensor(t2, st[:, :, 2], st[:, :, 5], ALU.add))
            link.wait()
            link.inc(nc.vector.tensor_scalar(env.mean[:, :], t0, 0.5, None, ALU.mult))
            link(nc.vector.scalar_tensor_tensor(t3, t1, 0.25, t1, ALU.mult, ALU.mult))
            link(nc.vector.scalar_tensor_tensor(t0, t2, 1.0 / P, t3, ALU.mult, ALU.add))
            link(nc.vector.tensor_scalar(t1, t0, 1e-5, None, ALU.add))
            dve.wait_ge(rooted, 1)
            link(nc.vector.reciprocal(env.rstd[:, :], t2))
            link.inc(nc.vector.tensor_scalar(env.keep[:, :], env.rstd[:, :], 1.0, None, ALU.add))
            link(nc.vector.scalar_tensor_tensor(env.shift[:, :], env.mean[:, :], -1.0, env.rstd[:, :],
                                                ALU.mult, ALU.mult))
            if second:
                k, eps, floor, gain = second
                link(nc.vector.tensor_tensor(t1, t0, env.rstd[:, :], ALU.mult))
                link(nc.vector.tensor_tensor(t3, t1, env.rstd[:, :], ALU.mult))
                link(nc.vector.tensor_scalar(t1, t3, float(k), float(eps), ALU.mult, ALU.add))
                dve.wait_ge(rooted, 2)
                link(nc.vector.tensor_scalar(t4, t2, float(floor), None, ALU.max))
                link(nc.vector.reciprocal(t3, t4))
                link.inc(nc.vector.tensor_scalar(env.root[:, :], t4, 1.0 / gain, None, ALU.mult))
                link(nc.vector.scalar_tensor_tensor(env.rnorm[:, :], t3, float(gain), env.rstd[:, :],
                                                    ALU.mult, ALU.mult))

        @block.scalar
        def _(act):
            act.wait_ge(vec, 7)
            nc.scalar.activation(t2, t1, ACT.Sqrt).then_inc(rooted, 1)
            if second:
                act.wait_ge(vec, 13)
                nc.scalar.activation(t2, t1, ACT.Sqrt).then_inc(rooted, 1)
            act.wait_ge(rooted, 2 if second else 1)


def first_stats(nc, env, x_dram):
    with ExitStack() as ctx:
        sb, ps, sem = scope(nc, ctx, "first")
        loaded, done = sem("loaded"), sem("done")
        block = ctx.enter_context(nc.Block())
        rows = x_dram.rearrange("b (s p) c -> p (b s) c", p=P)

        @block.sync
        def _(sp):
            for q in range(2):
                h = env.NT // 2
                sp.dma_start(env.X[:, q * h:(q + 1) * h, :], rows[:, q * h:(q + 1) * h, :]).then_inc(loaded, 16)

        @block.vector
        def _(dve):
            dve.wait_ge(loaded, 32)
            with dve.Fori(0, env.NT) as i:
                nc.vector.bn_stats(env.stats[:, i, :], env.X[:, i, :]).then_inc(done, 1)
            dve.wait_ge(done, env.NT)


class Front:

    def __init__(self, nc, env, sb, ps, sem, inner, out, scale=None, bias=None, banks=1, out_rows=None):
        self.nc, self.env, self.inner, self.out, self.scale, self.bias = nc, env, inner, out, scale, bias
        self.rows = out_rows or sb("rows", [P, 2, TPC, P])
        self.tp = ps("front", [P, banks, 512])
        self.banks = banks
        self.normed, self.turned, self.written = sem("normed"), sem("turned"), sem("written")

    def dve(self, eng, n, p, free=None):
        e, nc = self.env, self.nc
        eng.wait_ge(self.turned, n + 1)
        if free:
            eng.wait_ge(*free)
        r = e.rnorm if self.inner else e.rstd
        for k in range(TPC):
            t = n * TPC + k
            ins = nc.vector.tensor_scalar(self.rows[:, p, k, :], e.X[:, t, :], e.mean[:, bass.ds(t, 1)],
                                          r[:, bass.ds(t, 1)], ALU.subtract, ALU.mult)
        ins.then_inc(self.normed, 1)

    def credit(self, pe):
        pe.sem_inc(self.turned, 2)

    def credit_act(self, act):
        act.sem_inc(self.written, self.banks)

    def pe(self, eng, n, p):
        eng.wait_ge(self.normed, n + 1)
        eng.wait_ge(self.written, n + 1)
        for k in range(TPC):
            ins = self.nc.tensor.transpose(self.tp[:, p % self.banks, k * P:(k + 1) * P],
                                           self.rows[:, p, k, :], self.env.ident[:, :])
        ins.then_inc(self.turned, 1)

    def act(self, eng, n, p):
        eng.wait_ge(self.turned, n + 3)
        dst = self.out(p)
        src = self.tp[:, p % self.banks, :]
        if len(dst.shape) == 3:
            src = src.rearrange("p (s t) -> p s t", s=dst.shape[1])
        kw = {}
        if self.scale is not None:
            kw["scale"] = self.scale
        if self.bias is not None:
            kw["bias"] = self.bias
        if kw:
            ins = self.nc.scalar.activation(dst, src, ACT.Identity, **kw)
        else:
            ins = self.nc.scalar.copy(dst, src)
        ins.then_inc(self.written, 1)

    def wait(self, eng, n):
        eng.wait_ge(self.written, n + 1 + self.banks)


class Back:

    def __init__(self, nc, env, sb, ps, sem, tiles=TPC):
        self.nc, self.env, self.tiles = nc, env, tiles
        self.buf = sb("sum", [P, tiles, P])
        self.chain = sem("back")

    def dve(self, eng, n, out, y=True, gain=None, turn=None):
        e, nc, G = self.env, self.nc, self.tiles
        base = (n if turn is None else turn) * 3
        last = None
        for k in range(G if y else 0):
            t = n * G + k
            last = nc.vector.tensor_scalar(self.buf[:, k, :], e.X[:, t, :], e.keep[:, bass.ds(t, 1)],
                                           e.shift[:, bass.ds(t, 1)], ALU.mult, ALU.add)
        if y:
            last.then_inc(self.chain, 1)
        else:
            eng.sem_inc(self.chain, 1)
        eng.wait_ge(self.chain, base + 1)
        if gain is None:
            dst = e.X[:, bass.ds(n * G, G), :]
            last = nc.vector.tensor_tensor(dst, self.buf[:, :, :] if y else dst, out, ALU.add)
        else:
            for k in range(G):
                t = n * G + k
                dst = e.X[:, t, :]
                last = nc.vector.scalar_tensor_tensor(dst, out[:, k, :], gain[:, bass.ds(t, 1)],
                                                      self.buf[:, k, :] if y else dst, ALU.mult, ALU.add)
        last.then_inc(self.chain, 1)
        eng.wait_ge(self.chain, base + 2)
        for k in range(G):
            t = n * G + k
            last = nc.vector.bn_stats(e.stats[:, t, :], e.X[:, t, :])
        last.then_inc(self.chain, 1)
        eng.wait_ge(self.chain, base + 3)


def mamba(nc, env, a):
    NT, NC_, T = env.NT, env.NC, env.NT * P
    DI, DS, DTR, TAPS = 256, 16, 64, 4
    H = DI // P
    row_scales(nc, env, "m_sc", (1.0, 1e-5, 0.0, 1.0))
    with ExitStack() as outer:
        sb, ps, sem = scope(nc, outer, "m")
        wconv = sb("wconv", [P, TAPS, DI])
        wz = sb("wz", [P, DI])
        xprojT = sb("xprojT", [P, H, DTR + 2 * DS])
        dtT = sb("dtT", [DTR, DI])
        outT = sb("outT", [P, H, P])
        A = sb("A", [P, H, DS])
        convb, dtb, Dd = sb("convb", [P, H]), sb("dtb", [P, H]), sb("Dd", [P, H])
        g, b = sb("g", [P, 1]), sb("b", [P, 1])
        diagD = sb("diagD", [P, H, P])
        u = sb("u", [P, H, T])
        sz = sb("sz", [P, H, T])
        delta = sb("delta", [P, H, T])
        du = sb("du", [P, H, T])
        bc = sb("bc", [96, T], BF16)
        with ExitStack() as prep:
            psb, pps, psem = scope(nc, prep, "mp")
            in_w = psb("in_w", [P, 4, P])
            scaled = psb("scaled", [P, TAPS, H, P])
            cw = psb("cw", [P, H, TAPS])
            xp = psb("xp", [DTR + 2 * DS, DI])
            dtw = psb("dtw", [P, H, DTR])
            ow = psb("ow", [P, DI])
            ld, mt, ma_ = psem("ld"), psem("mt"), psem("ma")
            with nc.Block() as block:
                @block.sync
                def _(sp):
                    for dst, src in (
                        (in_w[:, :, :], a["in_w"].rearrange("(j p) c -> p j c", p=P)),
                        (cw[:, :, :], a["conv_w"].rearrange("(h p) o k -> p h (o k)", p=P)),
                        (xp[:, :], a["xproj_w"]),
                        (dtw[:, :, :], a["dt_w"].rearrange("(h p) r -> p h r", p=P)),
                        (ow[:, :], a["out_w"]),
                        (A[:, :, :], a["A_log"].rearrange("(h p) s -> p h s", p=P)),
                        (convb[:, :], a["conv_b"].rearrange("(h p) -> p h", p=P)),
                        (dtb[:, :], a["dt_b"].rearrange("(h p) -> p h", p=P)),
                        (Dd[:, :], a["D"].rearrange("(h p) -> p h", p=P)),
                        (g[:, :], a["norm_g"].rearrange("(p o) -> p o", o=1)),
                        (b[:, :], a["norm_b"].rearrange("(p o) -> p o", o=1)),
                    ):
                        sp.dma_start(dst, src, allow_slow_non_contiguous=True).then_inc(ld, 16)

                @block.vector
                def _(dve):
                    dve.wait_ge(ld, 16 * 11)
                    for k in range(TAPS):
                        for h in range(H):
                            nc.vector.tensor_scalar(scaled[:, k, h, :], in_w[:, h, :], cw[:, h, k:k + 1], None,
                                                    ALU.mult).then_inc(mt, 1)
                    for h in range(H):
                        nc.vector.tensor_scalar(diagD[:, h, :], env.ident[:, :], Dd[:, h:h + 1], None,
                                                ALU.mult).then_inc(mt, 1)
                    dve.wait_ge(mt, 10)

                @block.scalar
                def _(act):
                    act.wait_ge(ld, 16 * 11)
                    nc.scalar.activation(A[:, :, :], A[:, :, :], ACT.Exp).then_inc(ma_, 1)
                    act.wait_ge(ma_, 1)
                    nc.scalar.mul(A[:, :, :], A[:, :, :], -1.0).then_inc(ma_, 1)
                    act.wait_ge(ma_, 2)
            turn_weights(nc, env, "m_t", [],
                         [(scaled[:, k, h, :], wconv[:, k, h * P:(h + 1) * P]) for k in range(TAPS) for h in range(H)]
                         + [(in_w[:, 2 + h, :], wz[:, h * P:(h + 1) * P]) for h in range(H)]
                         + [(xp[:, h * P:(h + 1) * P], xprojT[:, h, :]) for h in range(H)]
                         + [(dtw[:, h, :], dtT[:, h * P:(h + 1) * P]) for h in range(H)]
                         + [(ow[:, h * P:(h + 1) * P], outT[:, h, :]) for h in range(H)])

        with ExitStack() as ctx:
            sb, ps, sem = scope(nc, ctx, "ma")
            PAD = TAPS - 1
            zc = sb("zc", [P, 2, SPC, PAD + SEQ])
            dr = sb("dr", [DTR, CH])
            bcf = sb("bcf", [2 * DS, 2, CH])
            pj = ps("pj", [P, 4, 512])
            pd = ps("pd", [P, 3, 512])
            padded, proj, gated, small, draw_, drd, split = (sem(x) for x in (
                "padded", "proj", "gated", "small", "dtraw", "drd", "split"))
            front = Front(nc, env, sb, ps, sem, True, lambda p: zc[:, p, :, PAD:PAD + SEQ],
                          scale=g[:, 0:1], bias=b[:, 0:1])
            block = ctx.enter_context(nc.Block())

            @block.gpsimd
            def _(pool):
                nc.gpsimd.memset(zc[:, :, :, 0:PAD], 0.0).then_inc(padded, 1)

            @block.vector
            def _(dve):
                with dve.Fori(0, NC_ // 2) as it:
                    for p in range(2):
                        n = it * 2 + p
                        front.dve(dve, n, p)
                    for p in range(2):
                        n = it * 2 + p
                        dve.wait_ge(small, 2 * n + 2)
                        link = Link(dve, split, n * 5)
                        cols = bass.ds(n * CH, CH)
                        link(nc.vector.tensor_copy(bc[0:32, cols], bcf[:, 0, :]))
                        link(nc.vector.tensor_tensor(bcf[:, 1, :], bcf[:, 0, :], bc[0:32, cols], ALU.subtract))
                        link(nc.vector.tensor_copy(bc[32:64, cols], bcf[:, 1, :]))
                        link(nc.vector.tensor_tensor(bcf[:, 0, :], bcf[:, 1, :], bc[32:64, cols], ALU.subtract))
                        link(nc.vector.tensor_copy(bc[64:96, cols], bcf[:, 0, :]))

            @block.tensor
            def _(pe):
                front.credit(pe)
                pe.wait_ge(padded, 1)
                with pe.Fori(0, NC_ // 2) as it:
                    for p in range(2):
                        n = it * 2 + p
                        front.pe(pe, n, p)
                        front.wait(pe, n)
                        for h in range(H):
                            pe.wait_ge(gated, 4 * n + 1 + h)
                            for k in range(TAPS):
                                ins = nc.tensor.matmul(pj[:, h, :], wconv[:, k, h * P:(h + 1) * P],
                                                       zc[:, p, :, k:k + SEQ], start=(k == 0), stop=(k == TAPS - 1))
                            ins.then_inc(proj, 1)
                        for h in range(H):
                            pe.wait_ge(gated, 4 * n + 3 + h)
                            nc.tensor.matmul(pj[:, 2 + h, :], wz[:, h * P:(h + 1) * P],
                                             zc[:, p, :, PAD:PAD + SEQ], start=True, stop=True).then_inc(proj, 1)
                        pe.wait_ge(gated, 4 * n + 4 + 2)
                        pe.wait_ge(small, 2 * n)
                        for h in range(H):
                            ins = nc.tensor.matmul(pd[0:96, 0, :], xprojT[:, h, :], u[:, h, bass.ds(n * CH, CH)],
                                                   start=(h == 0), stop=(h == H - 1))
                        ins.then_inc(draw_, 1)
                        pe.wait_ge(small, 2 * n + 1)
                        for h in range(H):
                            pe.wait_ge(drd, 2 * n + h + 1)
                            nc.tensor.matmul(pd[:, 1 + h, :], dtT[:, h * P:(h + 1) * P], dr[:, :],
                                             start=True, stop=True).then_inc(draw_, 1)

            @block.scalar
            def _(act):
                front.credit_act(act)
                act.sem_inc(gated, 4)
                act.sem_inc(drd, 2)
                with act.Fori(0, NC_ // 2) as it:
                    for p in range(2):
                        n = it * 2 + p
                        cols = bass.ds(n * CH, CH)
                        front.act(act, n, p)
                        for h in range(H):
                            hold(act, proj, 4 * n + 1 + h)
                            nc.scalar.activation(u[:, h, cols], pj[:, h, :], ACT.Silu,
                                                 bias=convb[:, h:h + 1]).then_inc(gated, 1)
                        for h in range(H):
                            hold(act, proj, 4 * n + 3 + h)
                            nc.scalar.activation(sz[:, h, cols], pj[:, 2 + h, :], ACT.Silu).then_inc(gated, 1)
                        act.wait_ge(draw_, 3 * n + 1)
                        nc.scalar.copy(dr[:, :], pd[0:DTR, 0, :]).then_inc(small, 1)
                        act.wait_ge(split, 5 * n)
                        nc.scalar.copy(bcf[:, 0, :], pd[DTR:DTR + 2 * DS, 0, :]).then_inc(small, 1)
                        for h in range(H):
                            hold(act, draw_, 3 * n + 2 + h)
                            nc.scalar.activation(delta[:, h, cols], pd[:, 1 + h, :], ACT.Identity,
                                                 bias=dtb[:, h:h + 1]).then_inc(drd, 1)

        with ExitStack() as ctx:
            sb, ps, sem = scope(nc, ctx, "mb")
            e = sb("e", [P, 2, H, CH])
            l = sb("l", [P, 2, H, CH])
            w = sb("w", [P, 2, H, CH])
            logs, vec, rest, done = sem("logs"), sem("vec"), sem("rest"), sem("done")
            block = ctx.enter_context(nc.Block())

            @block.scalar
            def _(act):
                with act.Fori(0, NC_ // 2) as it:
                    for p in range(2):
                        n = it * 2 + p
                        d = delta[:, :, bass.ds(n * CH, CH)]
                        hold(act, done, n + 1)
                        link = Link(act, logs, 3 * n)
                        link(nc.scalar.activation(l[:, p, :, :], d, ACT.Abs))
                        link(nc.scalar.activation(e[:, p, :, :], l[:, p, :, :], ACT.Exp, scale=-1.0))
                        link(nc.scalar.activation(l[:, p, :, :], e[:, p, :, :], ACT.Ln, bias=1.0))

            @block.gpsimd
            def _(pool):
                with pool.Fori(0, NC_ // 2) as it:
                    for p in range(2):
                        n = it * 2 + p
                        hold(pool, logs, 3 * n + 2)
                        link = Link(pool, rest, 2 * n)
                        link(nc.gpsimd.tensor_scalar(w[:, p, :, :], e[:, p, :, :], 1.0, -1.0, ALU.add, ALU.add))
                        link(nc.gpsimd.tensor_tensor(w[:, p, :, :], e[:, p, :, :], w[:, p, :, :], ALU.subtract))

            @block.vector
            def _(dve):
                dve.sem_inc(done, 2)
                with dve.Fori(0, NC_ // 2) as it:
                    for p in range(2):
                        n = it * 2 + p
                        cols = bass.ds(n * CH, CH)
                        d = delta[:, :, cols]
                        dve.wait_ge(logs, 3 * n + 3)
                        link = Link(dve, vec, 2 * n)
                        link(nc.vector.scalar_tensor_tensor(l[:, p, :, :], d, 0.0, l[:, p, :, :], ALU.max, ALU.add))
                        dve.wait_ge(rest, 2 * n + 2)
                        link(nc.vector.tensor_tensor(d, l[:, p, :, :], w[:, p, :, :], ALU.add))
                        nc.vector.tensor_tensor(du[:, :, cols], d, u[:, :, cols], ALU.mult).then_inc(done, 1)
                dve.wait_ge(done, NC_ + 2)

        with ExitStack() as ctx:
            sb, ps, sem = scope(nc, ctx, "mc")
            RB = 4
            dA = sb("dA", [P, RB, SPC, SEQ])
            h_ = sb("h", [P, RB, CH])
            cs = sb("cs", [P, 2, CH])
            hc = sb("hc", [P, RB, CH])
            Bp, Cp = ps("B", [P, 2, 512]), ps("C", [P, 2, 512])
            dbu = ps("dbu", [P, 2, 512])
            yp = ps("y", [P, H, 512])
            zeroed, bcast, cdone, decay, inject, scanned, outs, summed, y_out, moved = (sem(x) for x in (
                "zeroed", "bcast", "cdone", "decay", "inject", "scanned", "outs", "summed", "yout", "moved"))
            block = ctx.enter_context(nc.Block())
            Q = DS * H

            @block.tensor
            def _(pe):
                def sum_up(n, q):
                    s, h = q // H, q % H
                    pe.wait_ge(outs, n * Q + q + 1 + RB)
                    if s == 0:
                        pe.wait_ge(y_out, H * n)
                    nc.tensor.matmul(yp[:, h, :], env.ident[:, :], hc[:, q % RB, :], start=(s == 0), stop=False,
                                     ).then_inc(summed, 1)

                pe.sem_inc(summed, RB)
                with pe.Fori(0, NC_) as n:
                    cols = bass.ds(n * CH, CH)
                    for s in range(DS):
                        pe.wait_ge(inject, n * Q + H * (s - 1) + 2 * H)
                        pe.wait_ge(cdone, n * DS + s + 1)
                        nc.tensor.matmul(Bp[:, s % 2, :], env.sel[:, s, :], bc[:, cols], start=True, stop=True)
                        nc.tensor.matmul(Cp[:, s % 2, :], env.sel[:, DS + s, :], bc[:, cols],
                                         start=True, stop=True).then_inc(bcast, 1)
                        if s >= 1:
                            for h in range(H):
                                sum_up(n, (s - 1) * H + h)
                    for h in range(H):
                        sum_up(n, (DS - 1) * H + h)
                    for h in range(H):
                        nc.tensor.matmul(yp[:, h, :], diagD[:, h, :], u[:, h, cols], start=False,
                                         stop=True).then_inc(moved, 1)

            @block.scalar
            def _(act):
                act.sem_inc(cdone, 2)
                act.wait_ge(zeroed, 1)
                with act.Fori(0, NC_) as n:
                    for s in range(DS):
                        for h in range(H):
                            q = s * H + h
                            hold(act, scanned, n * Q + q + 1)
                            d = delta[:, h, bass.ds(n * CH, CH)].rearrange("p (s t) -> p s t", s=SPC)
                            nc.scalar.activation(dA[:, q % RB, :, 1:SEQ], d[:, :, 1:SEQ], ACT.Exp,
                                                 scale=A[:, h, s:s + 1]).then_inc(decay, 1)
                        act.wait_ge(bcast, n * DS + s + 1)
                        act.wait_ge(outs, n * Q + H * (s - 1) + RB)
                        nc.scalar.copy(cs[:, s % 2, :], Cp[:, s % 2, :]).then_inc(cdone, 1)

            @block.vector
            def _(dve):
                def inject_(n, q):
                    s, h = q // H, q % H
                    dve.wait_ge(bcast, n * DS + s + 1)
                    dve.wait_ge(scanned, n * Q + q - 1 + RB)
                    nc.vector.tensor_tensor(dbu[:, q % 2, :], du[:, h, bass.ds(n * CH, CH)], Bp[:, s % 2, :],
                                            ALU.mult).then_inc(inject, 1)

                dve.sem_inc(inject, 2 * H)
                dve.sem_inc(scanned, RB)
                with dve.Fori(0, NC_) as n:
                    inject_(n, 0)
                    for q in range(Q):
                        if q + 1 < Q:
                            inject_(n, q + 1)
                        dve.wait_ge(inject, n * Q + q + 1 + 2 * H)
                        dve.wait_ge(decay, n * Q + q + 1)
                        dve.wait_ge(outs, n * Q + q + 1)
                        nc.vector.tensor_tensor_scan(h_[:, q % RB, :], dA[:, q % RB, :, :].rearrange("p s t -> p (s t)"),
                                                     dbu[:, q % 2, :], 0.0, ALU.mult, ALU.add).then_inc(scanned, 1)
                    for h in range(H):
                        dve.wait_ge(moved, H * n + 1 + h)
                        z = sz[:, h, bass.ds(n * CH, CH)]
                        nc.vector.tensor_tensor(z, z, yp[:, h, :], ALU.mult).then_inc(y_out, 1)

            @block.gpsimd
            def _(pool):
                nc.gpsimd.memset(dA[:, :, :, 0:1], 0.0).then_inc(zeroed, 1)
                pool.sem_inc(outs, RB)
                with pool.Fori(0, NC_) as n:
                    for q in range(Q):
                        s = q // H
                        pool.wait_ge(scanned, n * Q + q + 1 + RB)
                        pool.wait_ge(cdone, n * DS + s + 1 + 2)
                        pool.wait_ge(summed, n * Q + q + 1)
                        nc.gpsimd.tensor_tensor(hc[:, q % RB, :], h_[:, q % RB, :], cs[:, s % 2, :],
                                                ALU.mult).then_inc(outs, 1)
        channels_out(nc, env, "md", H, lambda h: outT[:, h, :], lambda h, n: sz[:, h, bass.ds(n * CH, CH)])


def channels_out(nc, env, tag, K, weight, act_of, y=True):
    with ExitStack() as ctx:
        sb, ps, sem = scope(nc, ctx, tag)
        po, pt = ps("po", [P, 2, 512]), ps("pt", [P, 2, 512])
        oT = sb("oT", [P, 2, CH])
        made, held, turned, added = sem("made"), sem("held"), sem("turned"), sem("added")
        back = Back(nc, env, sb, ps, sem)
        block = ctx.enter_context(nc.Block())

        @block.tensor
        def _(pe):
            with pe.Fori(0, env.NC // 2) as it:
                for p in range(2):
                    n = it * 2 + p
                    pe.wait_ge(held, n + 1)
                    for k in range(K):
                        ins = nc.tensor.matmul(po[:, p, :], weight(k), act_of(k, n), start=(k == 0), stop=(k == K - 1))
                    ins.then_inc(made, 1)
                    pe.wait_ge(held, n + 3)
                    pe.wait_ge(added, n + 1)
                    for k in range(TPC):
                        ins = nc.tensor.transpose(pt[:, p, k * P:(k + 1) * P], oT[:, p, k * P:(k + 1) * P], env.ident[:, :])
                    ins.then_inc(turned, 1)

        @block.scalar
        def _(act):
            act.sem_inc(held, 2)
            with act.Fori(0, env.NC // 2) as it:
                for p in range(2):
                    n = it * 2 + p
                    act.wait_ge(made, n + 1)
                    act.wait_ge(added, n + 1)
                    nc.scalar.copy(oT[:, p, :], po[:, p, :]).then_inc(held, 1)

        @block.vector
        def _(dve):
            dve.sem_inc(added, 2)
            with dve.Fori(0, env.NC // 2) as it:
                for p in range(2):
                    n = it * 2 + p
                    dve.wait_ge(turned, n + 1)
                    back.dve(dve, n, pt[:, p, :].rearrange("p (k c) -> p k c", k=TPC), y=y)
                    dve.sem_inc(added, 1)


def front_pass(nc, env, tag, inner, ZT, scale=None, bias=None):
    with ExitStack() as ctx:
        sb, ps, sem = scope(nc, ctx, tag)
        rows = sb("rows", [P, 2, TPC, P])
        tp = ps("tp", [P, 2, 512])
        normed, turned, written = sem("normed"), sem("turned"), sem("written")
        block = ctx.enter_context(nc.Block())
        r = env.rnorm if inner else env.rstd

        @block.vector
        def _(dve):
            with dve.Fori(0, env.NC // 2) as it:
                for p in range(2):
                    n = it * 2 + p
                    dve.wait_ge(turned, n + 1)
                    for k in range(TPC):
                        t = n * TPC + k
                        ins = nc.vector.tensor_scalar(rows[:, p, k, :], env.X[:, t, :], env.mean[:, bass.ds(t, 1)],
                                                      r[:, bass.ds(t, 1)], ALU.subtract, ALU.mult)
                    ins.then_inc(normed, 1)

        @block.tensor
        def _(pe):
            pe.sem_inc(turned, 2)
            with pe.Fori(0, env.NC // 2) as it:
                for p in range(2):
                    n = it * 2 + p
                    pe.wait_ge(written, n + 1)
                    pe.wait_ge(normed, n + 1)
                    for k in range(TPC):
                        ins = nc.tensor.transpose(tp[:, p, k * P:(k + 1) * P], rows[:, p, k, :], env.ident[:, :])
                    ins.then_inc(turned, 1)

        @block.scalar
        def _(act):
            act.sem_inc(written, 2)
            with act.Fori(0, env.NC // 2) as it:
                for p in range(2):
                    n = it * 2 + p
                    hold(act, turned, n + 3)
                    dst = ZT[:, bass.ds(n * CH, CH)]
                    kw = {k: v for k, v in (("scale", scale), ("bias", bias)) if v is not None}
                    if kw:
                        nc.scalar.activation(dst, tp[:, p, :], ACT.Identity, **kw).then_inc(written, 1)
                    else:
                        nc.scalar.copy(dst, tp[:, p, :]).then_inc(written, 1)


def load(nc, tag, pairs):
    with ExitStack() as ctx:
        loaded = ctx.enter_context(nc.semaphore(f"{tag}_loaded"))
        block = ctx.enter_context(nc.Block())

        @block.sync
        def _(sp):
            for dst, src in pairs:
                sp.dma_start(dst, src, allow_slow_non_contiguous=True).then_inc(loaded, 16)
            sp.wait_ge(loaded, 16 * len(pairs))


def experts(nc, env, a, tag):
    NT, NC_, T = env.NT, env.NC, env.NT * P
    E, F = 8, 512
    J = F // P
    row_scales(nc, env, tag + "sc", (1.0, 1e-5, 0.0, 1.0))
    with ExitStack() as outer:
        sb, ps, sem = scope(nc, outer, tag)
        w1T = sb("w1T", [P, E, F])
        w2T = sb("w2T", [P, E, J, P])
        b1 = sb("b1", [P, E, J])
        b2 = sb("b2", [E, P])
        centT = sb("centT", [P, E])
        gT, bT = sb("gT", [P, E]), sb("bT", [P, E])
        ZT = sb("ZT", [P, T])
        ohT = sb("ohT", [E, T])
        off = sb("off", [E, T], BF16)
        alpha = sb("alpha", [P, NT])
        with ExitStack() as prep:
            psb, pps, psem = scope(nc, prep, tag + "p")
            w1 = psb("w1", [P, E, J, P])
            w2 = psb("w2", [P, E, F])
            load(nc, tag + "ld", [
                (w1[:, :, :, :], a["W1"].rearrange("e (j p) c -> p e j c", p=P)),
                (w2[:, :, :], a["W2"].rearrange("e d f -> d e f")),
                (b1[:, :, :], a["b1"].rearrange("e (j p) -> p e j", p=P)),
                (b2[:, :], a["b2"]),
                (centT[:, :], a["centroids"].rearrange("e c -> c e")),
                (gT[:, :], a["gamma"].rearrange("e c -> c e")),
                (bT[:, :], a["beta"].rearrange("e c -> c e"))])
            turn_weights(nc, env, tag + "t", [],
                         [(w1[:, e, j, :], w1T[:, e, j * P:(j + 1) * P]) for e in range(E) for j in range(J)]
                         + [(w2[:, e, j * P:(j + 1) * P], w2T[:, e, j, :]) for e in range(E) for j in range(J)])
            pb = pps("pb", [P, E, J, E])
            shifted, folded = psem("shifted"), psem("folded")
            with nc.Block() as block:
                @block.tensor
                def _(pe):
                    for e in range(E):
                        for j in range(J):
                            ins = nc.tensor.matmul(pb[:, e, j, :], w1T[:, e, j * P:(j + 1) * P], bT[:, :],
                                                   start=True, stop=True)
                    ins.then_inc(shifted, 1)

                @block.vector
                def _(dve):
                    dve.wait_ge(shifted, 1)
                    for e in range(E):
                        nc.vector.tensor_tensor(b1[:, e, :], b1[:, e, :], pb[:, e, :, e], ALU.add).then_inc(folded, 1)
                        nc.vector.tensor_scalar(w1T[:, e, :], w1T[:, e, :], gT[:, e:e + 1], None,
                                                ALU.mult).then_inc(folded, 1)
                    dve.wait_ge(folded, 2 * E)
        front_pass(nc, env, tag + "f", True, ZT[:, :])
        with ExitStack() as ctx:
            sb, ps, sem = scope(nc, ctx, tag + "r")
            zc = sb("zc", [P, 2, CH])
            sc = sb("sc", [P, TPC, E])
            mx, m2, arg = sb("mx", [P, TPC]), sb("m2", [P, TPC]), sb("arg", [P, TPC])
            hot = sb("hot", [P, TPC, E])
            psc, po = ps("psc", [P, 512]), ps("po", [P, 512])
            copied, scored, vec, turned, done = sem("copied"), sem("scored"), sem("vec"), sem("turned"), sem("done")
            block = ctx.enter_context(nc.Block())
            STEPS = 9

            @block.gpsimd
            def _(pool):
                with pool.Fori(0, NC_ // 2) as it:
                    for p in range(2):
                        n = it * 2 + p
                        hold(pool, scored, n + 1)
                        nc.gpsimd.tensor_copy(zc[:, p, :], ZT[:, bass.ds(n * CH, CH)]).then_inc(copied, 1)

            @block.tensor
            def _(pe):
                pe.sem_inc(scored, 2)
                with pe.Fori(0, NC_ // 2) as it:
                    for p in range(2):
                        n = it * 2 + p
                        pe.wait_ge(copied, n + 1)
                        pe.wait_ge(vec, STEPS * n)
                        for k in range(TPC):
                            ins = nc.tensor.matmul(psc[:, k * E:(k + 1) * E], zc[:, p, k * P:(k + 1) * P],
                                                   centT[:, :], start=True, stop=True)
                        ins.then_inc(scored, 1)
                        pe.wait_ge(vec, STEPS * n + 8)
                        pe.wait_ge(done, 2 * n)
                        for k in range(TPC):
                            ins = nc.tensor.transpose(po[0:E, k * P:(k + 1) * P], hot[:, k, :], env.ident[:, :])
                        ins.then_inc(turned, 1)

            @block.vector
            def _(dve):
                with dve.Fori(0, NC_ // 2) as it:
                    for p in range(2):
                        n = it * 2 + p
                        link = Link(dve, vec, STEPS * n)
                        dve.wait_ge(scored, n + 3)
                        link(nc.vector.tensor_copy(sc[:, :, :], psc[:, 0:TPC * E].rearrange("p (k e) -> p k e", e=E)))
                        link(nc.vector.tensor_reduce(mx[:, :], sc[:, :, :], AX, ALU.max))
                        bm = mx[:, :].rearrange("p (k o) -> p k o", o=1).broadcast_to([P, TPC, E])
                        link(nc.vector.tensor_tensor(hot[:, :, :], sc[:, :, :], bm, ALU.is_equal))
                        link(nc.vector.tensor_tensor(sc[:, :, :], hot[:, :, :], env.firsts[:, 0:TPC, :], ALU.mult))
                        link(nc.vector.tensor_reduce(m2[:, :], sc[:, :, :], AX, ALU.max))
                        b2_ = m2[:, :].rearrange("p (k o) -> p k o", o=1).broadcast_to([P, TPC, E])
                        link(nc.vector.tensor_tensor(hot[:, :, :], sc[:, :, :], b2_, ALU.is_equal))
                        link(nc.vector.tensor_scalar(arg[:, :], mx[:, :], 1.0, None, ALU.mult))
                        link(nc.vector.tensor_tensor(mx[:, :], arg[:, :], env.root[:, bass.ds(n * TPC, TPC)], ALU.mult))
                        dve.wait_ge(turned, n + 1)
                        dve.wait_ge(done, 2 * n + 2)
                        link(nc.vector.tensor_scalar(off[:, bass.ds(n * CH, CH)], ohT[:, bass.ds(n * CH, CH)],
                                                     1.0, 1e30, ALU.subtract, ALU.mult))

            @block.scalar
            def _(act):
                with act.Fori(0, NC_ // 2) as it:
                    for p in range(2):
                        n = it * 2 + p
                        hold(act, vec, STEPS * n + 8)
                        nc.scalar.activation(alpha[:, bass.ds(n * TPC, TPC)], mx[:, :], ACT.Sigmoid).then_inc(done, 1)
                        hold(act, turned, n + 1)
                        nc.scalar.copy(ohT[:, bass.ds(n * CH, CH)], po[0:E, :]).then_inc(done, 1)
        with ExitStack() as ctx:
            sb, ps, sem = scope(nc, ctx, tag + "e")
            hid = sb("hid", [P, 4, CH])
            oT = sb("oT", [P, CH])
            ph, py, pt = ps("ph", [P, 3, 512]), ps("py", [P, 2, 512]), ps("pt", [P, 2, 512])
            made, relued, used, summed, held, turned, added = (sem(x) for x in (
                "made", "relued", "used", "summed", "held", "turned", "added"))
            back = Back(nc, env, sb, ps, sem)
            block = ctx.enter_context(nc.Block())
            U = E * J

            @block.tensor
            def _(pe):
                def second(n, u):
                    e, j = u // J, u % J
                    pe.wait_ge(relued, n * U + u + 1 + 4)
                    nc.tensor.matmul(py[:, 0, :], w2T[:, e, j, :], hid[:, u % 4, :], start=(u == 0), stop=False
                                     ).then_inc(used, 1)

                pe.sem_inc(used, 4)
                with pe.Fori(0, NC_) as n:
                    cols = bass.ds(n * CH, CH)
                    for u in range(U):
                        e, j = u // J, u % J
                        hold(pe, relued, n * U + u + 3)
                        hb = ph[:, 0, :] if u % 2 == 0 else ph[:, 1, :]
                        nc.tensor.matmul(hb, env.row[:, e, :], off[:, cols], start=True, stop=False)
                        nc.tensor.matmul(hb, w1T[:, e, j * P:(j + 1) * P], ZT[:, cols], start=False,
                                         stop=True).then_inc(made, 1)
                        if u == 1:
                            pe.wait_ge(held, n)
                        if u >= 2:
                            second(n, u - 2)
                    second(n, U - 2)
                    second(n, U - 1)
                    nc.tensor.matmul(py[:, 0, :], b2[:, :], ohT[:, cols], start=False, stop=True).then_inc(summed, 1)
                    pe.wait_ge(held, n + 1)
                    pe.wait_ge(added, n)
                    for k in range(TPC):
                        ins = nc.tensor.transpose(pt[:, 0, k * P:(k + 1) * P], oT[:, k * P:(k + 1) * P], env.ident[:, :])
                    ins.then_inc(turned, 1)

            @block.scalar
            def _(act):
                act.sem_inc(relued, 4)
                with act.Fori(0, NC_) as n:
                    for u in range(U):
                        e, j = u // J, u % J
                        act.wait_ge(made, n * U + u + 1)
                        act.wait_ge(used, n * U + u + 1)
                        nc.scalar.activation(hid[:, u % 4, :], ph[:, u % 2, :], ACT.Relu,
                                             bias=b1[:, e, j:j + 1]).then_inc(relued, 1)
                    act.wait_ge(summed, n + 1)
                    act.wait_ge(turned, n)
                    nc.scalar.copy(oT[:, :], py[:, 0, :]).then_inc(held, 1)

            @block.vector
            def _(dve):
                with dve.Fori(0, NC_) as n:
                    dve.wait_ge(turned, n + 1)
                    back.dve(dve, n, pt[:, 0, :].rearrange("p (k c) -> p k c", k=TPC), gain=alpha)
                    dve.sem_inc(added, 1)


def products(nc, env, tag, items):
    with ExitStack() as ctx:
        sb, ps, sem = scope(nc, ctx, tag)
        out = ps("out", [P, 4, 512])
        made, kept = sem("made"), sem("kept")
        block = ctx.enter_context(nc.Block())

        @block.tensor
        def _(pe):
            for j, (w, x, dst, scale) in enumerate(items):
                if j >= 4:
                    pe.wait_ge(kept, j - 3)
                f = dst.shape[1]
                nc.tensor.matmul(out[:, j % 4, 0:f], w, x, start=True, stop=True).then_inc(made, 1)

        @block.vector
        def _(dve):
            for j, (w, x, dst, scale) in enumerate(items):
                dve.wait_ge(made, j + 1)
                nc.vector.tensor_scalar(dst, out[:, j % 4, 0:dst.shape[1]], scale, None, ALU.mult).then_inc(kept, 1)
            dve.wait_ge(kept, len(items))


def attention(nc, env, a, tag):
    NT, NC_, T = env.NT, env.NC, env.NT * P
    HD, D = 8, 128
    row_scales(nc, env, tag + "sc", (float(D), 0.0, 1e-12, float(D) ** 0.5))
    with ExitStack() as outer:
        sb, ps, sem = scope(nc, outer, tag)
        M, N = sb("M", [P, HD, P]), sb("N", [P, HD, P])
        g = sb("g", [P, 1])
        ZT = sb("ZT", [P, T])
        with ExitStack() as prep:
            psb, pps, psem = scope(nc, prep, tag + "p")
            w = psb("w", [P, 3, HD, P])
            wo, woT = psb("wo", [P, HD * D]), psb("woT", [P, HD, P])
            load(nc, tag + "ld", [(w[:, :, :, :], a["w_qkv"].rearrange("(j h p) c -> p j h c", p=P, h=HD)),
                                  (wo[:, :], a["w_out"]),
                                  (g[:, :], a["gamma"].rearrange("(p o) -> p o", o=1))])
            turn_weights(nc, env, tag + "t", [], [(wo[:, h * P:(h + 1) * P], woT[:, h, :]) for h in range(HD)])
            products(nc, env, tag + "w",
                     [(w[:, 0, h, :], w[:, 1, h, :], M[:, h, :], float(D) ** -0.5) for h in range(HD)]
                     + [(w[:, 2, h, :], woT[:, h, :], N[:, h, :], g[:, 0:1]) for h in range(HD)])
        front_pass(nc, env, tag + "f", True, ZT[:, :], scale=g[:, 0:1])
        with ExitStack() as ctx:
            sb, ps, sem = scope(nc, ctx, tag + "a")
            vz = sb("vz", [P, 2, 2, P])
            qT = sb("qT", [P, 2, SEQ])
            pr = sb("pr", [P, 2, 3, P])
            pT = sb("pT", [P, 2, 3, P])
            nm, den, inv = sb("nm", [P, 2, 2]), sb("den", [P, 2, 2]), sb("inv", [P, 2, 2])
            yT = sb("yT", [P, 2, HD, SEQ])
            pq, psc, pp = ps("pq", [P, 2, 512]), ps("psc", [P, 2, 512]), ps("pp", [P, 2, 512])
            py, pout = ps("py", [P, 512]), ps("pout", [P, 512])
            valued, asked, q_in, scored, maxed, expd, scaled, turned, t_in, mixed, y_in, made, added = (
                sem(x) for x in ("valued", "asked", "qin", "scored", "maxed", "expd", "scaled", "turned", "tin",
                                 "mixed", "yin", "made", "added"))
            inner_ = sem("inner")
            back = Back(nc, env, sb, ps, sem, tiles=2)
            block = ctx.enter_context(nc.Block())
            NB = NT // 2
            U = 2 * HD

            @block.tensor
            def _(pe):
                def ask(it, u):
                    b, h = u // HD, u % HD
                    m = it * U + u
                    pe.wait_ge(q_in, m + 1)
                    nc.tensor.matmul(pq[:, u % 2, 0:SEQ], M[:, h, :], ZT[:, bass.ds((it * 2 + b) * SEQ, SEQ)],
                                     start=True, stop=True).then_inc(asked, 1)

                def score(it, u):
                    b = u // HD
                    m = it * U + u
                    pe.wait_ge(q_in, m + 3)
                    pe.wait_ge(expd, m + 1)
                    base = (it * 2 + b) * SEQ
                    S = psc[:, u % 2, :]
                    nc.tensor.matmul(S[:, 0:P], env.identb[:, :], env.causal[:, :], start=True, stop=False)
                    nc.tensor.matmul(S[:, 0:P], qT[:, u % 2, 0:P], ZT[:, bass.ds(base, P)], start=False, stop=True)
                    nc.tensor.matmul(S[:, 2 * P:3 * P], env.identb[:, :], env.causal[:, :], start=True, stop=True)
                    nc.tensor.matmul(S[:, P:3 * P], qT[:, u % 2, P:2 * P], ZT[:, bass.ds(base, SEQ)], start=False,
                                     stop=True, skip_group_check=True).then_inc(scored, 1)

                def turn(it, u):
                    m = it * U + u
                    pe.wait_ge(scaled, m + 1)
                    pe.wait_ge(t_in, m + 1)
                    for k in range(3):
                        ins = nc.tensor.transpose(pp[:, u % 2, k * P:(k + 1) * P], pr[:, u % 2, k, :], env.ident[:, :])
                    ins.then_inc(turned, 1)

                def mix(it, u):
                    b = u // HD
                    m = it * U + u
                    if u % HD == 0:
                        pe.wait_ge(valued, it * 2 + b + 1)
                    pe.wait_ge(t_in, m + 3)
                    pe.wait_ge(y_in, m)
                    nc.tensor.matmul(py[:, P:SEQ], vz[:, b, 1, :], pT[:, u % 2, 2, :], start=True, stop=True)
                    nc.tensor.matmul(py[:, 0:SEQ], vz[:, b, 0, :], pT[:, u % 2, 0:2, :], start=False,
                                     stop=True, skip_group_check=True).then_inc(mixed, 1)

                def project(it, b):
                    pe.wait_ge(y_in, it * U + (b + 1) * HD)
                    pe.wait_ge(added, it * 2 + b)
                    for k in range(2):
                        for h in range(HD):
                            ins = nc.tensor.matmul(pout[:, k * P:(k + 1) * P], yT[:, b, h, k * P:(k + 1) * P],
                                                   N[:, h, :], start=(h == 0), stop=(h == HD - 1))
                    ins.then_inc(made, 1)

                pe.sem_inc(turned, 2)
                with pe.Fori(0, NB // 2) as it:
                    ask(it, 0)
                    for u in range(U + 2):
                        if u + 1 < U:
                            ask(it, u + 1)
                        if u < U:
                            score(it, u)
                        if u >= 1 and u - 1 < U:
                            turn(it, u - 1)
                        if u >= 2:
                            mix(it, u - 2)
                        if u == HD + 3:
                            project(it, 0)
                    project(it, 1)

            @block.scalar
            def _(act):
                act.sem_inc(q_in, 2)
                act.sem_inc(expd, 2)
                with act.Fori(0, NB // 2) as it:
                    def q_copy(u):
                        m = it * U + u
                        act.wait_ge(asked, m + 1)
                        act.wait_ge(expd, m + 1)
                        nc.scalar.copy(qT[:, u % 2, :], pq[:, u % 2, 0:SEQ]).then_inc(q_in, 1)

                    def y_copy(u):
                        act.wait_ge(mixed, it * U + u + 1)
                        nc.scalar.copy(yT[:, u // HD, u % HD, :], py[:, 0:SEQ]).then_inc(y_in, 1)

                    q_copy(0)
                    for u in range(U + 2):
                        if u + 1 < U:
                            q_copy(u + 1)
                        if u < U:
                            m = it * U + u
                            act.wait_ge(maxed, m + 1)
                            act.wait_ge(turned, m - 1 + 2)
                            S = psc[:, u % 2, :]
                            nc.scalar.activation(pr[:, u % 2, 0, :], S[:, 0:P], ACT.Exp, bias=nm[:, u % 2, 0:1],
                                                 accum_out=den[:, u % 2, 0:1])
                            nc.scalar.activation(pr[:, u % 2, 1:3, :], S[:, P:3 * P].rearrange("p (k c) -> p k c", k=2),
                                                 ACT.Exp, bias=nm[:, u % 2, 1:2],
                                                 accum_out=den[:, u % 2, 1:2]).then_inc(expd, 1)
                        if u >= 2:
                            if u - 2 == 0:
                                act.wait_ge(made, 2 * it)
                            y_copy(u - 2)

            @block.vector
            def _(dve):
                def rows(it, b):
                    for k in range(2):
                        t = (it * 2 + b) * 2 + k
                        ins = nc.vector.tensor_scalar(vz[:, b, k, :], env.X[:, t, :], env.mean[:, bass.ds(t, 1)],
                                                      env.rnorm[:, bass.ds(t, 1)], ALU.subtract, ALU.mult)
                    ins.then_inc(valued, 1)

                dve.sem_inc(t_in, 2)
                with dve.Fori(0, NB // 2) as it:
                    dve.wait_ge(mixed, it * U)
                    rows(it, 0)
                    rows(it, 1)
                    for u in range(U + 1):
                        if u < U:
                            m = it * U + u
                            S = psc[:, u % 2, :]
                            dve.wait_ge(scored, m + 1)
                            nc.vector.tensor_reduce(nm[:, u % 2, 0:1], S[:, 0:P], AX, ALU.max, negate=True)
                            nc.vector.tensor_reduce(nm[:, u % 2, 1:2], S[:, P:3 * P], AX, ALU.max,
                                                    negate=True).then_inc(maxed, 1)
                        if u >= 1:
                            v = u - 1
                            m = it * U + v
                            if v >= 1:
                                w_ = v - 1
                                mm = it * U + w_
                                dve.wait_ge(turned, mm + 1 + 2)
                                dve.wait_ge(mixed, mm - 1 + 0) if w_ >= 2 else None
                                nc.vector.tensor_copy(pT[:, w_ % 2, :, :],
                                                      pp[:, w_ % 2, 0:3 * P].rearrange("p (k c) -> p k c", k=3)
                                                      ).then_inc(t_in, 1)
                            dve.wait_ge(expd, m + 1 + 2)
                            nc.vector.reciprocal(inv[:, v % 2, :], den[:, v % 2, :]).then_inc(inner_, 1)
                            dve.wait_ge(inner_, m + 1)
                            nc.vector.tensor_scalar(pr[:, v % 2, 0, :], pr[:, v % 2, 0, :], inv[:, v % 2, 0:1], None,
                                                    ALU.mult)
                            nc.vector.tensor_scalar(pr[:, v % 2, 1:3, :], pr[:, v % 2, 1:3, :], inv[:, v % 2, 1:2], None,
                                                    ALU.mult).then_inc(scaled, 1)
                        if u == HD + 5:
                            dve.wait_ge(made, it * 2 + 1)
                            back.dve(dve, it * 2, pout[:, 0:2 * P].rearrange("p (k c) -> p k c", k=2), y=False)
                            dve.sem_inc(added, 1)
                    dve.wait_ge(turned, it * U + U + 2)
                    nc.vector.tensor_copy(pT[:, 1, :, :], pp[:, 1, 0:3 * P].rearrange("p (k c) -> p k c", k=3)
                                          ).then_inc(t_in, 1)
                    dve.wait_ge(made, it * 2 + 2)
                    back.dve(dve, it * 2 + 1, pout[:, 0:2 * P].rearrange("p (k c) -> p k c", k=2), y=False)
                    dve.sem_inc(added, 1)


def product_keys(nc, env, a, tag):
    NT, NC_, T = env.NT, env.NC, env.NT * P
    HD, K, NE = 8, 32, 1024
    J = NE // P
    row_scales(nc, env, tag + "sc", (1.0, 1e-6, 0.0, 1.0))
    with ExitStack() as outer:
        sb, ps, sem = scope(nc, outer, tag)
        G = sb("G", [P, HD, 2, K])
        downT, up = sb("downT", [P, NE]), sb("up", [P, J, P])
        g = sb("g", [P, 1])
        ZT = sb("ZT", [P, T])
        with ExitStack() as prep:
            psb, pps, psem = scope(nc, prep, tag + "p")
            wq = psb("wq", [P, HD * 2, P])
            keys = psb("keys", [P, 2, 2, P])
            keysT = psb("keysT", [P, 2, HD * K])
            down = psb("down", [P, J, P])
            load(nc, tag + "ld", [(wq[:, :, :], a["w_q"].rearrange("(j p) c -> p j c", p=P)),
                                  (keys[:, :, :, :], a["keys"].rearrange("(u h) k s d -> (h k) u s d", u=2)),
                                  (down[:, :, :], a["expert_down"].rearrange("(j p) c -> p j c", p=P)),
                                  (up[:, :, :], a["expert_up"].rearrange("(j p) c -> p j c", p=P)),
                                  (g[:, :], a["norm_w"].rearrange("(p o) -> p o", o=1))])
            turn_weights(nc, env, tag + "t", [],
                         [(down[:, j, :], downT[:, j * P:(j + 1) * P]) for j in range(J)]
                         + [(keys[:, t, s, :], keysT[:, s, t * P:(t + 1) * P]) for t in range(2) for s in range(2)])
            products(nc, env, tag + "w", [(wq[:, 2 * h + s, :], keysT[:, s, h * K:(h + 1) * K], G[:, h, s, :], 1.0)
                                          for h in range(HD) for s in range(2)])
        front_pass(nc, env, tag + "f", True, ZT[:, :], scale=g[:, 0:1])
        with ExitStack() as ctx:
            sb, ps, sem = scope(nc, ctx, tag + "a")
            zc = sb("zc", [P, 2, P])
            sims = sb("sims", [P, 2, HD, 2, K])
            top = sb("top", [P, 2, HD, 2, 8])
            cand = sb("cand", [P, HD, 8, 8])
            best = sb("best", [P, HD, 8])
            thr = sb("thr", [P, HD])
            sums = sb("sums", [P, 4, K, K])
            w = sb("w", [P, 2, NE])
            gl = sb("gl", [P, 2, J, P])
            hid = sb("hid", [P, J, P])
            psim, phd, pw, pout = ps("psim", [P, 512]), ps("phd", [P, J, P]), ps("pw", [P, 2, J, P]), ps("pout", [P, 512])
            copied, scored, s_in, pooled, vec, weighed, summed, hidden, gelud, mixed, made, added = (
                sem(x) for x in ("copied", "scored", "sin", "pooled", "vec", "weighed", "summed", "hidden",
                                 "gelud", "mixed", "made", "added"))
            back = Back(nc, env, sb, ps, sem, tiles=1)
            block = ctx.enter_context(nc.Block())
            OURS = [h for h in range(HD) if h % 4 != 3 or True]
            POOL = [h for h in range(HD) if h % 3 == 2]
            NPOOL, NDVE = len(POOL), HD - len(POOL)

            def sum_of(p, h):
                s1 = sims[:, p, h, 0, :].rearrange("p (i o) -> p i o", o=1).broadcast_to([P, K, K])
                s2 = sims[:, p, h, 1, :].rearrange("p (o j) -> p o j", o=1).broadcast_to([P, K, K])
                return s1, s2

            STEPS = 4 + NDVE

            @block.gpsimd
            def _(pool):
                with pool.Fori(0, NT // 2) as it:
                    for p in range(2):
                        t = it * 2 + p
                        hold(pool, scored, t + 1)
                        nc.gpsimd.tensor_copy(zc[:, p, :], ZT[:, bass.ds(t * P, P)]).then_inc(copied, 1)
                        pool.wait_ge(s_in, t + 1 + 2)
                        for k, h in enumerate(POOL):
                            pool.wait_ge(weighed, t * HD + (POOL[k - 2] + 1 if k >= 2 else POOL[NPOOL - 2 + k] + 1 - HD) + HD)
                            s1, s2 = sum_of(p, h)
                            nc.gpsimd.tensor_tensor(sums[:, 2 + k % 2, :, :], s1, s2, ALU.add).then_inc(pooled, 1)

            @block.tensor
            def _(pe):
                pe.sem_inc(scored, 2)
                pe.sem_inc(summed, 2)
                with pe.Fori(0, NT // 2) as it:
                    def sim(p):
                        t = it * 2 + p
                        pe.wait_ge(copied, t + 1)
                        pe.wait_ge(s_in, t + 2)
                        nc.tensor.matmul(psim[:, :], zc[:, p, :], G[:, :, :, :].rearrange("p h s k -> p (h s k)"),
                                         start=True, stop=True).then_inc(scored, 1)
                        pe.wait_ge(gelud, t + 2)
                        for j in range(J):
                            ins = nc.tensor.matmul(phd[:, j, :], downT[:, j * P:(j + 1) * P], ZT[:, bass.ds(t * P, P)],
                                                   start=True, stop=True)
                        ins.then_inc(hidden, 1)

                    def out(p):
                        t = it * 2 + p
                        pe.wait_ge(mixed, t + 1)
                        pe.wait_ge(added, t)
                        for j in range(J):
                            ins = nc.tensor.matmul(pout[:, 0:P], hid[:, j, :], up[:, j, :], start=(j == 0), stop=(j == J - 1))
                        ins.then_inc(made, 1)

                    sim(0)
                    for p in range(2):
                        t = it * 2 + p
                        pe.wait_ge(mixed, t - 1 + 0) if p == 1 else pe.wait_ge(mixed, t)
                        for h in range(HD):
                            pe.wait_ge(weighed, t * HD + h + 1 + HD)
                            for j in range(J):
                                ins = nc.tensor.matmul(pw[:, p, j, :], w[:, h % 2, j * P:(j + 1) * P], env.ident[:, :],
                                                       start=(h == 0 and j % 4 == 0), stop=(h == HD - 1 and j % 4 == 3),
                                                       skip_group_check=True)
                            ins.then_inc(summed, 1)
                            if p == 0 and h == 1:
                                sim(1)
                            if p == 1 and h == 3:
                                out(0)
                    out(1)

            @block.scalar
            def _(act):
                act.sem_inc(s_in, 2)
                act.sem_inc(gelud, 2)
                with act.Fori(0, NT // 2) as it:
                    for p in range(2):
                        t = it * 2 + p
                        act.wait_ge(scored, t + 1 + 2)
                        act.wait_ge(weighed, (t - 1) * HD + HD)
                        nc.scalar.copy(sims[:, p, :, :, :].rearrange("p h s k -> p (h s k)"), psim[:, :]).then_inc(s_in, 1)
                        act.wait_ge(hidden, t + 1)
                        act.wait_ge(mixed, t - 1) if p == 1 else act.wait_ge(mixed, t)
                        for q in range(2):
                            ins = nc.scalar.activation(gl[:, p, 4 * q:4 * q + 4, :], phd[:, 4 * q:4 * q + 4, :], ACT.Gelu)
                        ins.then_inc(gelud, 1)

            @block.vector
            def _(dve):
                def finish(it, p):
                    t = it * 2 + p
                    dve.wait_ge(summed, (t + 1) * HD + 2)
                    dve.wait_ge(gelud, t + 1 + 2)
                    dve.wait_ge(made, t)
                    for q in range(2):
                        ins = nc.vector.tensor_tensor(hid[:, 4 * q:4 * q + 4, :], gl[:, p, 4 * q:4 * q + 4, :],
                                                      pw[:, p, 4 * q:4 * q + 4, :], ALU.mult)
                    ins.then_inc(mixed, 1)

                def residual(it, p):
                    t = it * 2 + p
                    dve.wait_ge(made, t + 1)
                    back.dve(dve, t, pout[:, 0:P].rearrange("p (k c) -> p k c", k=1), y=False)
                    dve.sem_inc(added, 1)

                dve.sem_inc(weighed, HD)
                with dve.Fori(0, NT // 2) as it:
                    for p in range(2):
                        t = it * 2 + p
                        hold(dve, s_in, t + 1 + 2)
                        link = Link(dve, vec, STEPS * t)
                        for h in range(HD):
                            for s in range(2):
                                ins = nc.vector.max(top[:, p, h, s, :], sims[:, p, h, s, :])
                        link(ins)
                        t1 = top[:, p, :, 0, :].rearrange("p h (i o) -> p h i o", o=1).broadcast_to([P, HD, 8, 8])
                        t2 = top[:, p, :, 1, :].rearrange("p h (o i) -> p h o i", o=1).broadcast_to([P, HD, 8, 8])
                        link(nc.vector.tensor_tensor(cand[:, :, :, :], t1, t2, ALU.add))
                        dve.nop(nofuse=True)
                        for h in range(HD):
                            ins = nc.vector.max(best[:, h, :], cand[:, h, :, :].rearrange("p i j -> p (i j)"))
                        link(ins)
                        link(nc.vector.tensor_scalar(thr[:, :], best[:, :, 7], 1.1754944e-38, None, ALU.max))
                        mine = [h for h in range(HD) if h not in POOL]

                        def form(k):
                            s1, s2 = sum_of(p, mine[k])
                            link.inc(nc.vector.tensor_tensor(sums[:, k % 2, :, :], s1, s2, ALU.add))

                        for h in range(HD):
                            if h in POOL:
                                k = POOL.index(h)
                                dve.wait_ge(pooled, t * NPOOL + k + 1)
                                src = sums[:, 2 + k % 2, :, :]
                            else:
                                k = mine.index(h)
                                if k >= 2:
                                    dve.wait_ge(weighed, t * HD + mine[k - 2] + 1 + HD)
                                form(k)
                                link.wait()
                                src = sums[:, k % 2, :, :]
                            dve.wait_ge(summed, t * HD + h + 1)
                            nc.vector.scalar_tensor_tensor(w[:, h % 2, :].rearrange("p (i j) -> p i j", i=K), src,
                                                           thr[:, h:h + 1], src, ALU.is_ge, ALU.mult).then_inc(weighed, 1)
                            if p == 1 and h == 1:
                                finish(it, 0)
                            if p == 1 and h == 5:
                                residual(it, 0)
                    finish(it, 1)
                    residual(it, 1)


def rotary(nc, env, a, tag):
    NT, NC_, T = env.NT, env.NC, env.NT * P
    HD, D, S = 16, 8, 8
    NB = NT // 2
    row_scales(nc, env, tag + "sc", None)
    with ExitStack() as outer:
        sb, ps, sem = scope(nc, outer, tag)
        wT, pT = sb("wT", [P, 3 * P]), sb("pT", [P, P])
        wkq, qw = sb("wkq", [P, D]), sb("qw", [P, D])
        KK, QQ = sb("KK", [P, NT, P]), sb("QQ", [P, NT, P])
        V = sb("V", [P, NT, HD, D + 1])
        norm2 = sb("norm2", [P, 2, NT, HD])
        with ExitStack() as prep:
            psb, pps, psem = scope(nc, prep, tag + "p")
            w, pw = psb("w", [P, 3, P]), psb("pw", [P, P])
            ZT = psb("ZT", [P, T])
            zc = psb("zc", [P, 2, CH])
            rope = psb("rope", [P, 2, 2, P])
            load(nc, tag + "ld", [(w[:, :, :], a["W_kqv"].rearrange("(j p) c -> p j c", p=P)),
                                  (pw[:, :], a["W_proj"]),
                                  (rope[:, :, :, :], a["rope"]),
                                  (wkq[:, :], a["k_norm_w"].rearrange("(o d) -> o d", o=1).broadcast_to([P, D])),
                                  (qw[:, :], a["q_norm_w"].rearrange("(o d) -> o d", o=1).broadcast_to([P, D]))])
            turn_weights(nc, env, tag + "t", [], [(w[:, j, :], wT[:, j * P:(j + 1) * P]) for j in range(3)]
                         + [(pw[:, :], pT[:, :])])
            front_pass(nc, env, tag + "f", False, ZT[:, :])
            t1, t2 = psb("t1", [P, 2, 2, 2 * P]), psb("t2", [P, 2, 2, 2 * P])
            sq = psb("sq", [P, 2, TPC, P])
            pk, pv = pps("pk", [P, 2, TPC, 2 * P]), pps("pv", [P, 2, TPC, P])
            copied, made, taken, vin, cosd, rotated, squared, normed = (psem(x) for x in (
                "copied", "made", "taken", "vin", "cosd", "rotated", "squared", "normed"))
            with nc.Block() as block:
                @block.gpsimd
                def _(pool):
                    nc.gpsimd.memset(V[:, :, :, D:D + 1], 1.0)
                    with pool.Fori(0, NC_ // 2) as it:
                        for p in range(2):
                            n = it * 2 + p
                            hold(pool, made, n + 1)
                            nc.gpsimd.tensor_copy(zc[:, p, :], ZT[:, bass.ds(n * CH, CH)]).then_inc(copied, 1)
                            for q in range(2):
                                m = 2 * n + q
                                pool.wait_ge(cosd, 3 * m + 3 + 12)
                                for z, dst in ((0, KK), (1, QQ)):
                                    ins = nc.gpsimd.tensor_tensor(dst[:, bass.ds(2 * m, 2), :], t1[:, q, :, z * P:(z + 1) * P],
                                                                  t2[:, q, :, z * P:(z + 1) * P], ALU.add)
                                ins.then_inc(rotated, 1)

                @block.tensor
                def _(pe):
                    pe.sem_inc(made, 2)
                    with pe.Fori(0, NC_ // 2) as it:
                        for p in range(2):
                            n = it * 2 + p
                            pe.wait_ge(copied, n + 1)
                            pe.wait_ge(cosd, 6 * n + 6)
                            pe.wait_ge(vin, n + 1)
                            for k in range(TPC):
                                z = zc[:, p, k * P:(k + 1) * P]
                                nc.tensor.matmul(pk[:, p, k, :], z, wT[:, 0:2 * P], start=True, stop=True)
                                ins = nc.tensor.matmul(pv[:, p, k, :], z, wT[:, 2 * P:3 * P], start=True, stop=True)
                            ins.then_inc(made, 1)

                @block.vector
                def _(dve):
                    dve.sem_inc(cosd, 12)
                    with dve.Fori(0, NC_ // 2) as it:
                        for p in range(2):
                            n = it * 2 + p
                            dve.wait_ge(made, n + 1 + 2)
                            for q in range(2):
                                m = 2 * n + q
                                dve.wait_ge(rotated, m)
                                for z in range(2):
                                    x = pk[:, p, 2 * q:2 * q + 2, z * P:(z + 1) * P]
                                    ins = nc.vector.tensor_tensor(t1[:, q, :, z * P:(z + 1) * P], x, rope[:, :, 0, :], ALU.mult)
                                ins.then_inc(cosd, 1)
                                for half in range(2):
                                    for z in range(2):
                                        def part(v, f):
                                            return v.rearrange("p t (h f d) -> p t h f d", f=2, d=D // 2)[:, :, :, f, :]
                                        x = part(pk[:, p, 2 * q:2 * q + 2, z * P:(z + 1) * P], 1 - half)
                                        ins = nc.vector.tensor_tensor(part(t2[:, q, :, z * P:(z + 1) * P], half), x,
                                                                      part(rope[:, :, 1, :], half), ALU.mult)
                                    ins.then_inc(cosd, 1)
                            for z in range(2):
                                dve.wait_ge(squared, 2 * n + z + 1)
                                nc.vector.tensor_reduce(norm2[:, z, bass.ds(n * TPC, TPC), :],
                                                        sq[:, z, :, :].rearrange("p t (h d) -> p t h d", d=D), AX,
                                                        ALU.add).then_inc(normed, 1)

                @block.scalar
                def _(act):
                    act.sem_inc(vin, 2)
                    with act.Fori(0, NC_ // 2) as it:
                        for p in range(2):
                            n = it * 2 + p
                            hold(act, made, n + 1 + 2)
                            for k in range(TPC):
                                ins = nc.scalar.copy(V[:, n * TPC + k, :, 0:D], pv[:, p, k, :].rearrange(
                                    "p (h d) -> p h d", d=D))
                            ins.then_inc(vin, 1)
                            act.wait_ge(rotated, 2 * n + 2)
                            hold(act, normed, 2 * n)
                            for z, src in ((0, KK), (1, QQ)):
                                nc.scalar.activation(sq[:, z, :, :], src[:, bass.ds(n * TPC, TPC), :], ACT.Square
                                                     ).then_inc(squared, 1)
        with ExitStack() as ctx:
            sb, ps, sem = scope(nc, ctx, tag + "n")
            rms = sb("rms", [P, 2, NT, HD])
            rooted, vec, done, weighed = sem("rooted"), sem("vec"), sem("done"), sem("weighed")
            block = ctx.enter_context(nc.Block())

            @block.scalar
            def _(act):
                nc.scalar.activation(rms[:, :, :, :], norm2[:, :, :, :], ACT.Sqrt, scale=1.0 / D).then_inc(rooted, 1)

            @block.vector
            def _(dve):
                link = Link(dve, vec)
                link(nc.vector.tensor_tensor(wkq[:, :], wkq[:, :], qw[:, :], ALU.mult))
                dve.wait_ge(rooted, 1)
                link(nc.vector.tensor_scalar(rms[:, :, :, :], rms[:, :, :, :], 1e-6, None, ALU.add))
                link(nc.vector.reciprocal(norm2[:, :, :, :], rms[:, :, :, :]))
                for z, x in ((0, KK), (1, QQ)):
                    v = x[:, :, :].rearrange("p t (h d) -> p (t h) d", d=D)
                    f = norm2[:, z, :, :].rearrange("p t (h o) -> p (t h) o", o=1).broadcast_to([P, NT * HD, D])
                    nc.vector.tensor_tensor(v, v, f, ALU.mult).then_inc(done, 1)
                dve.wait_ge(done, 1)
                v = KK[:, :, :].rearrange("p t (h d) -> p (t h) d", d=D)
                f = wkq[:, :].rearrange("p (o d) -> p o d", o=1).broadcast_to([P, NT * HD, D])
                link(nc.vector.scalar_tensor_tensor(v, v, float(D) ** -0.5, f, ALU.mult, ALU.mult))
                dve.wait_ge(done, 2)
        with ExitStack() as ctx:
            sb, ps, sem = scope(nc, ctx, tag + "a")
            KS, QS = sb("KS", [P, 2, 2 * HD * S * D], BF16), sb("QS", [P, 2, 2 * HD * S * D], BF16)
            rk, rq = sb("rk", [P, 2, 2 * P]), sb("rq", [P, 2, 2 * P])
            KT, QT = sb("KT", [P, 2, HD // 2, SEQ], BF16), sb("QT", [P, 2, HD // 2, SEQ], BF16)
            nm = sb("nm", [P, 2, HD])
            nr = sb("nr", [P, 2, HD])
            nb = sb("nb", [P, 2, 2, 64], BF16)
            nT = sb("nT", [P, 2, SEQ], BF16)
            pr = sb("pr", [P, 3, 3 * P])
            inv = sb("inv", [P, 2, HD])
            yt, yT = sb("yt", [P, 2, HD, D]), sb("yT", [P, SEQ])
            ptr = ps("ptr", [P, 2, 1024], BF16)
            psc, pst = ps("psc", [P, 2, 512]), ps("pst", [P, 2, 512])
            py, pout = ps("py", [P, 2, HD, 16]), ps("pout", [P, 512])
            (zeroed, kcast, qcast, krest, qrest, placed, t_in, scored, maxed, nmaxed, n_placed, n_in, shifted, expd, mixed,
             y_norm, y_placed, y_in, made, added, ainv) = (sem(x) for x in (
                "zeroed", "kcast", "qcast", "krest", "qrest", "placed", "tin", "scored", "maxed", "nmaxed",
                "nplaced", "nin", "shifted", "expd", "mixed", "ynorm", "yplaced", "yin", "made", "added", "ainv"))
            back = Back(nc, env, sb, ps, sem, tiles=2)
            block = ctx.enter_context(nc.Block())

            def first_head(u):
                g = 8 * (u // 3 % 2) + u // 6
                return g if u % 3 == 0 else g + 4 * (u % 3 - 1)

            def slots(buf, p):
                return buf[:, p, :].rearrange("p (g s d) -> p g s d", s=S, d=D)

            def spread(x, k):
                return x.rearrange("p (g o d) -> p g o d", o=1, d=D).broadcast_to([P, 2 * HD, k, D])

            def heads(x):
                return x.rearrange("p (g d) -> p g d", d=D)

            def steps(eng, first, second, tail):
                first(0, 0)
                with eng.Fori(0, NB // 2 - 1) as it:
                    second(it * 2, 0, True)
                    second(it * 2 + 1, 1, True)
                second(NB - 2, 0, True)
                second(NB - 1, 1, False)

            @block.scalar
            def _(act):
                def cast(n, p):
                    k = KK[:, bass.ds(2 * n, 2), :].rearrange("p t c -> p (t c)")
                    ks = slots(KS, p)
                    hold(act, placed, 4 * (n - 1) + 4)
                    nc.scalar.copy(ks[:, :, 0:3, :], spread(k, 3)).then_inc(kcast, 1)
                    act.wait_ge(krest, 2 * n + 1)
                    nc.scalar.copy(ks[:, :, 3:5, :], spread(rk[:, 0, :], 2)).then_inc(kcast, 1)
                    act.wait_ge(krest, 2 * n + 2)
                    nc.scalar.copy(ks[:, :, 5, :], heads(rk[:, 1, :])).then_inc(kcast, 1)

                def second(n, p, more):
                    for h in range(HD):
                        m = n * HD + h
                        act.wait_ge(shifted, m + 1)
                        act.wait_ge(mixed, m + 1)
                        nc.scalar.activation(pr[:, h % 2, :], pst[:, h % 2, 0:3 * P], ACT.Exp).then_inc(expd, 1)
                        if h == 1 and more:
                            cast(n + 1, 1 - p)
                    act.wait_ge(y_placed, n + 1)
                    nc.scalar.copy(yT[:, :], pout[:, 0:SEQ]).then_inc(y_in, 1)

                act.sem_inc(expd, 2)
                act.wait_ge(zeroed, 1)
                steps(act, cast, second, None)

            @block.gpsimd
            def _(pool):
                nc.gpsimd.memset(KS[:, :, :], 0.0).then_inc(zeroed, 1)
                nc.gpsimd.memset(QS[:, :, :], 0.0).then_inc(zeroed, 1)
                nc.gpsimd.memset(nb[:, :, :, :], 0.0).then_inc(zeroed, 1)

                def rest(n, p):
                    ks, qs = slots(KS, p), slots(QS, p)
                    k = KK[:, bass.ds(2 * n, 2), :].rearrange("p t (h d) -> p (t h) d", d=D)
                    q = QQ[:, bass.ds(2 * n, 2), :].rearrange("p t (h d) -> p (t h) d", d=D)
                    pool.wait_ge(kcast, 3 * n + 1)
                    nc.gpsimd.tensor_tensor(heads(rk[:, 0, :]), k, ks[:, :, 0, :], ALU.subtract).then_inc(krest, 1)
                    pool.wait_ge(qcast, 5 * n + 2)
                    nc.gpsimd.tensor_tensor(heads(rq[:, 0, :]), q, qs[:, :, 0, :], ALU.subtract).then_inc(qrest, 1)
                    pool.wait_ge(kcast, 3 * n + 2)
                    pool.wait_ge(krest, 2 * n + 1)
                    nc.gpsimd.tensor_tensor(heads(rk[:, 1, :]), heads(rk[:, 0, :]), ks[:, :, 3, :], ALU.subtract).then_inc(krest, 1)
                    pool.wait_ge(qcast, 5 * n + 4)
                    pool.wait_ge(qrest, 2 * n + 1)
                    nc.gpsimd.tensor_tensor(heads(rq[:, 1, :]), heads(rq[:, 0, :]), qs[:, :, 1, :], ALU.subtract).then_inc(qrest, 1)

                def second(n, p, more):
                    if more:
                        rest(n + 1, 1 - p)

                steps(pool, rest, second, None)

            @block.tensor
            def _(pe):
                def place(n, p, g):
                    m = 4 * n + g
                    if g == 0:
                        pe.wait_ge(kcast, 3 * n + 3)
                    if g == 2:
                        pe.wait_ge(qcast, 5 * n + 5)
                    pe.wait_ge(t_in, m + 1)
                    src = (KS if g < 2 else QS)[:, p, :].rearrange("p (t a c) -> p t a c", t=2, c=P)
                    for a_ in range(4):
                        for t in range(2):
                            ins = nc.tensor.transpose(ptr[:, g % 2, (a_ * 2 + t) * P:(a_ * 2 + t + 1) * P],
                                                      src[:, t, 4 * (g % 2) + a_, :], env.identb[:, :])
                    ins.then_inc(placed, 1)

                def rows_of(h):
                    return slice(64 * (h % 2), 64 * (h % 2) + 64)

                def score(n, p, u):
                    m = 12 * n + u
                    if u == 0:
                        pe.wait_ge(t_in, 4 * n + 4 + 2)
                    pe.wait_ge(maxed, m + 1)
                    B = psc[:, u % 2, :]
                    g = first_head(u)
                    if u % 3 == 0:
                        for k in range(4):
                            h = g + 2 * k
                            r_ = rows_of(h)
                            o = B[:, k * P:(k + 1) * P]
                            nc.tensor.matmul(o, env.identb[:, :], env.causal[:, :], start=True, stop=False)
                            ins = nc.tensor.matmul(o, QT[r_, p, h // 2, 0:P], KT[r_, p, h // 2, 0:P], start=False, stop=True)
                    else:
                        for k in range(2):
                            h = g + 2 * k
                            r_ = rows_of(h)
                            nc.tensor.matmul(B[:, k * SEQ + P:(k + 1) * SEQ], env.identb[:, :], env.causal[:, :],
                                             start=True, stop=True)
                            ins = nc.tensor.matmul(B[:, k * SEQ:(k + 1) * SEQ], QT[r_, p, h // 2, P:SEQ],
                                                   KT[r_, p, h // 2, :], start=False, stop=True, skip_group_check=True)
                    ins.then_inc(scored, 1)

                def turn_max(n, p):
                    pe.wait_ge(nmaxed, 5 * n + 5)
                    pe.wait_ge(t_in, 4 * n + 4 + 2)
                    for t in range(2):
                        ins = nc.tensor.transpose(ptr[:, 0, t * P:(t + 1) * P],
                                                  nb[:, t, :, :].rearrange("p s h -> p (s h)"), env.identb[:, :])
                    ins.then_inc(n_placed, 1)

                def shift(n, p, h):
                    m = n * HD + h
                    pe.wait_ge(expd, m + 1)
                    if h == 0:
                        pe.wait_ge(n_in, n + 1)
                    B = pst[:, h % 2, :]
                    r_ = rows_of(h)
                    one = env.three[r_, h, :]
                    for c0, c1, j0, i0 in ((0, SEQ, 0, 0), (SEQ, SEQ + P, P, P)):
                        nc.tensor.matmul(B[:, c0:c0 + P], env.identb[:, :], env.causalT[:, :], start=True, stop=True)
                        nc.tensor.matmul(B[:, c0:c1], one, nT[r_, p, i0:SEQ], start=False, stop=True, skip_group_check=True)
                        ins = nc.tensor.matmul(B[:, c0:c1], KT[r_, p, h // 2, j0:j0 + P], QT[r_, p, h // 2, i0:SEQ],
                                               start=False, stop=True, skip_group_check=True)
                    ins.then_inc(shifted, 1)

                def mix(n, p, h):
                    m = n * HD + h
                    pe.wait_ge(expd, m + 1 + 2)
                    if h == 0:
                        pe.wait_ge(y_norm, n)
                    e = pr[:, h % 2, :]
                    v0, v1 = V[:, 2 * n, h, :], V[:, 2 * n + 1, h, :]
                    nc.tensor.matmul(py[:, 0, h, 0:D + 1], e[:, 0:P], v0, start=True, stop=True)
                    nc.tensor.matmul(py[:, 1, h, 0:D + 1], e[:, P:2 * P], v0, start=True, stop=False)
                    nc.tensor.matmul(py[:, 1, h, 0:D + 1], e[:, 2 * P:3 * P], v1, start=False, stop=True).then_inc(mixed, 1)

                def first(n, p):
                    for g in range(4):
                        place(n, p, g)
                    for u in range(12):
                        score(n, p, u)
                    turn_max(n, p)

                def second(n, p, more):
                    A = []
                    if more:
                        A = [lambda g=g: place(n + 1, 1 - p, g) for g in range(4)]
                        A += [lambda u=u: score(n + 1, 1 - p, u) for u in range(12)]
                    for h in range(HD + 1):
                        if h < HD:
                            shift(n, p, h)
                        if h >= 3:
                            for _ in range(2):
                                if A:
                                    A.pop(0)()
                        if h >= 1:
                            mix(n, p, h - 1)
                    while A:
                        A.pop(0)()
                    pe.wait_ge(y_norm, n + 1)
                    pe.wait_ge(added, n)
                    for t in range(2):
                        ins = nc.tensor.transpose(pout[:, t * P:(t + 1) * P], yt[:, t, :, :].rearrange("p h d -> p (h d)"),
                                                  env.ident[:, :])
                    ins.then_inc(y_placed, 1)
                    if more:
                        turn_max(n + 1, 1 - p)
                    pe.wait_ge(y_in, n + 1)
                    for t in range(2):
                        ins = nc.tensor.matmul(pout[:, SEQ + t * P:SEQ + (t + 1) * P], yT[:, t * P:(t + 1) * P], pT[:, :],
                                               start=True, stop=True)
                    ins.then_inc(made, 1)

                pe.sem_inc(placed, 4)
                pe.sem_inc(mixed, 2)
                steps(pe, first, second, None)

            @block.vector
            def _(dve):
                def cast(n, p):
                    q = QQ[:, bass.ds(2 * n, 2), :].rearrange("p t (h d) -> p (t h) d", d=D)
                    qs = slots(QS, p)
                    q1 = QQ[:, bass.ds(2 * n, 2), :].rearrange("p t c -> p (t c)")
                    hold(dve, placed, 4 * (n - 1) + 4)
                    nc.vector.tensor_copy(qs[:, :, 0, :], q).then_inc(qcast, 1)
                    nc.vector.tensor_copy(qs[:, :, 3:6:2, :], spread(q1, 2)).then_inc(qcast, 1)
                    dve.wait_ge(qrest, 2 * n + 1)
                    nc.vector.tensor_copy(qs[:, :, 1, :], heads(rq[:, 0, :])).then_inc(qcast, 1)
                    nc.vector.tensor_copy(qs[:, :, 4, :], heads(rq[:, 0, :])).then_inc(qcast, 1)
                    dve.wait_ge(qrest, 2 * n + 2)
                    nc.vector.tensor_copy(qs[:, :, 2, :], heads(rq[:, 1, :])).then_inc(qcast, 1)

                def maxima(n, p):
                    for g in range(4):
                        dve.wait_ge(placed, 4 * n + g + 1 + 4)
                        dst = (KT if g < 2 else QT)[:, p, 4 * (g % 2):4 * (g % 2) + 4, :]
                        nc.vector.tensor_copy(dst, ptr[:, g % 2, :].rearrange("p (a c) -> p a c", a=4)).then_inc(t_in, 1)
                    for u in range(12):
                        g = first_head(u)
                        dve.wait_ge(scored, 12 * n + u + 1)
                        if u % 3 == 0:
                            dst, src = nm[:, 0, g:g + 7:2], psc[:, u % 2, :].rearrange("p (k c) -> p k c", k=4)
                        else:
                            dst, src = nm[:, 1, g:g + 3:2], psc[:, u % 2, :].rearrange("p (k c) -> p k c", k=2)
                        nc.vector.tensor_reduce(dst, src, AX, ALU.max, negate=True).then_inc(maxed, 1)
                    dve.wait_ge(maxed, 12 * n + 12 + 2)
                    dve.wait_ge(n_placed, n)
                    link = Link(dve, nmaxed, 5 * n)
                    def both(x):
                        return x.rearrange("p t (o h) -> p t o h", o=1).broadcast_to([P, 2, 2, HD])

                    link(nc.vector.tensor_copy(nb[:, :, :, 0:HD], both(nm[:, :, :])))
                    link(nc.vector.tensor_tensor(nr[:, :, :], nm[:, :, :], nb[:, :, 0, 0:HD], ALU.subtract))
                    link(nc.vector.tensor_copy(nb[:, :, :, HD:2 * HD], both(nr[:, :, :])))
                    link(nc.vector.tensor_tensor(nm[:, :, :], nr[:, :, :], nb[:, :, 0, HD:2 * HD], ALU.subtract))
                    link(nc.vector.tensor_copy(nb[:, :, :, 2 * HD:3 * HD], both(nm[:, :, :])))

                def max_in(n, p):
                    dve.wait_ge(n_placed, n + 1)
                    nc.vector.tensor_copy(nT[:, p, :], ptr[:, 0, 0:SEQ]).then_inc(n_in, 1)

                def first(n, p):
                    cast(n, p)
                    maxima(n, p)
                    max_in(n, p)

                def second(n, p, more):
                    if more:
                        cast(n + 1, 1 - p)
                        maxima(n + 1, 1 - p)
                    dve.wait_ge(mixed, n * HD + HD + 2)
                    nc.vector.reciprocal(inv[:, :, :], py[:, :, :, D]).then_inc(ainv, 1)
                    dve.wait_ge(ainv, 2 * n + 1)
                    for t in range(2):
                        f = inv[:, t, :].rearrange("p (h o) -> p h o", o=1).broadcast_to([P, HD, D])
                        ins = nc.vector.tensor_tensor(yt[:, t, :, :], py[:, t, :, 0:D], f, ALU.mult)
                    ins.then_inc(y_norm, 1)
                    dve.sem_inc(ainv, 1)
                    if more:
                        max_in(n + 1, 1 - p)
                    dve.wait_ge(made, n + 1)
                    back.dve(dve, n, pout[:, SEQ:2 * SEQ].rearrange("p (k c) -> p k c", k=2), y=False)
                    dve.sem_inc(added, 1)

                dve.sem_inc(t_in, 2)
                dve.sem_inc(maxed, 2)
                dve.wait_ge(zeroed, 3)
                steps(dve, first, second, None)


def state_space(nc, env, a, tag):
    NT, NC_, T = env.NT, env.NC, env.NT * P
    DS, TAPS, EPS = 64, 4, 1e-4
    NB, GH = NT // 2, NC_ // 2
    row_scales(nc, env, tag + "sc", None)
    with ExitStack() as outer:
        sb, ps, sem = scope(nc, outer, tag)
        wT = sb("wT", [P, 3, DS])
        outT = sb("outT", [P, P])
        cw, cb = sb("cw", [P, TAPS]), sb("cb", [P, 1])
        bias = sb("bias", [P, 3])
        A, near, rA = sb("A", [P, 1]), sb("near", [P, 1]), sb("rA", [P, 1])
        ob, ones = sb("ob", [1, P]), sb("ones", [1, P])
        ZT, XC = sb("ZT", [P, T]), sb("XC", [P, T])
        with ExitStack() as prep:
            psb, pps, psem = scope(nc, prep, tag + "p")
            wd = psb("wd", [DS, P])
            wbc = psb("wbc", [DS, 2, 2, P])
            wm = psb("wm", [DS, 2, P])
            ow = psb("ow", [P, 2, DS])
            bb = psb("bb", [P, 2, 2])
            t = psb("t", [P, 4])
            pw, pb = a["in_proj_w"], a["in_proj_b"]
            loads = [(wd[:, :], pw[0:DS, :]),
                     (wbc[:, :, :, :], pw[DS:5 * DS, :].rearrange("(z n g) c -> n z g c", z=2, g=2)),
                     (cw[:, :], a["conv_w"].rearrange("c o k -> c (o k)")),
                     (cb[:, :], a["conv_b"].rearrange("(p o) -> p o", o=1)),
                     (ob[:, :], a["out_proj_b"].rearrange("(o d) -> o d", o=1))]
            for half in range(2):
                r_ = slice(half * DS, (half + 1) * DS)
                loads += [(bias[r_, 0:1], pb[0:DS].rearrange("(p o) -> p o", o=1)),
                          (bb[r_, :, :], pb[DS:5 * DS].rearrange("(z n g) -> n z g", z=2, g=2)),
                          (A[r_, :], a["A_log"].rearrange("(p o) -> p o", o=1)),
                          (ow[:, half, :], a["out_proj_w"])]
            load(nc, tag + "ld", loads)
            vec, ex = psem("vec"), psem("ex")
            with nc.Block() as block:
                @block.scalar
                def _(act):
                    nc.scalar.activation(t[:, 0:1], A[:, :], ACT.Exp).then_inc(ex, 1)

                @block.vector
                def _(dve):
                    link = Link(dve, vec)
                    link(nc.vector.memset(ones[:, :], 1.0))
                    for z in range(2):
                        link(nc.vector.tensor_tensor(wm[:, z, :], wbc[:, z, 0, :], wbc[:, z, 1, :], ALU.add))
                        link(nc.vector.tensor_scalar(wm[:, z, :], wm[:, z, :], 0.5, None, ALU.mult))
                        link(nc.vector.tensor_tensor(bias[:, 1 + z:2 + z], bb[:, z, 0:1], bb[:, z, 1:2], ALU.add))
                        link(nc.vector.tensor_scalar(bias[:, 1 + z:2 + z], bias[:, 1 + z:2 + z], 0.5, None, ALU.mult))
                    dve.wait_ge(ex, 1)
                    link(nc.vector.tensor_scalar(near[:, :], t[:, 0:1], EPS, None, ALU.is_lt))
                    link(nc.vector.tensor_scalar(A[:, :], t[:, 0:1], -1.0, None, ALU.mult))
                    link(nc.vector.tensor_tensor(t[:, 1:2], A[:, :], near[:, :], ALU.subtract))
                    link(nc.vector.reciprocal(t[:, 2:3], t[:, 1:2]))
                    link(nc.vector.tensor_scalar(t[:, 3:4], near[:, :], -1.0, 1.0, ALU.mult, ALU.add))
                    link(nc.vector.tensor_tensor(rA[:, :], t[:, 2:3], t[:, 3:4], ALU.mult))
            turn_weights(nc, env, tag + "t", [], [(wd[:, :], wT[:, 0, :])]
                         + [(wm[:, z, :], wT[:, 1 + z, :]) for z in range(2)]
                         + [(ow[:, :, :].rearrange("p a n -> p (a n)"), outT[:, :])])
        front_pass(nc, env, tag + "f", False, ZT[:, :])
        with ExitStack() as ctx:
            sb, ps, sem = scope(nc, ctx, tag + "c")
            vec = sem("vec")
            block = ctx.enter_context(nc.Block())
            L = SEQ - 1

            @block.vector
            def _(dve):
                link = Link(dve, vec)
                z = ZT[:, :].rearrange("p (s t) -> p s t", t=SEQ)
                x = XC[:, :].rearrange("p (s t) -> p s t", t=SEQ)
                link(nc.vector.memset(x[:, :, L:SEQ], 0.0))
                link(nc.vector.tensor_scalar(x[:, :, 0:L], z[:, :, 0:L], cw[:, 1:2], cb[:, 0:1], ALU.mult, ALU.add))
                for k, lo, hi in ((0, 1, L), (2, 0, L), (3, 0, L - 1)):
                    link(nc.vector.scalar_tensor_tensor(x[:, :, lo:hi], z[:, :, lo + k - 1:hi + k - 1], cw[:, k:k + 1],
                                                        x[:, :, lo:hi], ALU.mult, ALU.add))
        with ExitStack() as ctx:
            sb, ps, sem = scope(nc, ctx, tag + "s")
            d, l, e, w, c, ab, q, h_, y = (sb(k, [P, CH]) for k in ("d", "l", "e", "w", "c", "ab", "q", "h", "y"))
            pp, po = ps("pp", [P, 3, 512]), ps("po", [P, 2, 512])
            made, acts, vec, outs, added = sem("made"), sem("acts"), sem("vec"), sem("outs"), sem("added")
            back = Back(nc, env, sb, ps, sem)
            block = ctx.enter_context(nc.Block())
            STEPS = 15

            @block.tensor
            def _(pe):
                for g in range(GH):
                    pe.wait_ge(vec, STEPS * g)
                    for z in range(3):
                        for half in range(2):
                            n = g + half * GH
                            ins = nc.tensor.matmul(pp[half * DS:(half + 1) * DS, z, :], wT[:, z, :],
                                                   XC[:, n * CH:(n + 1) * CH], start=True, stop=True)
                    ins.then_inc(made, 1)
                    pe.wait_ge(vec, STEPS * g + STEPS)
                    pe.wait_ge(added, 2 * g)
                    for half in range(2):
                        r_ = slice(half * DS, (half + 1) * DS)
                        for k in range(TPC):
                            o = po[:, half, k * P:(k + 1) * P]
                            nc.tensor.matmul(o, ones[:, :], ob[:, :], start=True, stop=False)
                            ins = nc.tensor.matmul(o, y[r_, k * P:(k + 1) * P], outT[r_, :], start=False, stop=True)
                        ins.then_inc(outs, 1)

            @block.scalar
            def _(act):
                for g in range(GH):
                    link = Link(act, acts, 5 * g)
                    act.wait_ge(made, g + 1)
                    link(nc.scalar.activation(d[:, :], pp[:, 0, :], ACT.Identity, bias=bias[:, 0:1]))
                    link(nc.scalar.activation(l[:, :], d[:, :], ACT.Abs))
                    link(nc.scalar.activation(e[:, :], l[:, :], ACT.Exp, scale=-1.0))
                    link(nc.scalar.activation(l[:, :], e[:, :], ACT.Ln, bias=1.0))
                    act.wait_ge(vec, STEPS * g + 4)
                    link(nc.scalar.activation(ab[:, :], d[:, :], ACT.Exp, scale=A[:, 0:1]))

            @block.vector
            def _(dve):
                for g in range(GH):
                    link = Link(dve, vec, STEPS * g)
                    dve.wait_ge(acts, 5 * g + 3)
                    link(nc.vector.tensor_scalar(w[:, :], e[:, :], 1.0, -1.0, ALU.add, ALU.add))
                    link(nc.vector.tensor_tensor(c[:, :], e[:, :], w[:, :], ALU.subtract))
                    dve.wait_ge(acts, 5 * g + 4)
                    link(nc.vector.scalar_tensor_tensor(l[:, :], d[:, :], 0.0, l[:, :], ALU.max, ALU.add))
                    link(nc.vector.tensor_tensor(d[:, :], l[:, :], c[:, :], ALU.add))
                    link(nc.vector.tensor_scalar(w[:, :], d[:, :], A[:, 0:1], None, ALU.mult))
                    link(nc.vector.tensor_scalar(q[:, :], w[:, :], 1.0 / 6.0, 0.5, ALU.mult, ALU.add))
                    link(nc.vector.tensor_tensor(c[:, :], q[:, :], w[:, :], ALU.mult))
                    link(nc.vector.tensor_scalar(q[:, :], c[:, :], 1.0, near[:, 0:1], ALU.add, ALU.mult))
                    dve.wait_ge(acts, 5 * g + 5)
                    link(nc.vector.tensor_scalar(w[:, :], ab[:, :], 1.0, rA[:, 0:1], ALU.subtract, ALU.mult))
                    link(nc.vector.tensor_tensor(c[:, :], w[:, :], q[:, :], ALU.add))
                    link(nc.vector.scalar_tensor_tensor(q[:, :], pp[:, 1, :], bias[:, 1:2], c[:, :], ALU.add, ALU.mult))
                    for s in range(SPC):
                        cols = slice(s * SEQ, (s + 1) * SEQ)
                        link(nc.vector.tensor_tensor_scan(h_[:, cols], ab[:, cols], q[:, cols], 0.0, ALU.mult, ALU.add))
                    dve.wait_ge(outs, 2 * g)
                    link(nc.vector.scalar_tensor_tensor(y[:, :], pp[:, 2, :], bias[:, 2:3], h_[:, :], ALU.add, ALU.mult))
                    link(nc.vector.tensor_scalar(w[:, 0:1], w[:, 0:1], 1.0, None, ALU.mult))
                    for half in range(2):
                        dve.wait_ge(outs, 2 * g + half + 1)
                        back.dve(dve, g + half * GH, po[:, half, :].rearrange("p (k c) -> p k c", k=TPC), y=False,
                                 turn=2 * g + half)
                        dve.sem_inc(added, 1)


def store(nc, env, out):
    with ExitStack() as ctx:
        stored = ctx.enter_context(nc.semaphore("stored"))
        block = ctx.enter_context(nc.Block())

        @block.sync
        def _(sp):
            sp.dma_start(out.rearrange("b (s p) c -> p (b s) c", p=P), env.X[:, :, :]).then_inc(stored, 16)
            sp.wait_ge(stored, 16)


STAGES = ("mamba", "experts", "attention", "experts", "rotary", "product_keys", "state_space", "product_keys")


def hybrid(nc, args, out, stages=STAGES):
    Lent.handles = []
    env = Env()
    nb = args["L0_attn_a_x"].shape[0]
    env.NT = nb * SEQ // P
    env.NC = env.NT // TPC
    with ExitStack() as ctx:
        sb, ps, sem = scope(nc, ctx, "g")
        env.X = sb("X", [P, env.NT, P])
        env.stats = sb("stats", [P, env.NT, 6])
        env.mean, env.rstd = sb("mean", [P, env.NT]), sb("rstd", [P, env.NT])
        env.keep, env.shift = sb("keep", [P, env.NT]), sb("shift", [P, env.NT])
        env.root, env.rnorm = sb("root", [P, env.NT]), sb("rnorm", [P, env.NT])
        env.ident = sb("ident", [P, P])
        env.sel = sb("sel", [96, 32, P], BF16)
        env.row = sb("row", [8, 8, P], BF16)
        env.firsts = sb("firsts", [P, TPC, 8])
        env.identb = sb("identb", [P, P], BF16)
        env.causal = sb("causal", [P, P], BF16)
        env.causalT = sb("causalT", [P, P], BF16)
        env.three = sb("three", [P, 16, P], BF16)
        turn_weights(nc, env, "const", [(env.causalT[:, :], args["c_causalT"]), (env.three[:, :, :], args["c_three"]),
                      (env.identb[:, :], args["c_identb"]), (env.causal[:, :], args["c_causal"]),
                      (env.ident[:, :], args["c_ident"]), (env.sel[:, :, :], args["c_sel"]),
                      (env.row[:, :, :], args["c_row"]), (env.firsts[:, :, :], args["c_firsts"])], [])
        first_stats(nc, env, args["L0_attn_a_x"])
        def of(prefix):
            return {k[len(prefix):]: v for k, v in args.items() if k.startswith(prefix)}

        for i, s in enumerate(stages):
            if s == "attention":
                attention(nc, env, of("L0_attn_b_"), f"b{i}")
            if s == "rotary":
                rotary(nc, env, dict(of("L1_attn_a_"), rope=args["c_rope"]), f"r{i}")
            if s == "state_space":
                state_space(nc, env, of("L1_attn_b_"), f"s{i}")
            if s == "product_keys":
                product_keys(nc, env, of("L1_ffn_"), f"k{i}")
            if s == "experts":
                experts(nc, env, of("L0_ffn_"), f"e{i}")
            if s == "mamba":
                mamba(nc, env, of("L0_attn_a_"))
            sweep(nc)
        store(nc, env, out)


def shape_constants():
    bf = mybir.dt.np(BF16)
    sel = np.zeros((96, 32, P), bf)
    for part in range(3):
        for s in range(32):
            sel[32 * part + s, s, :] = 1
    row = np.zeros((8, 8, P), bf)
    for e in range(8):
        row[e, e, :] = 1
    firsts = np.tile(np.arange(8, 0, -1, dtype=np.float32), (P, TPC, 1))
    causal = np.where(np.arange(P)[None, :] > np.arange(P)[:, None], np.float32(-1e30), np.float32(0)).astype(bf)
    three = np.zeros((P, 16, P), bf)
    for half in range(2):
        for part in range(3):
            for h in range(16):
                three[64 * half + 16 * part + h, h, :] = 1
    inv = (np.float32(1.0) / np.power(np.float32(10000.0), np.arange(0, 8, 2, dtype=np.float32) / np.float32(8)))
    freqs = (np.arange(SEQ, dtype=np.float32)[:, None] * inv[None, :].astype(np.float32)).astype(np.float32)
    cos, sin = np.cos(freqs), np.sin(freqs)
    one = np.stack([np.concatenate([cos, cos], 1), np.concatenate([-sin, sin], 1)], 1)
    rope = np.tile(one, (1, 1, 16)).reshape(2, P, 2, P).transpose(1, 0, 2, 3)
    return {"c_three": three, "c_rope": np.ascontiguousarray(rope.astype(np.float32)), "c_causalT": np.ascontiguousarray(causal.T), "c_identb": np.eye(P, dtype=bf), "c_causal": causal, "c_row": row, "c_firsts": firsts, "c_ident": np.eye(P, dtype=np.float32), "c_sel": sel}


def hybrid_layers_kernel(nc, *operands):
    hybrid(nc, dict(zip(_INS + _TABLES, operands[:-1])), operands[-1])


_INS = ['L0_attn_a_x', 'L0_attn_a_norm_g', 'L0_attn_a_norm_b', 'L0_attn_a_in_w', 'L0_attn_a_conv_w',
        'L0_attn_a_conv_b', 'L0_attn_a_xproj_w', 'L0_attn_a_dt_w', 'L0_attn_a_dt_b', 'L0_attn_a_A_log',
        'L0_attn_a_D', 'L0_attn_a_out_w', 'L0_attn_b_gamma', 'L0_attn_b_w_qkv', 'L0_attn_b_w_out',
        'L0_ffn_centroids', 'L0_ffn_gamma', 'L0_ffn_beta', 'L0_ffn_W1', 'L0_ffn_b1', 'L0_ffn_W2',
        'L0_ffn_b2', 'L1_attn_a_W_kqv', 'L1_attn_a_W_proj', 'L1_attn_a_q_norm_w', 'L1_attn_a_k_norm_w',
        'L1_attn_b_conv_w', 'L1_attn_b_conv_b', 'L1_attn_b_in_proj_w', 'L1_attn_b_in_proj_b',
        'L1_attn_b_A_log', 'L1_attn_b_out_proj_w', 'L1_attn_b_out_proj_b', 'L1_ffn_w_q', 'L1_ffn_keys',
        'L1_ffn_expert_down', 'L1_ffn_expert_up', 'L1_ffn_norm_w']
_TABLES = ['c_ident', 'c_identb', 'c_sel', 'c_row', 'c_three', 'c_firsts', 'c_causal', 'c_causalT', 'c_rope']
_OUTS = [((16, 256, 128), 'float32')]


def kernel(**inputs):
    import numpy as _np
    import concourse.bacc as _bacc
    from concourse import mybir as _mybir
    from concourse.bass_utils import run_bass_kernel_spmd as _run

    nc = _bacc.Bacc("TRN2", target_bir_lowering=False, num_devices=1)
    tables = shape_constants()
    arrays, args = {}, []
    for name in _INS + _TABLES:
        a = _np.ascontiguousarray(inputs[name] if name in inputs else tables[name])
        arrays[f"in_{name}_dram"] = a
        args.append(nc.dram_tensor(f"in_{name}_dram", a.shape, _mybir.dt.from_np(a.dtype), kind="ExternalInput").ap())
    for i, (shape, dtype) in enumerate(_OUTS):
        dt = _mybir.dt.from_np(_np.dtype(dtype))
        args.append(nc.dram_tensor(f"out_{i}_dram", shape, dt, kind="ExternalOutput").ap())
    hybrid_layers_kernel(nc, *args)
    r = _run(nc, [arrays], core_ids=[0])
    got = tuple(r.results[0][f"out_{i}_dram"] for i in range(len(_OUTS)))
    return got[0]
```

```python
from contextlib import ExitStack

import numpy as np

import concourse.bass as bass
from concourse import mybir

P = 128
TPC = 4
CH = TPC * P
SEQ = 256
SPC = CH // SEQ

F32 = mybir.dt.float32
BF16 = mybir.dt.bfloat16
I32 = mybir.dt.int32
ALU = mybir.AluOpType
ACT = mybir.ActivationFunctionType
AX = mybir.AxisListType.X


class Env:
    pass


class Lent:
    handles = []


def sweep(nc):
    nc.clear_and_free_semaphores(Lent.handles)
    Lent.handles = []
    nc.all_engine_barrier()


class Link:

    def __init__(self, eng, sem, base=0):
        self.eng, self.sem, self.base, self.n = eng, sem, base, 0

    def __call__(self, ins):
        ins.then_inc(self.sem, 1)
        self.n += 1
        self.eng.wait_ge(self.sem, self.base + self.n)

    def inc(self, ins):
        ins.then_inc(self.sem, 1)
        self.n += 1

    def wait(self, back=0):
        self.eng.wait_ge(self.sem, self.base + self.n - back)


def hold(eng, sem, value):
    if not (isinstance(value, int) and value <= 0):
        eng.wait_ge(sem, value)
        eng.nop(nofuse=True)


def need(eng, sem, value):
    if not (isinstance(value, int) and value <= 0):
        eng.wait_ge(sem, value)


def rounds(eng, count, body):
    body(0, True, count == 1)
    if count > 2:
        with eng.Fori(1, count - 1) as it:
            body(it, False, False)
    if count > 1:
        body(count - 1, False, True)


def scope(nc, ctx, tag):
    def sb(name, shape, dt=F32):
        return ctx.enter_context(nc.sbuf_tensor(f"{tag}_{name}", shape, dt))

    def ps(name, shape, dt=F32):
        return ctx.enter_context(nc.psum_tensor(f"{tag}_{name}", shape, dt))

    def sem(name):
        handle = nc.alloc_semaphore(name=f"{tag}_{name}")
        Lent.handles.append(handle)
        return handle

    return sb, ps, sem


def turn_weights(nc, env, tag, loads, turns, extra=None):
    with ExitStack() as ctx:
        sb, ps, sem = scope(nc, ctx, tag)
        turned = ps("turned", [P, 8, 512])
        loaded, placed, evacuated = sem("loaded"), sem("placed"), sem("evacuated")
        block = ctx.enter_context(nc.Block())

        @block.sync
        def _(sp):
            for dst, src in loads:
                sp.dma_start(dst, src, allow_slow_non_contiguous=True).then_inc(loaded, 16)
            sp.wait_ge(loaded, 16 * len(loads))

        if turns:
            @block.tensor
            def _(pe):
                pe.wait_ge(loaded, 16 * len(loads))
                for j, (src, dst) in enumerate(turns):
                    p, f = src.shape[0], dst.shape[0]
                    if j >= 8:
                        pe.wait_ge(evacuated, j - 7)
                    nc.tensor.transpose(turned[0:f, j % 8, 0:p], src, env.ident[0:p, 0:p]).then_inc(placed, 1)

            @block.vector
            def _(dve):
                for j, (src, dst) in enumerate(turns):
                    p, f = src.shape[0], dst.shape[0]
                    dve.wait_ge(placed, j + 1)
                    nc.vector.tensor_copy(dst, turned[0:f, j % 8, 0:p]).then_inc(evacuated, 1)
                dve.wait_ge(evacuated, len(turns))


def row_scales(nc, env, tag, second):
    NT = env.NT
    with ExitStack() as ctx:
        sb, ps, sem = scope(nc, ctx, tag)
        tmp = sb("tmp", [P, 5, NT])
        rooted, vec = sem("rooted"), sem("vec")
        block = ctx.enter_context(nc.Block())
        st, t0, t1, t2, t3, t4 = env.stats, tmp[:, 0, :], tmp[:, 1, :], tmp[:, 2, :], tmp[:, 3, :], tmp[:, 4, :]

        @block.vector
        def _(dve):
            link = Link(dve, vec)
            link.inc(nc.vector.tensor_tensor(t0, st[:, :, 1], st[:, :, 4], ALU.add))
            link.inc(nc.vector.tensor_tensor(t1, st[:, :, 1], st[:, :, 4], ALU.subtract))
            link.inc(nc.vector.tensor_tensor(t2, st[:, :, 2], st[:, :, 5], ALU.add))
            link.wait()
            link.inc(nc.vector.tensor_scalar(env.mean[:, :], t0, 0.5, None, ALU.mult))
            link(nc.vector.scalar_tensor_tensor(t3, t1, 0.25, t1, ALU.mult, ALU.mult))
            link(nc.vector.scalar_tensor_tensor(t0, t2, 1.0 / P, t3, ALU.mult, ALU.add))
            link(nc.vector.tensor_scalar(t1, t0, 1e-5, None, ALU.add))
            dve.wait_ge(rooted, 1)
            link(nc.vector.reciprocal(env.rstd[:, :], t2))
            link.inc(nc.vector.tensor_scalar(env.keep[:, :], env.rstd[:, :], 1.0, None, ALU.add))
            link(nc.vector.scalar_tensor_tensor(env.shift[:, :], env.mean[:, :], -1.0, env.rstd[:, :],
                                                ALU.mult, ALU.mult))
            if second:
                k, eps, floor, gain = second
                link(nc.vector.tensor_tensor(t1, t0, env.rstd[:, :], ALU.mult))
                link(nc.vector.tensor_tensor(t3, t1, env.rstd[:, :], ALU.mult))
                link(nc.vector.tensor_scalar(t1, t3, float(k), float(eps), ALU.mult, ALU.add))
                dve.wait_ge(rooted, 2)
                link(nc.vector.tensor_scalar(t4, t2, float(floor), None, ALU.max))
                link(nc.vector.reciprocal(t3, t4))
                link.inc(nc.vector.tensor_scalar(env.root[:, :], t4, 1.0 / gain, None, ALU.mult))
                link(nc.vector.scalar_tensor_tensor(env.rnorm[:, :], t3, float(gain), env.rstd[:, :],
                                                    ALU.mult, ALU.mult))

        @block.scalar
        def _(act):
            act.wait_ge(vec, 7)
            nc.scalar.activation(t2, t1, ACT.Sqrt).then_inc(rooted, 1)
            if second:
                act.wait_ge(vec, 13)
                nc.scalar.activation(t2, t1, ACT.Sqrt).then_inc(rooted, 1)
            act.wait_ge(rooted, 2 if second else 1)


def first_stats(nc, env, x_dram):
    with ExitStack() as ctx:
        sb, ps, sem = scope(nc, ctx, "first")
        loaded, done = sem("loaded"), sem("done")
        block = ctx.enter_context(nc.Block())
        rows = x_dram.rearrange("b (s p) c -> p (b s) c", p=P)

        @block.sync
        def _(sp):
            for q in range(2):
                h = env.NT // 2
                sp.dma_start(env.X[:, q * h:(q + 1) * h, :], rows[:, q * h:(q + 1) * h, :]).then_inc(loaded, 16)

        @block.vector
        def _(dve):
            dve.wait_ge(loaded, 32)
            with dve.Fori(0, env.NT) as i:
                nc.vector.bn_stats(env.stats[:, i, :], env.X[:, i, :]).then_inc(done, 1)
            dve.wait_ge(done, env.NT)


class Front:

    def __init__(self, nc, env, sb, ps, sem, inner, out, scale=None, bias=None, banks=1, out_rows=None):
        self.nc, self.env, self.inner, self.out, self.scale, self.bias = nc, env, inner, out, scale, bias
        self.rows = out_rows or sb("rows", [P, 2, TPC, P])
        self.tp = ps("front", [P, banks, 512])
        self.banks = banks
        self.normed, self.turned, self.written = sem("normed"), sem("turned"), sem("written")

    def dve(self, eng, n, p, free=None):
        e, nc = self.env, self.nc
        eng.wait_ge(self.turned, n + 1)
        if free:
            eng.wait_ge(*free)
        r = e.rnorm if self.inner else e.rstd
        for k in range(TPC):
            t = n * TPC + k
            ins = nc.vector.tensor_scalar(self.rows[:, p, k, :], e.X[:, t, :], e.mean[:, bass.ds(t, 1)],
                                          r[:, bass.ds(t, 1)], ALU.subtract, ALU.mult)
        ins.then_inc(self.normed, 1)

    def credit(self, pe):
        pe.sem_inc(self.turned, 2)

    def credit_act(self, act):
        act.sem_inc(self.written, self.banks)

    def pe(self, eng, n, p):
        eng.wait_ge(self.normed, n + 1)
        eng.wait_ge(self.written, n + 1)
        for k in range(TPC):
            ins = self.nc.tensor.transpose(self.tp[:, p % self.banks, k * P:(k + 1) * P],
                                           self.rows[:, p, k, :], self.env.ident[:, :])
        ins.then_inc(self.turned, 1)

    def act(self, eng, n, p):
        eng.wait_ge(self.turned, n + 3)
        dst = self.out(p)
        src = self.tp[:, p % self.banks, :]
        if len(dst.shape) == 3:
            src = src.rearrange("p (s t) -> p s t", s=dst.shape[1])
        kw = {}
        if self.scale is not None:
            kw["scale"] = self.scale
        if self.bias is not None:
            kw["bias"] = self.bias
        if kw:
            ins = self.nc.scalar.activation(dst, src, ACT.Identity, **kw)
        else:
            ins = self.nc.scalar.copy(dst, src)
        ins.then_inc(self.written, 1)

    def wait(self, eng, n):
        eng.wait_ge(self.written, n + 1 + self.banks)


class Back:

    def __init__(self, nc, env, sb, ps, sem, tiles=TPC):
        self.nc, self.env, self.tiles = nc, env, tiles
        self.buf = sb("sum", [P, tiles, P])
        self.chain = sem("back")

    def dve(self, eng, n, out, y=True, gain=None, turn=None):
        e, nc, G = self.env, self.nc, self.tiles
        base = (n if turn is None else turn) * 3
        last = None
        for k in range(G if y else 0):
            t = n * G + k
            last = nc.vector.tensor_scalar(self.buf[:, k, :], e.X[:, t, :], e.keep[:, bass.ds(t, 1)],
                                           e.shift[:, bass.ds(t, 1)], ALU.mult, ALU.add)
        if y:
            last.then_inc(self.chain, 1)
        else:
            eng.sem_inc(self.chain, 1)
        eng.wait_ge(self.chain, base + 1)
        if gain is None:
            dst = e.X[:, bass.ds(n * G, G), :]
            last = nc.vector.tensor_tensor(dst, self.buf[:, :, :] if y else dst, out, ALU.add)
        else:
            for k in range(G):
                t = n * G + k
                dst = e.X[:, t, :]
                last = nc.vector.scalar_tensor_tensor(dst, out[:, k, :], gain[:, bass.ds(t, 1)],
                                                      self.buf[:, k, :] if y else dst, ALU.mult, ALU.add)
        last.then_inc(self.chain, 1)
        eng.wait_ge(self.chain, base + 2)
        for k in range(G):
            t = n * G + k
            last = nc.vector.bn_stats(e.stats[:, t, :], e.X[:, t, :])
        last.then_inc(self.chain, 1)
        eng.wait_ge(self.chain, base + 3)


def mamba(nc, env, a):
    NT, NC_, T = env.NT, env.NC, env.NT * P
    DI, DS, DTR, TAPS = 256, 16, 64, 4
    H = DI // P
    row_scales(nc, env, "m_sc", (1.0, 1e-5, 0.0, 1.0))
    with ExitStack() as outer:
        sb, ps, sem = scope(nc, outer, "m")
        outT = sb("outT", [P, H, P])
        A = sb("A", [P, H, DS])
        convb, dtb, Dd = sb("convb", [P, H]), sb("dtb", [P, H]), sb("Dd", [P, H])
        g, b = sb("g", [P, 1]), sb("b", [P, 1])
        diagD = sb("diagD", [P, H, P])
        u = sb("u", [P, H, T])
        sz = sb("sz", [P, H, T])
        delta = sb("delta", [P, H, T])
        du = sb("du", [P, H, T])
        bc = sb("bc", [96, T], BF16)
        projections = ExitStack()
        sb, _, _ = scope(nc, projections, "mw")
        wconv = sb("wconv", [P, TAPS, DI])
        wz = sb("wz", [P, DI])
        xprojT = sb("xprojT", [P, H, DTR + 2 * DS])
        dtT = sb("dtT", [DTR, DI])
        with ExitStack() as prep:
            psb, pps, psem = scope(nc, prep, "mp")
            in_w = psb("in_w", [P, 4, P])
            scaled = psb("scaled", [P, TAPS, H, P])
            cw = psb("cw", [P, H, TAPS])
            xp = psb("xp", [DTR + 2 * DS, DI])
            dtw = psb("dtw", [P, H, DTR])
            ow = psb("ow", [P, DI])
            ld, mt, ma_ = psem("ld"), psem("mt"), psem("ma")
            with nc.Block() as block:
                @block.sync
                def _(sp):
                    for dst, src in (
                        (in_w[:, :, :], a["in_w"].rearrange("(j p) c -> p j c", p=P)),
                        (cw[:, :, :], a["conv_w"].rearrange("(h p) o k -> p h (o k)", p=P)),
                        (xp[:, :], a["xproj_w"]),
                        (dtw[:, :, :], a["dt_w"].rearrange("(h p) r -> p h r", p=P)),
                        (ow[:, :], a["out_w"]),
                        (A[:, :, :], a["A_log"].rearrange("(h p) s -> p h s", p=P)),
                        (convb[:, :], a["conv_b"].rearrange("(h p) -> p h", p=P)),
                        (dtb[:, :], a["dt_b"].rearrange("(h p) -> p h", p=P)),
                        (Dd[:, :], a["D"].rearrange("(h p) -> p h", p=P)),
                        (g[:, :], a["norm_g"].rearrange("(p o) -> p o", o=1)),
                        (b[:, :], a["norm_b"].rearrange("(p o) -> p o", o=1)),
                    ):
                        sp.dma_start(dst, src, allow_slow_non_contiguous=True).then_inc(ld, 16)

                @block.vector
                def _(dve):
                    dve.wait_ge(ld, 16 * 11)
                    for k in range(TAPS):
                        for h in range(H):
                            nc.vector.tensor_scalar(scaled[:, k, h, :], in_w[:, h, :], cw[:, h, k:k + 1], None,
                                                    ALU.mult).then_inc(mt, 1)
                    for h in range(H):
                        nc.vector.tensor_scalar(diagD[:, h, :], env.ident[:, :], Dd[:, h:h + 1], None,
                                                ALU.mult).then_inc(mt, 1)
                    dve.wait_ge(mt, 10)

                @block.scalar
                def _(act):
                    act.wait_ge(ld, 16 * 11)
                    nc.scalar.activation(A[:, :, :], A[:, :, :], ACT.Exp).then_inc(ma_, 1)
                    act.wait_ge(ma_, 1)
                    nc.scalar.mul(A[:, :, :], A[:, :, :], -1.0).then_inc(ma_, 1)
                    act.wait_ge(ma_, 2)
            turn_weights(nc, env, "m_t", [],
                         [(scaled[:, k, h, :], wconv[:, k, h * P:(h + 1) * P]) for k in range(TAPS) for h in range(H)]
                         + [(in_w[:, 2 + h, :], wz[:, h * P:(h + 1) * P]) for h in range(H)]
                         + [(xp[:, h * P:(h + 1) * P], xprojT[:, h, :]) for h in range(H)]
                         + [(dtw[:, h, :], dtT[:, h * P:(h + 1) * P]) for h in range(H)]
                         + [(ow[:, h * P:(h + 1) * P], outT[:, h, :]) for h in range(H)])

        with ExitStack() as ctx:
            sb, ps, sem = scope(nc, ctx, "ma")
            PAD = TAPS - 1
            zc = sb("zc", [P, 2, SPC, PAD + SEQ])
            dr = sb("dr", [DTR, CH])
            bcf = sb("bcf", [2 * DS, 2, CH])
            pj = ps("pj", [P, 4, 512])
            pd = ps("pd", [P, 3, 512])
            padded, proj, gated, small, draw_, drd, split = (sem(x) for x in (
                "padded", "proj", "gated", "small", "dtraw", "drd", "split"))
            front = Front(nc, env, sb, ps, sem, True, lambda p: zc[:, p, :, PAD:PAD + SEQ],
                          scale=g[:, 0:1], bias=b[:, 0:1])
            block = ctx.enter_context(nc.Block())

            @block.gpsimd
            def _(pool):
                nc.gpsimd.memset(zc[:, :, :, 0:PAD], 0.0).then_inc(padded, 1)

            @block.vector
            def _(dve):
                with dve.Fori(0, NC_ // 2) as it:
                    for p in range(2):
                        n = it * 2 + p
                        front.dve(dve, n, p)
                    for p in range(2):
                        n = it * 2 + p
                        dve.wait_ge(small, 2 * n + 2)
                        link = Link(dve, split, n * 5)
                        cols = bass.ds(n * CH, CH)
                        link(nc.vector.tensor_copy(bc[0:32, cols], bcf[:, 0, :]))
                        link(nc.vector.tensor_tensor(bcf[:, 1, :], bcf[:, 0, :], bc[0:32, cols], ALU.subtract))
                        link(nc.vector.tensor_copy(bc[32:64, cols], bcf[:, 1, :]))
                        link(nc.vector.tensor_tensor(bcf[:, 0, :], bcf[:, 1, :], bc[32:64, cols], ALU.subtract))
                        link(nc.vector.tensor_copy(bc[64:96, cols], bcf[:, 0, :]))

            @block.tensor
            def _(pe):
                front.credit(pe)
                pe.wait_ge(padded, 1)
                with pe.Fori(0, NC_ // 2) as it:
                    for p in range(2):
                        n = it * 2 + p
                        front.pe(pe, n, p)
                        front.wait(pe, n)
                        for h in range(H):
                            pe.wait_ge(gated, 4 * n + 1 + h)
                            for k in range(TAPS):
                                ins = nc.tensor.matmul(pj[:, h, :], wconv[:, k, h * P:(h + 1) * P],
                                                       zc[:, p, :, k:k + SEQ], start=(k == 0), stop=(k == TAPS - 1))
                            ins.then_inc(proj, 1)
                        for h in range(H):
                            pe.wait_ge(gated, 4 * n + 3 + h)
                            nc.tensor.matmul(pj[:, 2 + h, :], wz[:, h * P:(h + 1) * P],
                                             zc[:, p, :, PAD:PAD + SEQ], start=True, stop=True).then_inc(proj, 1)
                        pe.wait_ge(gated, 4 * n + 4 + 2)
                        pe.wait_ge(small, 2 * n)
                        for h in range(H):
                            ins = nc.tensor.matmul(pd[0:96, 0, :], xprojT[:, h, :], u[:, h, bass.ds(n * CH, CH)],
                                                   start=(h == 0), stop=(h == H - 1))
                        ins.then_inc(draw_, 1)
                        pe.wait_ge(small, 2 * n + 1)
                        for h in range(H):
                            pe.wait_ge(drd, 2 * n + h + 1)
                            nc.tensor.matmul(pd[:, 1 + h, :], dtT[:, h * P:(h + 1) * P], dr[:, :],
                                             start=True, stop=True).then_inc(draw_, 1)

            @block.scalar
            def _(act):
                front.credit_act(act)
                act.sem_inc(gated, 4)
                act.sem_inc(drd, 2)
                with act.Fori(0, NC_ // 2) as it:
                    for p in range(2):
                        n = it * 2 + p
                        cols = bass.ds(n * CH, CH)
                        front.act(act, n, p)
                        for h in range(H):
                            hold(act, proj, 4 * n + 1 + h)
                            nc.scalar.activation(u[:, h, cols], pj[:, h, :], ACT.Silu,
                                                 bias=convb[:, h:h + 1]).then_inc(gated, 1)
                        for h in range(H):
                            hold(act, proj, 4 * n + 3 + h)
                            nc.scalar.activation(sz[:, h, cols], pj[:, 2 + h, :], ACT.Silu).then_inc(gated, 1)
                        act.wait_ge(draw_, 3 * n + 1)
                        nc.scalar.copy(dr[:, :], pd[0:DTR, 0, :]).then_inc(small, 1)
                        act.wait_ge(split, 5 * n)
                        nc.scalar.copy(bcf[:, 0, :], pd[DTR:DTR + 2 * DS, 0, :]).then_inc(small, 1)
                        for h in range(H):
                            hold(act, draw_, 3 * n + 2 + h)
                            nc.scalar.activation(delta[:, h, cols], pd[:, 1 + h, :], ACT.Identity,
                                                 bias=dtb[:, h:h + 1]).then_inc(drd, 1)

        projections.close()

        with ExitStack() as ctx:
            sb, ps, sem = scope(nc, ctx, "mb")
            e = sb("e", [P, 2, H, CH])
            l = sb("l", [P, 2, H, CH])
            w = sb("w", [P, 2, H, CH])
            logs, vec, rest, done = sem("logs"), sem("vec"), sem("rest"), sem("done")
            block = ctx.enter_context(nc.Block())

            @block.scalar
            def _(act):
                with act.Fori(0, NC_ // 2) as it:
                    for p in range(2):
                        n = it * 2 + p
                        d = delta[:, :, bass.ds(n * CH, CH)]
                        hold(act, done, n + 1)
                        link = Link(act, logs, 3 * n)
                        link(nc.scalar.activation(l[:, p, :, :], d, ACT.Abs))
                        link(nc.scalar.activation(e[:, p, :, :], l[:, p, :, :], ACT.Exp, scale=-1.0))
                        link(nc.scalar.activation(l[:, p, :, :], e[:, p, :, :], ACT.Ln, bias=1.0))

            @block.gpsimd
            def _(pool):
                with pool.Fori(0, NC_ // 2) as it:
                    for p in range(2):
                        n = it * 2 + p
                        hold(pool, logs, 3 * n + 2)
                        link = Link(pool, rest, 2 * n)
                        link(nc.gpsimd.tensor_scalar(w[:, p, :, :], e[:, p, :, :], 1.0, -1.0, ALU.add, ALU.add))
                        link(nc.gpsimd.tensor_tensor(w[:, p, :, :], e[:, p, :, :], w[:, p, :, :], ALU.subtract))

            @block.vector
            def _(dve):
                dve.sem_inc(done, 2)
                with dve.Fori(0, NC_ // 2) as it:
                    for p in range(2):
                        n = it * 2 + p
                        cols = bass.ds(n * CH, CH)
                        d = delta[:, :, cols]
                        dve.wait_ge(logs, 3 * n + 3)
                        link = Link(dve, vec, 2 * n)
                        link(nc.vector.scalar_tensor_tensor(l[:, p, :, :], d, 0.0, l[:, p, :, :], ALU.max, ALU.add))
                        dve.wait_ge(rest, 2 * n + 2)
                        link(nc.vector.tensor_tensor(d, l[:, p, :, :], w[:, p, :, :], ALU.add))
                        nc.vector.tensor_tensor(du[:, :, cols], d, u[:, :, cols], ALU.mult).then_inc(done, 1)
                dve.wait_ge(done, NC_ + 2)

        with ExitStack() as ctx:
            sb, ps, sem = scope(nc, ctx, "mc")
            RB, RH, LAG = 4, 8, 3
            dA = sb("dA", [P, RB, SPC, SEQ])
            h_ = sb("h", [P, RB, CH])
            cs = sb("cs", [P, 2, CH])
            hc = sb("hc", [P, RH, CH])
            Bp, Cp = ps("B", [P, 2, 512]), ps("C", [P, 2, 512])
            dbu = ps("dbu", [P, 2, 512])
            yp = ps("y", [P, H, 512])
            zeroed, bcast, cdone, decay, inject, scanned, outs, summed, y_out, moved = (sem(x) for x in (
                "zeroed", "bcast", "cdone", "decay", "inject", "scanned", "outs", "summed", "yout", "moved"))
            block = ctx.enter_context(nc.Block())
            Q = DS * H

            @block.tensor
            def _(pe):
                def spread(n, s):
                    g = n * DS + s
                    cols = bass.ds(n * CH, CH)
                    need(pe, inject, H * (g - 1))
                    need(pe, cdone, g - 1)
                    nc.tensor.matmul(Bp[:, s % 2, :], env.sel[:, s, :], bc[:, cols], start=True, stop=True)
                    nc.tensor.matmul(Cp[:, s % 2, :], env.sel[:, DS + s, :], bc[:, cols],
                                     start=True, stop=True).then_inc(bcast, 1)

                def sum_up(n, s):
                    for h in range(H):
                        q = s * H + h
                        need(pe, outs, n * Q + q + 1)
                        if s == 0:
                            need(pe, y_out, H * n)
                        nc.tensor.matmul(yp[:, h, :], env.ident[:, :], hc[:, q % RH, :], start=(s == 0), stop=False,
                                         ).then_inc(summed, 1)
                    if s == DS - 1:
                        for h in range(H):
                            nc.tensor.matmul(yp[:, h, :], diagD[:, h, :], u[:, h, bass.ds(n * CH, CH)], start=False,
                                             stop=True).then_inc(moved, 1)

                def body(n, first, last):
                    for s in range(DS):
                        spread(n, s)
                        if s >= LAG:
                            sum_up(n, s - LAG)
                        elif not first:
                            sum_up(n - 1, s - LAG + DS)

                rounds(pe, NC_, body)
                for s in range(DS - LAG, DS):
                    sum_up(NC_ - 1, s)

            @block.scalar
            def _(act):
                act.wait_ge(zeroed, 1)

                def body(n, first, last):
                    for s in range(DS):
                        for h in range(H):
                            q = s * H + h
                            hold(act, scanned, n * Q + q + 1 - RB)
                            d = delta[:, h, bass.ds(n * CH, CH)].rearrange("p (s t) -> p s t", s=SPC)
                            nc.scalar.activation(dA[:, q % RB, :, 1:SEQ], d[:, :, 1:SEQ], ACT.Exp,
                                                 scale=A[:, h, s:s + 1]).then_inc(decay, 1)
                        need(act, bcast, n * DS + s + 1)
                        need(act, outs, H * (n * DS + s - 1))
                        nc.scalar.copy(cs[:, s % 2, :], Cp[:, s % 2, :]).then_inc(cdone, 1)

                rounds(act, NC_, body)

            @block.vector
            def _(dve):
                def bring(n, q):
                    s, h = q // H, q % H
                    need(dve, bcast, n * DS + s + 1)
                    need(dve, scanned, n * Q + q - 1)
                    nc.vector.tensor_tensor(dbu[:, q % 2, :], du[:, h, bass.ds(n * CH, CH)], Bp[:, s % 2, :],
                                            ALU.mult).then_inc(inject, 1)

                def gate(n):
                    for h in range(H):
                        need(dve, moved, H * n + 1 + h)
                        z = sz[:, h, bass.ds(n * CH, CH)]
                        nc.vector.tensor_tensor(z, z, yp[:, h, :], ALU.mult).then_inc(y_out, 1)

                def body(n, first, last):
                    for q in range(Q):
                        if q + 1 < Q:
                            bring(n, q + 1)
                        elif not last:
                            bring(n + 1, 0)
                        if q == LAG * H and not first:
                            gate(n - 1)
                        need(dve, inject, n * Q + q + 1)
                        need(dve, decay, n * Q + q + 1)
                        need(dve, outs, n * Q + q + 1 - RB)
                        nc.vector.tensor_tensor_scan(h_[:, q % RB, :], dA[:, q % RB, :, :].rearrange("p s t -> p (s t)"),
                                                     dbu[:, q % 2, :], 0.0, ALU.mult, ALU.add).then_inc(scanned, 1)

                bring(0, 0)
                rounds(dve, NC_, body)
                gate(NC_ - 1)

            @block.gpsimd
            def _(pool):
                nc.gpsimd.memset(dA[:, :, :, 0:1], 0.0).then_inc(zeroed, 1)

                def body(n, first, last):
                    for q in range(Q):
                        s = q // H
                        need(pool, scanned, n * Q + q + 1)
                        need(pool, cdone, n * DS + s + 1)
                        need(pool, summed, n * Q + q + 1 - RH)
                        nc.gpsimd.tensor_tensor(hc[:, q % RH, :], h_[:, q % RB, :], cs[:, s % 2, :],
                                                ALU.mult).then_inc(outs, 1)

                rounds(pool, NC_, body)

        channels_out(nc, env, "md", H, lambda h: outT[:, h, :], lambda h, n: sz[:, h, bass.ds(n * CH, CH)])


def channels_out(nc, env, tag, K, weight, act_of, y=True):
    with ExitStack() as ctx:
        sb, ps, sem = scope(nc, ctx, tag)
        po, pt = ps("po", [P, 2, 512]), ps("pt", [P, 2, 512])
        oT = sb("oT", [P, 2, CH])
        made, held, turned, added = sem("made"), sem("held"), sem("turned"), sem("added")
        back = Back(nc, env, sb, ps, sem)
        block = ctx.enter_context(nc.Block())

        @block.tensor
        def _(pe):
            with pe.Fori(0, env.NC // 2) as it:
                for p in range(2):
                    n = it * 2 + p
                    pe.wait_ge(held, n + 1)
                    for k in range(K):
                        ins = nc.tensor.matmul(po[:, p, :], weight(k), act_of(k, n), start=(k == 0), stop=(k == K - 1))
                    ins.then_inc(made, 1)
                    pe.wait_ge(held, n + 3)
                    pe.wait_ge(added, n + 1)
                    for k in range(TPC):
                        ins = nc.tensor.transpose(pt[:, p, k * P:(k + 1) * P], oT[:, p, k * P:(k + 1) * P], env.ident[:, :])
                    ins.then_inc(turned, 1)

        @block.scalar
        def _(act):
            act.sem_inc(held, 2)
            with act.Fori(0, env.NC // 2) as it:
                for p in range(2):
                    n = it * 2 + p
                    act.wait_ge(made, n + 1)
                    act.wait_ge(added, n + 1)
                    nc.scalar.copy(oT[:, p, :], po[:, p, :]).then_inc(held, 1)

        @block.vector
        def _(dve):
            dve.sem_inc(added, 2)
            with dve.Fori(0, env.NC // 2) as it:
                for p in range(2):
                    n = it * 2 + p
                    dve.wait_ge(turned, n + 1)
                    back.dve(dve, n, pt[:, p, :].rearrange("p (k c) -> p k c", k=TPC), y=y)
                    dve.sem_inc(added, 1)


def front_pass(nc, env, tag, inner, ZT, scale=None, bias=None):
    with ExitStack() as ctx:
        sb, ps, sem = scope(nc, ctx, tag)
        rows = sb("rows", [P, 2, TPC, P])
        tp = ps("tp", [P, 2, 512])
        normed, turned, written = sem("normed"), sem("turned"), sem("written")
        block = ctx.enter_context(nc.Block())
        r = env.rnorm if inner else env.rstd

        @block.vector
        def _(dve):
            with dve.Fori(0, env.NC // 2) as it:
                for p in range(2):
                    n = it * 2 + p
                    dve.wait_ge(turned, n + 1)
                    for k in range(TPC):
                        t = n * TPC + k
                        ins = nc.vector.tensor_scalar(rows[:, p, k, :], env.X[:, t, :], env.mean[:, bass.ds(t, 1)],
                                                      r[:, bass.ds(t, 1)], ALU.subtract, ALU.mult)
                    ins.then_inc(normed, 1)

        @block.tensor
        def _(pe):
            pe.sem_inc(turned, 2)
            with pe.Fori(0, env.NC // 2) as it:
                for p in range(2):
                    n = it * 2 + p
                    pe.wait_ge(written, n + 1)
                    pe.wait_ge(normed, n + 1)
                    for k in range(TPC):
                        ins = nc.tensor.transpose(tp[:, p, k * P:(k + 1) * P], rows[:, p, k, :], env.ident[:, :])
                    ins.then_inc(turned, 1)

        @block.scalar
        def _(act):
            act.sem_inc(written, 2)
            with act.Fori(0, env.NC // 2) as it:
                for p in range(2):
                    n = it * 2 + p
                    hold(act, turned, n + 3)
                    dst = ZT[:, bass.ds(n * CH, CH)]
                    kw = {k: v for k, v in (("scale", scale), ("bias", bias)) if v is not None}
                    if kw:
                        nc.scalar.activation(dst, tp[:, p, :], ACT.Identity, **kw).then_inc(written, 1)
                    else:
                        nc.scalar.copy(dst, tp[:, p, :]).then_inc(written, 1)


def load(nc, tag, pairs):
    with ExitStack() as ctx:
        loaded = ctx.enter_context(nc.semaphore(f"{tag}_loaded"))
        block = ctx.enter_context(nc.Block())

        @block.sync
        def _(sp):
            for dst, src in pairs:
                sp.dma_start(dst, src, allow_slow_non_contiguous=True).then_inc(loaded, 16)
            sp.wait_ge(loaded, 16 * len(pairs))


def experts(nc, env, a, tag):
    NT, NC_, T = env.NT, env.NC, env.NT * P
    E, F = 8, 512
    J = F // P
    NJ = (NT + E - 1 + 1) // 2 * 2
    row_scales(nc, env, tag + "sc", (1.0, 1e-5, 0.0, 1.0))
    with ExitStack() as outer:
        sb, ps, sem = scope(nc, outer, tag)
        w1T = sb("w1T", [P, E, F])
        w2T = sb("w2T", [P, E, F])
        b1 = sb("b1", [P, E, J])
        b2 = sb("b2", [1, E, P])
        centT = sb("centT", [P, E])
        gT, bT = sb("gT", [P, E]), sb("bT", [P, E])
        alpha = sb("alpha", [P, NT])
        ones = sb("ones", [1, P])
        slot = sb("slot", [P, NT], I32)
        expert = sb("expert", [P, NJ], I32)
        ZS = sb("ZS", [P, NJ, P])
        YS = sb("YS", [P, NJ, P])
        with ExitStack() as prep:
            psb, pps, psem = scope(nc, prep, tag + "p")
            w1 = psb("w1", [P, E, J, P])
            w2 = psb("w2", [P, E, F])
            load(nc, tag + "ld", [
                (w1[:, :, :, :], a["W1"].rearrange("e (j p) c -> p e j c", p=P)),
                (w2[:, :, :], a["W2"].rearrange("e d f -> d e f")),
                (b1[:, :, :], a["b1"].rearrange("e (j p) -> p e j", p=P)),
                (b2[:, :, :], a["b2"].rearrange("(o e) c -> o e c", o=1)),
                (centT[:, :], a["centroids"].rearrange("e c -> c e")),
                (gT[:, :], a["gamma"].rearrange("e c -> c e")),
                (bT[:, :], a["beta"].rearrange("e c -> c e"))])
            turn_weights(nc, env, tag + "t", [],
                         [(w1[:, e, j, :], w1T[:, e, j * P:(j + 1) * P]) for e in range(E) for j in range(J)]
                         + [(w2[:, e, j * P:(j + 1) * P], w2T[:, e, j * P:(j + 1) * P]) for e in range(E) for j in range(J)])
            pb = pps("pb", [P, E, J, E])
            shifted, folded = psem("shifted"), psem("folded")
            with nc.Block() as block:
                @block.tensor
                def _(pe):
                    for e in range(E):
                        for j in range(J):
                            ins = nc.tensor.matmul(pb[:, e, j, :], w1T[:, e, j * P:(j + 1) * P], bT[:, :],
                                                   start=True, stop=True)
                    ins.then_inc(shifted, 1)

                @block.vector
                def _(dve):
                    dve.wait_ge(shifted, 1)
                    for e in range(E):
                        nc.vector.tensor_tensor(b1[:, e, :], b1[:, e, :], pb[:, e, :, e], ALU.add).then_inc(folded, 1)
                        nc.vector.tensor_scalar(w1T[:, e, :], w1T[:, e, :], gT[:, e:e + 1], None,
                                                ALU.mult).then_inc(folded, 1)
                    dve.wait_ge(folded, 2 * E)
        with ExitStack() as route:
            rsb, rps, rsem = scope(nc, route, tag + "q")
            ZT = rsb("ZT", [P, T])
            hot = rsb("hot", [P, NT, E], BF16)
            choose(nc, env, tag, ZT, centT, hot, alpha)
            place(nc, env, tag, hot, slot, expert, ZS, ones, NJ)
        sorted_experts(nc, env, tag, ZS, YS, w1T, w2T, b1, b2, ones, expert, NJ)
        collect(nc, env, tag, YS, slot, alpha, NJ)


def choose(nc, env, tag, ZT, centT, hot, alpha):
    NT, NC_ = env.NT, env.NC
    E = 8
    front_pass(nc, env, tag + "f", True, ZT[:, :])
    with ExitStack() as ctx:
        sb, ps, sem = scope(nc, ctx, tag + "r")
        zc = sb("zc", [P, 2, CH])
        sc, rank = sb("sc", [P, TPC, E]), sb("rank", [P, TPC, E])
        mx, m2, arg = sb("mx", [P, TPC]), sb("m2", [P, TPC]), sb("arg", [P, 2, TPC])
        psc = ps("psc", [P, 512])
        copied, scored, vec, done = sem("copied"), sem("scored"), sem("vec"), sem("done")
        block = ctx.enter_context(nc.Block())
        STEPS = 7

        @block.gpsimd
        def _(pool):
            with pool.Fori(0, NC_ // 2) as it:
                for p in range(2):
                    n = it * 2 + p
                    hold(pool, scored, n + 1)
                    nc.gpsimd.tensor_copy(zc[:, p, :], ZT[:, bass.ds(n * CH, CH)]).then_inc(copied, 1)

        @block.tensor
        def _(pe):
            pe.sem_inc(scored, 2)
            with pe.Fori(0, NC_ // 2) as it:
                for p in range(2):
                    n = it * 2 + p
                    pe.wait_ge(copied, n + 1)
                    pe.wait_ge(vec, STEPS * n)
                    for k in range(TPC):
                        ins = nc.tensor.matmul(psc[:, k * E:(k + 1) * E], zc[:, p, k * P:(k + 1) * P],
                                               centT[:, :], start=True, stop=True)
                    ins.then_inc(scored, 1)

        @block.vector
        def _(dve):
            with dve.Fori(0, NC_ // 2) as it:
                for p in range(2):
                    n = it * 2 + p
                    link = Link(dve, vec, STEPS * n)
                    dve.wait_ge(scored, n + 3)
                    link(nc.vector.tensor_copy(sc[:, :, :], psc[:, 0:TPC * E].rearrange("p (k e) -> p k e", e=E)))
                    link(nc.vector.tensor_reduce(mx[:, :], sc[:, :, :], AX, ALU.max))
                    bm = mx[:, :].rearrange("p (k o) -> p k o", o=1).broadcast_to([P, TPC, E])
                    link(nc.vector.tensor_tensor(rank[:, :, :], sc[:, :, :], bm, ALU.is_equal))
                    link(nc.vector.tensor_tensor(sc[:, :, :], rank[:, :, :], env.firsts[:, 0:TPC, :], ALU.mult))
                    link(nc.vector.tensor_reduce(m2[:, :], sc[:, :, :], AX, ALU.max))
                    b2_ = m2[:, :].rearrange("p (k o) -> p k o", o=1).broadcast_to([P, TPC, E])
                    link.inc(nc.vector.tensor_tensor(hot[:, bass.ds(n * TPC, TPC), :], sc[:, :, :], b2_, ALU.is_equal))
                    dve.wait_ge(done, n)
                    link(nc.vector.tensor_tensor(arg[:, p, :], mx[:, :], env.root[:, bass.ds(n * TPC, TPC)], ALU.mult))

        @block.scalar
        def _(act):
            with act.Fori(0, NC_ // 2) as it:
                for p in range(2):
                    n = it * 2 + p
                    hold(act, vec, STEPS * n + 7)
                    nc.scalar.activation(alpha[:, bass.ds(n * TPC, TPC)], arg[:, p, :], ACT.Sigmoid).then_inc(done, 1)


def place(nc, env, tag, hot, slot, expert, ZS, ones, NJ):
    NT = env.NT
    E = 8
    with ExitStack() as ctx:
        sb, ps, sem = scope(nc, ctx, tag + "l")
        rows = sb("rows", [P, NT, P])
        per, incl, at = sb("per", [P, E, NT]), sb("incl", [P, E, NT]), sb("at", [P, E, NT])
        keep = sb("keep", [P, E, NT])
        above = sb("above", [P, E, NT])
        tiles, ends, one8, first = sb("tiles", [P, E]), sb("ends", [P, E]), sb("one8", [P, E]), sb("first", [P, E])
        below = sb("below", [P, NJ, E - 1])
        slotf, expertf = sb("slotf", [P, NT]), sb("expertf", [P, NJ])
        counts = ps("counts", [P, 2, 512])
        counted, set_, vec, formed, scattered, loaded, zeroed, cleared = (sem(x) for x in (
            "counted", "set", "vec", "formed", "scattered", "loaded", "zeroed", "cleared"))
        block = ctx.enter_context(nc.Block())
        CLEAR = not env.sorted_rows_written
        env.sorted_rows_written = True
        GROUPS = 4

        @block.tensor
        def _(pe):
            h = hot[:, :, :].rearrange("p t e -> p (t e)")
            for k in range(2):
                ins = nc.tensor.matmul(counts[:, k, 0:NT * E], env.ranks[:, k, :], h, start=True, stop=True)
            ins.then_inc(counted, 1)

        @block.gpsimd
        def _(pool):
            nc.gpsimd.memset(keep[:, :, :], 1.0)
            nc.gpsimd.memset(one8[:, :], 1.0)
            nc.gpsimd.memset(ones[:, :], 1.0)
            nc.gpsimd.memset(ZS[:, :, :], 0.0).then_inc(set_, 1)
            pool.wait_ge(set_, 1)
            nc.gpsimd.memset(keep[:, :, 0:1], 0.0).then_inc(set_, 1)
            pool.wait_ge(vec, 12)
            if CLEAR:
                pool.wait_ge(cleared, 16)
            for t in range(NT):
                pool.wait_ge(formed, t + 1)
                nc.gpsimd.indirect_dma_start(env.sorted_rows[:, :], bass.IndirectOffsetOnAxis(slot[:, t:t + 1], 0),
                                             rows[:, t, :], None).then_inc(scattered, 16)

        @block.vector
        def _(dve):
            link = Link(dve, vec)
            def ei(x):
                return x.rearrange("p (t e) -> p e t", e=E)

            def over(x, n):
                return x.rearrange("p (e o) -> p e o", o=1).broadcast_to([P, E, n])

            dve.wait_ge(counted, 1)
            dve.wait_ge(set_, 2)
            link(nc.vector.tensor_copy(per[:, :, :], ei(counts[:, 1, 0:NT * E])))
            link(nc.vector.tensor_tensor_scan(incl[:, :, :].rearrange("p e t -> p (e t)"),
                                              keep[:, :, :].rearrange("p e t -> p (e t)"),
                                              per[:, :, :].rearrange("p e t -> p (e t)"), 0.0, ALU.mult, ALU.add))
            link.inc(nc.vector.tensor_tensor(at[:, :, :], incl[:, :, :], per[:, :, :], ALU.subtract))
            link(nc.vector.tensor_tensor(above[:, :, :], incl[:, :, NT - 1:NT].broadcast_to([P, E, NT]),
                                         env.steps[:, 0:1, 0:NT].broadcast_to([P, E, NT]), ALU.is_gt))
            link(nc.vector.tensor_reduce(tiles[:, :], above[:, :, :], AX, ALU.add))
            link(nc.vector.tensor_tensor_scan(ends[:, :], one8[:, :], tiles[:, :], 0.0, ALU.mult, ALU.add))
            link(nc.vector.tensor_tensor(first[:, :], ends[:, :], tiles[:, :], ALU.subtract))
            link(nc.vector.scalar_tensor_tensor(at[:, :, :], over(first[:, :], NT), float(P), at[:, :, :],
                                                ALU.mult, ALU.add))
            link(nc.vector.tensor_tensor(at[:, :, :], at[:, :, :], ei(counts[:, 0, 0:NT * E]), ALU.add))
            link(nc.vector.tensor_tensor(at[:, :, :], at[:, :, :], hot[:, :, :].rearrange("p t e -> p e t"), ALU.mult))
            link(nc.vector.tensor_reduce(slotf[:, :], at[:, :, :].rearrange("p e t -> p t e"), AX, ALU.add))
            link(nc.vector.tensor_copy(slot[:, :], slotf[:, :]))
            with dve.Fori(0, NT) as t:
                nc.vector.tensor_scalar(rows[:, t, :], env.X[:, t, :], env.mean[:, bass.ds(t, 1)],
                                        env.rnorm[:, bass.ds(t, 1)], ALU.subtract, ALU.mult).then_inc(formed, 1)
            e_ = ends[:, 0:E - 1].rearrange("p (o e) -> p o e", o=1).broadcast_to([P, NJ, E - 1])
            j_ = env.steps[:, 1, 0:NJ].rearrange("p (j o) -> p j o", o=1).broadcast_to([P, NJ, E - 1])
            link(nc.vector.tensor_tensor(below[:, :, :], e_, j_, ALU.is_le))
            link(nc.vector.tensor_reduce(expertf[:, :], below[:, :, :], AX, ALU.add))
            link(nc.vector.tensor_copy(expert[:, :], expertf[:, :]))
            dve.wait_ge(formed, NT)

        @block.sync
        def _(sp):
            view = env.sorted_rows.rearrange("(j p) c -> p j c", p=P)
            sp.wait_ge(set_, 1)
            if CLEAR:
                sp.dma_start(view, ZS[:, :, :]).then_inc(cleared, 16)
                sp.wait_ge(cleared, 16)
            sp.wait_ge(scattered, 16 * NT)
            for g in range(GROUPS):
                js = slice(NJ * g // GROUPS, NJ * (g + 1) // GROUPS)
                sp.dma_start(ZS[:, js, :], view[:, js, :]).then_inc(loaded, 16)
            sp.wait_ge(loaded, 16 * GROUPS)


def sorted_experts(nc, env, tag, ZS, YS, w1T, w2T, b1, b2, ones, expert, NJ):
    E, F = 8, 512
    J = F // P
    with ExitStack() as ctx:
        sb, ps, sem = scope(nc, ctx, tag + "e")
        zs, zT = sb("zs", [P, 2, P]), sb("zT", [P, 2, P])
        w1s, w2s = sb("w1s", [P, 2, F]), sb("w2s", [P, 2, F])
        b1s, b2s = sb("b1s", [P, 2, J]), sb("b2s", [1, 2, P])
        hid = sb("hid", [P, 2, J, P])
        pz, ph, po = ps("pz", [P, 2, 512]), ps("ph", [P, 2, 2, 512]), ps("po", [P, 2, 512])
        zcopied, turned, z_in, staged1, staged2, made, relu_a, relu_d, summed, kept, stored = (sem(x) for x in (
            "zcopied", "turned", "zin", "staged1", "staged2", "made", "relua", "relud", "summed", "kept", "stored"))
        block = ctx.enter_context(nc.Block())

        @block.tensor
        def _(pe):
            def turn(j, p):
                need(pe, zcopied, j + 1)
                need(pe, z_in, j - 1)
                nc.tensor.transpose(pz[:, p, 0:P], zs[:, p, :], env.ident[:, :]).then_inc(turned, 1)

            def first(j, p):
                need(pe, staged1, j + 1)
                need(pe, z_in, j + 1)
                need(pe, relu_a, j - 1)
                need(pe, relu_d, j - 1)
                for k in range(J):
                    ins = nc.tensor.matmul(ph[:, p, k // 2, (k % 2) * P:(k % 2 + 1) * P], w1s[:, p, k * P:(k + 1) * P],
                                           zT[:, p, :], start=True, stop=True)
                    if k % 2:
                        ins.then_inc(made, 1)

            def second(j, p):
                need(pe, relu_a, j + 1)
                need(pe, relu_d, j + 1)
                need(pe, staged2, j + 1)
                need(pe, kept, j - 1)
                for k in range(J):
                    nc.tensor.matmul(po[:, p, 0:P], hid[:, p, k, :], w2s[:, p, k * P:(k + 1) * P],
                                     start=(k == 0), stop=False)
                nc.tensor.matmul(po[:, p, 0:P], ones[:, :], b2s[:, p, :], start=False, stop=True).then_inc(summed, 1)

            def body(it, begin, last):
                for p in range(2):
                    j = it * 2 + p
                    if not (last and p):
                        turn(j + 1, 1 - p)
                    first(j, p)
                    if not (begin and p == 0):
                        second(j - 1, 1 - p)

            turn(0, 0)
            rounds(pe, NJ // 2, body)
            second(NJ - 1, 1)

        def relu(eng, j, p, half):
            for k in (2 * half, 2 * half + 1):
                src = ph[:, p, half, (k % 2) * P:(k % 2 + 1) * P]
                if half:
                    ins = nc.vector.tensor_scalar(hid[:, p, k, :], src, b1s[:, p, k:k + 1], 0.0, ALU.add, ALU.max)
                else:
                    ins = nc.scalar.activation(hid[:, p, k, :], src, ACT.Relu, bias=b1s[:, p, k:k + 1])
            return ins

        @block.scalar
        def _(act):
            def bring(j, p):
                hold(act, turned, j - 1)
                nc.scalar.copy(zs[:, p, :], ZS[:, j, :]).then_inc(zcopied, 1)

            def stage(j, p):
                e = act.value_load(expert[0:1, bass.ds(j, 1)], min_val=0, max_val=E - 1)
                hold(act, summed, j - 1)
                nc.scalar.copy(b2s[:, p, :], b2[:, e, :])
                nc.scalar.copy(w2s[:, p, :], w2T[:, e, :]).then_inc(staged2, 1)

            def enter(j, p):
                need(act, turned, j + 1)
                need(act, made, 2 * (j - 1))
                nc.scalar.copy(zT[:, p, :], pz[:, p, 0:P]).then_inc(z_in, 1)

            def body(it, begin, last):
                for p in range(2):
                    j = it * 2 + p
                    if not last:
                        bring(j + 2, p)
                    if not (last and p):
                        enter(j + 1, 1 - p)
                    need(act, made, 2 * j + 1)
                    need(act, summed, j - 1)
                    relu(act, j, p, 0).then_inc(relu_a, 1)
                    stage(j, p)

            bring(0, 0)
            bring(1, 1)
            enter(0, 0)
            rounds(act, NJ // 2, body)

        @block.vector
        def _(dve):
            def stage(j, p):
                e = dve.value_load(expert[0:1, bass.ds(j, 1)], min_val=0, max_val=E - 1)
                need(dve, relu_a, j - 1)
                need(dve, relu_d, j - 1)
                hold(dve, made, 2 * (j - 1))
                nc.vector.tensor_copy(b1s[:, p, :], b1[:, e, :])
                nc.vector.tensor_copy(w1s[:, p, :], w1T[:, e, :]).then_inc(staged1, 1)

            def keep(j, p):
                hold(dve, summed, j + 1)
                nc.vector.tensor_copy(YS[:, j, :], po[:, p, 0:P]).then_inc(kept, 1)

            def body(it, begin, last):
                for p in range(2):
                    j = it * 2 + p
                    if not (last and p):
                        stage(j + 1, 1 - p)
                    need(dve, made, 2 * j + 2)
                    need(dve, summed, j - 1)
                    need(dve, staged1, j + 1)
                    relu(dve, j, p, 1).then_inc(relu_d, 1)
                    if not (begin and p == 0):
                        keep(j - 1, 1 - p)

            stage(0, 0)
            rounds(dve, NJ // 2, body)
            keep(NJ - 1, 1)

        @block.sync
        def _(sp):
            view = env.sorted_out.rearrange("(j p) c -> p j c", p=P)
            GROUPS = 4
            for g in range(GROUPS):
                js = slice(NJ * g // GROUPS, NJ * (g + 1) // GROUPS)
                sp.wait_ge(kept, js.stop)
                sp.dma_start(view[:, js, :], YS[:, js, :]).then_inc(stored, 16)
            sp.wait_ge(stored, 16 * GROUPS)


def collect(nc, env, tag, YS, slot, alpha, NJ):
    NT, NC_ = env.NT, env.NC
    with ExitStack() as ctx:
        sb, ps, sem = scope(nc, ctx, tag + "c")
        own = YS
        gathered = [sem(f"gathered{n}") for n in range(NC_)]
        back = Back(nc, env, sb, ps, sem)
        block = ctx.enter_context(nc.Block())

        @block.gpsimd
        def _(pool):
            for t in range(NT):
                nc.gpsimd.indirect_dma_start(own[:, t, :], None, env.sorted_out[:, :],
                                             bass.IndirectOffsetOnAxis(slot[:, t:t + 1], 0)
                                             ).then_inc(gathered[t // TPC], 16)

        @block.vector
        def _(dve):
            for n in range(NC_):
                dve.wait_ge(gathered[n], 16 * TPC)
                back.dve(dve, n, own[:, n * TPC:(n + 1) * TPC, :], gain=alpha)


def products(nc, env, tag, items):
    with ExitStack() as ctx:
        sb, ps, sem = scope(nc, ctx, tag)
        out = ps("out", [P, 4, 512])
        made, kept = sem("made"), sem("kept")
        block = ctx.enter_context(nc.Block())

        @block.tensor
        def _(pe):
            for j, (w, x, dst, scale) in enumerate(items):
                if j >= 4:
                    pe.wait_ge(kept, j - 3)
                f = dst.shape[1]
                nc.tensor.matmul(out[:, j % 4, 0:f], w, x, start=True, stop=True).then_inc(made, 1)

        @block.vector
        def _(dve):
            for j, (w, x, dst, scale) in enumerate(items):
                dve.wait_ge(made, j + 1)
                nc.vector.tensor_scalar(dst, out[:, j % 4, 0:dst.shape[1]], scale, None, ALU.mult).then_inc(kept, 1)
            dve.wait_ge(kept, len(items))


def attention(nc, env, a, tag):
    NT, NC_, T = env.NT, env.NC, env.NT * P
    HD, D = 8, 128
    row_scales(nc, env, tag + "sc", (float(D), 0.0, 1e-12, float(D) ** 0.5))
    with ExitStack() as outer:
        sb, ps, sem = scope(nc, outer, tag)
        M, N = sb("M", [P, HD, P]), sb("N", [P, HD, P])
        g = sb("g", [P, 1])
        ZT = sb("ZT", [P, T])
        with ExitStack() as prep:
            psb, pps, psem = scope(nc, prep, tag + "p")
            w = psb("w", [P, 3, HD, P])
            wo, woT = psb("wo", [P, HD * D]), psb("woT", [P, HD, P])
            load(nc, tag + "ld", [(w[:, :, :, :], a["w_qkv"].rearrange("(j h p) c -> p j h c", p=P, h=HD)),
                                  (wo[:, :], a["w_out"]),
                                  (g[:, :], a["gamma"].rearrange("(p o) -> p o", o=1))])
            turn_weights(nc, env, tag + "t", [], [(wo[:, h * P:(h + 1) * P], woT[:, h, :]) for h in range(HD)])
            products(nc, env, tag + "w",
                     [(w[:, 0, h, :], w[:, 1, h, :], M[:, h, :], float(D) ** -0.5) for h in range(HD)]
                     + [(w[:, 2, h, :], woT[:, h, :], N[:, h, :], g[:, 0:1]) for h in range(HD)])
        front_pass(nc, env, tag + "f", True, ZT[:, :], scale=g[:, 0:1])
        with ExitStack() as ctx:
            sb, ps, sem = scope(nc, ctx, tag + "a")
            vz = sb("vz", [P, 2, 2, P])
            qT = sb("qT", [P, 2, SEQ])
            pr = sb("pr", [P, 2, 3, P])
            pT = sb("pT", [P, 2, 3, P])
            nm, den, inv = sb("nm", [P, 2, 2]), sb("den", [P, 2, 2]), sb("inv", [P, 2, 2])
            yT = sb("yT", [P, 2, HD, SEQ])
            pq, psc, pp = ps("pq", [P, 2, 512]), ps("psc", [P, 2, 512]), ps("pp", [P, 2, 512])
            py, pout = ps("py", [P, 512]), ps("pout", [P, 512])
            valued, asked, q_in, scored, maxed, expd, scaled, turned, t_in, mixed, y_in, made, added = (
                sem(x) for x in ("valued", "asked", "qin", "scored", "maxed", "expd", "scaled", "turned", "tin",
                                 "mixed", "yin", "made", "added"))
            inner_ = sem("inner")
            back = Back(nc, env, sb, ps, sem, tiles=2)
            block = ctx.enter_context(nc.Block())
            NB = NT // 2
            U = 2 * HD

            @block.tensor
            def _(pe):
                def ask(it, u):
                    b, h = u // HD, u % HD
                    m = it * U + u
                    pe.wait_ge(q_in, m + 1)
                    nc.tensor.matmul(pq[:, u % 2, 0:SEQ], M[:, h, :], ZT[:, bass.ds((it * 2 + b) * SEQ, SEQ)],
                                     start=True, stop=True).then_inc(asked, 1)

                def score(it, u):
                    b = u // HD
                    m = it * U + u
                    pe.wait_ge(q_in, m + 3)
                    pe.wait_ge(expd, m + 1)
                    base = (it * 2 + b) * SEQ
                    S = psc[:, u % 2, :]
                    nc.tensor.matmul(S[:, 0:P], env.identb[:, :], env.causal[:, :], start=True, stop=False)
                    nc.tensor.matmul(S[:, 0:P], qT[:, u % 2, 0:P], ZT[:, bass.ds(base, P)], start=False, stop=True)
                    nc.tensor.matmul(S[:, 2 * P:3 * P], env.identb[:, :], env.causal[:, :], start=True, stop=True)
                    nc.tensor.matmul(S[:, P:3 * P], qT[:, u % 2, P:2 * P], ZT[:, bass.ds(base, SEQ)], start=False,
                                     stop=True, skip_group_check=True).then_inc(scored, 1)

                def turn(it, u):
                    m = it * U + u
                    pe.wait_ge(scaled, m + 1)
                    pe.wait_ge(t_in, m + 1)
                    for k in range(3):
                        ins = nc.tensor.transpose(pp[:, u % 2, k * P:(k + 1) * P], pr[:, u % 2, k, :], env.ident[:, :])
                    ins.then_inc(turned, 1)

                def mix(it, u):
                    b = u // HD
                    m = it * U + u
                    if u % HD == 0:
                        pe.wait_ge(valued, it * 2 + b + 1)
                    pe.wait_ge(t_in, m + 3)
                    pe.wait_ge(y_in, m)
                    nc.tensor.matmul(py[:, P:SEQ], vz[:, b, 1, :], pT[:, u % 2, 2, :], start=True, stop=True)
                    nc.tensor.matmul(py[:, 0:SEQ], vz[:, b, 0, :], pT[:, u % 2, 0:2, :], start=False,
                                     stop=True, skip_group_check=True).then_inc(mixed, 1)

                def project(it, b):
                    pe.wait_ge(y_in, it * U + (b + 1) * HD)
                    pe.wait_ge(added, it * 2 + b)
                    for k in range(2):
                        for h in range(HD):
                            ins = nc.tensor.matmul(pout[:, k * P:(k + 1) * P], yT[:, b, h, k * P:(k + 1) * P],
                                                   N[:, h, :], start=(h == 0), stop=(h == HD - 1))
                    ins.then_inc(made, 1)

                pe.sem_inc(turned, 2)
                with pe.Fori(0, NB // 2) as it:
                    ask(it, 0)
                    for u in range(U + 2):
                        if u + 1 < U:
                            ask(it, u + 1)
                        if u < U:
                            score(it, u)
                        if u >= 1 and u - 1 < U:
                            turn(it, u - 1)
                        if u >= 2:
                            mix(it, u - 2)
                        if u == HD + 3:
                            project(it, 0)
                    project(it, 1)

            @block.scalar
            def _(act):
                act.sem_inc(q_in, 2)
                act.sem_inc(expd, 2)
                with act.Fori(0, NB // 2) as it:
                    def q_copy(u):
                        m = it * U + u
                        act.wait_ge(asked, m + 1)
                        act.wait_ge(expd, m + 1)
                        nc.scalar.copy(qT[:, u % 2, :], pq[:, u % 2, 0:SEQ]).then_inc(q_in, 1)

                    def y_copy(u):
                        act.wait_ge(mixed, it * U + u + 1)
                        nc.scalar.copy(yT[:, u // HD, u % HD, :], py[:, 0:SEQ]).then_inc(y_in, 1)

                    q_copy(0)
                    for u in range(U + 2):
                        if u + 1 < U:
                            q_copy(u + 1)
                        if u < U:
                            m = it * U + u
                            act.wait_ge(maxed, m + 1)
                            act.wait_ge(turned, m - 1 + 2)
                            S = psc[:, u % 2, :]
                            nc.scalar.activation(pr[:, u % 2, 0, :], S[:, 0:P], ACT.Exp, bias=nm[:, u % 2, 0:1],
                                                 accum_out=den[:, u % 2, 0:1])
                            nc.scalar.activation(pr[:, u % 2, 1:3, :], S[:, P:3 * P].rearrange("p (k c) -> p k c", k=2),
                                                 ACT.Exp, bias=nm[:, u % 2, 1:2],
                                                 accum_out=den[:, u % 2, 1:2]).then_inc(expd, 1)
                        if u >= 2:
                            if u - 2 == 0:
                                act.wait_ge(made, 2 * it)
                            y_copy(u - 2)

            @block.vector
            def _(dve):
                def rows(it, b):
                    for k in range(2):
                        t = (it * 2 + b) * 2 + k
                        ins = nc.vector.tensor_scalar(vz[:, b, k, :], env.X[:, t, :], env.mean[:, bass.ds(t, 1)],
                                                      env.rnorm[:, bass.ds(t, 1)], ALU.subtract, ALU.mult)
                    ins.then_inc(valued, 1)

                dve.sem_inc(t_in, 2)
                with dve.Fori(0, NB // 2) as it:
                    dve.wait_ge(mixed, it * U)
                    rows(it, 0)
                    rows(it, 1)
                    for u in range(U + 1):
                        if u < U:
                            m = it * U + u
                            S = psc[:, u % 2, :]
                            dve.wait_ge(scored, m + 1)
                            nc.vector.tensor_reduce(nm[:, u % 2, 0:1], S[:, 0:P], AX, ALU.max, negate=True)
                            nc.vector.tensor_reduce(nm[:, u % 2, 1:2], S[:, P:3 * P], AX, ALU.max,
                                                    negate=True).then_inc(maxed, 1)
                        if u >= 1:
                            v = u - 1
                            m = it * U + v
                            if v >= 1:
                                w_ = v - 1
                                mm = it * U + w_
                                dve.wait_ge(turned, mm + 1 + 2)
                                dve.wait_ge(mixed, mm - 1 + 0) if w_ >= 2 else None
                                nc.vector.tensor_copy(pT[:, w_ % 2, :, :],
                                                      pp[:, w_ % 2, 0:3 * P].rearrange("p (k c) -> p k c", k=3)
                                                      ).then_inc(t_in, 1)
                            dve.wait_ge(expd, m + 1 + 2)
                            nc.vector.reciprocal(inv[:, v % 2, :], den[:, v % 2, :]).then_inc(inner_, 1)
                            dve.wait_ge(inner_, m + 1)
                            nc.vector.tensor_scalar(pr[:, v % 2, 0, :], pr[:, v % 2, 0, :], inv[:, v % 2, 0:1], None,
                                                    ALU.mult)
                            nc.vector.tensor_scalar(pr[:, v % 2, 1:3, :], pr[:, v % 2, 1:3, :], inv[:, v % 2, 1:2], None,
                                                    ALU.mult).then_inc(scaled, 1)
                        if u == HD + 5:
                            dve.wait_ge(made, it * 2 + 1)
                            back.dve(dve, it * 2, pout[:, 0:2 * P].rearrange("p (k c) -> p k c", k=2), y=False)
                            dve.sem_inc(added, 1)
                    dve.wait_ge(turned, it * U + U + 2)
                    nc.vector.tensor_copy(pT[:, 1, :, :], pp[:, 1, 0:3 * P].rearrange("p (k c) -> p k c", k=3)
                                          ).then_inc(t_in, 1)
                    dve.wait_ge(made, it * 2 + 2)
                    back.dve(dve, it * 2 + 1, pout[:, 0:2 * P].rearrange("p (k c) -> p k c", k=2), y=False)
                    dve.sem_inc(added, 1)


def product_keys(nc, env, a, tag):
    NT, NC_, T = env.NT, env.NC, env.NT * P
    HD, K, NE = 8, 32, 1024
    J = NE // P
    row_scales(nc, env, tag + "sc", (1.0, 1e-6, 0.0, 1.0))
    with ExitStack() as outer:
        sb, ps, sem = scope(nc, outer, tag)
        G = sb("G", [P, HD, 2, K])
        downT, up = sb("downT", [P, NE]), sb("up", [P, J, P])
        g = sb("g", [P, 1])
        ZT = sb("ZT", [P, T])
        with ExitStack() as prep:
            psb, pps, psem = scope(nc, prep, tag + "p")
            wq = psb("wq", [P, HD * 2, P])
            keys = psb("keys", [P, 2, 2, P])
            keysT = psb("keysT", [P, 2, HD * K])
            down = psb("down", [P, J, P])
            load(nc, tag + "ld", [(wq[:, :, :], a["w_q"].rearrange("(j p) c -> p j c", p=P)),
                                  (keys[:, :, :, :], a["keys"].rearrange("(u h) k s d -> (h k) u s d", u=2)),
                                  (down[:, :, :], a["expert_down"].rearrange("(j p) c -> p j c", p=P)),
                                  (up[:, :, :], a["expert_up"].rearrange("(j p) c -> p j c", p=P)),
                                  (g[:, :], a["norm_w"].rearrange("(p o) -> p o", o=1))])
            turn_weights(nc, env, tag + "t", [],
                         [(down[:, j, :], downT[:, j * P:(j + 1) * P]) for j in range(J)]
                         + [(keys[:, t, s, :], keysT[:, s, t * P:(t + 1) * P]) for t in range(2) for s in range(2)])
            products(nc, env, tag + "w", [(wq[:, 2 * h + s, :], keysT[:, s, h * K:(h + 1) * K], G[:, h, s, :], 1.0)
                                          for h in range(HD) for s in range(2)])
        front_pass(nc, env, tag + "f", True, ZT[:, :], scale=g[:, 0:1])
        with ExitStack() as ctx:
            sb, ps, sem = scope(nc, ctx, tag + "a")
            zc = sb("zc", [P, 2, P])
            sims = sb("sims", [P, 2, HD, 2, K])
            top = sb("top", [P, HD, 2, 8])
            cand = sb("cand", [P, HD, 8, 8])
            best = sb("best", [P, HD, 8])
            thr = sb("thr", [P, 2, HD])
            PR, DR, WR = 4, 2, 4
            psums, dsums = sb("psums", [P, PR, K, K]), sb("dsums", [P, DR, K, K])
            w = sb("w", [P, WR, NE])
            gl = sb("gl", [P, 2, J, P])
            hid = sb("hid", [P, J, P])
            psim, phd, pw, pout = ps("psim", [P, 512]), ps("phd", [P, J, P]), ps("pw", [P, 2, J, P]), ps("pout", [P, 512])
            copied, scored, s_in, pooled, paired, vec, weighed, summed, hidden, gelud, mixed, made, added = (
                sem(x) for x in ("copied", "scored", "sin", "pooled", "paired", "vec", "weighed", "summed", "hidden",
                                 "gelud", "mixed", "made", "added"))
            back = Back(nc, env, sb, ps, sem, tiles=1)
            block = ctx.enter_context(nc.Block())
            DVE_SUMS = (2, 6)
            POOL_SUMS = tuple(h for h in range(HD) if h not in DVE_SUMS)
            NP, ND = len(POOL_SUMS), len(DVE_SUMS)
            UNITS = ((0, 1), (2,), (3,), (4, 5), (6,), (7,))
            NU = len(UNITS)
            unit_of = {h: u for u, hs in enumerate(UNITS) for h in hs}
            PAIRS = tuple(hs for hs in UNITS if len(hs) == 2)
            PRELIM, STEPS = 4, 4 + ND

            def sum_of(p, h):
                s1 = sims[:, p, h, 0, :].rearrange("p (i o) -> p i o", o=1).broadcast_to([P, K, K])
                s2 = sims[:, p, h, 1, :].rearrange("p (o j) -> p o j", o=1).broadcast_to([P, K, K])
                return s1, s2

            @block.gpsimd
            def _(pool):
                def form(t, p, k):
                    h = POOL_SUMS[k]
                    need(pool, s_in, t + 1)
                    back_t, back_k = (t, k - PR) if k >= PR else (t - 1, k - PR + NP)
                    need(pool, weighed, back_t * HD + POOL_SUMS[back_k] + 1)
                    s1, s2 = sum_of(p, h)
                    nc.gpsimd.tensor_tensor(psums[:, (NP * p + k) % PR, :, :], s1, s2, ALU.add).then_inc(pooled, 1)

                def pair(t, i):
                    h, g_ = PAIRS[i]
                    need(pool, weighed, t * HD + g_ + 1)
                    nc.gpsimd.tensor_tensor(w[:, h % WR, :], w[:, h % WR, :], w[:, g_ % WR, :], ALU.add).then_inc(paired, 1)

                for k in range(PR):
                    form(0, 0, k)

                def body(it, first, last):
                    for p in range(2):
                        t = it * 2 + p
                        final = last and p == 1
                        form(t, p, 4)
                        pair(t, 0)
                        form(t, p, 5)
                        if not final:
                            form(t + 1, 1 - p, 0)
                            form(t + 1, 1 - p, 1)
                        pair(t, 1)
                        if not final:
                            form(t + 1, 1 - p, 2)
                            form(t + 1, 1 - p, 3)

                rounds(pool, NT // 2, body)

            @block.tensor
            def _(pe):
                def sim(t, p):
                    need(pe, copied, t + 1)
                    need(pe, s_in, t)
                    nc.tensor.matmul(psim[:, :], zc[:, p, :], G[:, :, :, :].rearrange("p h s k -> p (h s k)"),
                                     start=True, stop=True).then_inc(scored, 1)

                def hide(t):
                    hold(pe, gelud, t)
                    for j in range(J):
                        ins = nc.tensor.matmul(phd[:, j, :], downT[:, j * P:(j + 1) * P], ZT[:, bass.ds(t * P, P)],
                                               start=True, stop=True)
                    ins.then_inc(hidden, 1)

                def out(t):
                    need(pe, mixed, t + 1)
                    need(pe, added, t)
                    for j in range(J):
                        ins = nc.tensor.matmul(pout[:, 0:P], hid[:, j, :], up[:, j, :], start=(j == 0), stop=(j == J - 1))
                    ins.then_inc(made, 1)

                def body(it, first, last):
                    for p in range(2):
                        t = it * 2 + p
                        for u, hs in enumerate(UNITS):
                            if u == 0:
                                if not (last and p == 1):
                                    sim(t + 1, 1 - p)
                                need(pe, mixed, t - 1)
                            if len(hs) == 2:
                                need(pe, paired, t * len(PAIRS) + PAIRS.index(hs) + 1)
                            else:
                                need(pe, weighed, t * HD + hs[0] + 1)
                            for j in range(J):
                                ins = nc.tensor.matmul(pw[:, p, j, :], w[:, hs[0] % WR, j * P:(j + 1) * P], env.ident[:, :],
                                                       start=(u == 0 and j % 4 == 0), stop=(u == NU - 1 and j % 4 == 3),
                                                       skip_group_check=True)
                            ins.then_inc(summed, 1)
                            if u == 1 and not (first and p == 0):
                                out(t - 1)
                            if u == 2 and not (last and p == 1):
                                hide(t + 1)

                sim(0, 0)
                hide(0)
                rounds(pe, NT // 2, body)
                out(NT - 1)

            @block.scalar
            def _(act):
                def body(it, first, last):
                    for p in range(2):
                        t = it * 2 + p
                        hold(act, scored, t - 1)
                        nc.scalar.copy(zc[:, p, :], ZT[:, bass.ds(t * P, P)]).then_inc(copied, 1)
                        need(act, weighed, (t - 1) * HD)
                        need(act, scored, t + 1)
                        nc.scalar.copy(sims[:, p, :, :, :].rearrange("p h s k -> p (h s k)"), psim[:, :]).then_inc(s_in, 1)
                        need(act, mixed, t - 1)
                        need(act, hidden, t + 1)
                        for q in range(2):
                            ins = nc.scalar.activation(gl[:, p, 4 * q:4 * q + 4, :], phd[:, 4 * q:4 * q + 4, :], ACT.Gelu)
                        ins.then_inc(gelud, 1)

                rounds(act, NT // 2, body)

            @block.vector
            def _(dve):
                def prelim(t, p, step, count):
                    if step == 0:
                        hold(dve, s_in, t + 1)
                        for h in range(HD):
                            for s in range(2):
                                ins = nc.vector.max(top[:, h, s, :], sims[:, p, h, s, :])
                    if step == 1:
                        dve.wait_ge(vec, count)
                        t1 = top[:, :, 0, :].rearrange("p h (i o) -> p h i o", o=1).broadcast_to([P, HD, 8, 8])
                        t2 = top[:, :, 1, :].rearrange("p h (o i) -> p h o i", o=1).broadcast_to([P, HD, 8, 8])
                        ins = nc.vector.tensor_tensor(cand[:, :, :, :], t1, t2, ALU.add)
                    if step == 2:
                        hold(dve, vec, count)
                        for h in range(HD):
                            ins = nc.vector.max(best[:, h, :], cand[:, h, :, :].rearrange("p i j -> p (i j)"))
                    if step == 3:
                        dve.wait_ge(vec, count)
                        ins = nc.vector.tensor_scalar(thr[:, p, :], best[:, :, 7], 1.1754944e-38, None, ALU.max)
                    ins.then_inc(vec, 1)

                def form(t, p, k):
                    need(dve, weighed, (t - 1) * HD + DVE_SUMS[k] + 1)
                    s1, s2 = sum_of(p, DVE_SUMS[k])
                    nc.vector.tensor_tensor(dsums[:, k, :, :], s1, s2, ALU.add).then_inc(vec, 1)

                def weigh(t, p, h, count):
                    if h in DVE_SUMS:
                        src = dsums[:, DVE_SUMS.index(h), :, :]
                        dve.wait_ge(vec, count)
                    else:
                        k = POOL_SUMS.index(h)
                        src = psums[:, (NP * p + k) % PR, :, :]
                        need(dve, pooled, t * NP + k + 1)
                    back_t, back_h = (t, h - WR) if h >= WR else (t - 1, h + HD - WR)
                    need(dve, summed, back_t * NU + unit_of[back_h] + 1)
                    nc.vector.scalar_tensor_tensor(w[:, h % WR, :].rearrange("p (i j) -> p i j", i=K), src,
                                                   thr[:, p, h:h + 1], src, ALU.is_ge, ALU.mult).then_inc(weighed, 1)

                def finish(t, p):
                    need(dve, summed, (t + 1) * NU)
                    need(dve, gelud, t + 1)
                    need(dve, made, t)
                    for q in range(2):
                        ins = nc.vector.tensor_tensor(hid[:, 4 * q:4 * q + 4, :], gl[:, p, 4 * q:4 * q + 4, :],
                                                      pw[:, p, 4 * q:4 * q + 4, :], ALU.mult)
                    ins.then_inc(mixed, 1)

                def residual(t):
                    need(dve, made, t + 1)
                    back.dve(dve, t, pout[:, 0:P].rearrange("p (k c) -> p k c", k=1), y=False)
                    dve.sem_inc(added, 1)

                for step in range(PRELIM):
                    prelim(0, 0, step, step)

                def body(it, first, last):
                    for p in range(2):
                        t = it * 2 + p
                        done = PRELIM + STEPS * t
                        begun, final = first and p == 0, last and p == 1
                        dve.wait_ge(vec, done)
                        weigh(t, p, 0, done)
                        form(t, p, 0)
                        weigh(t, p, 1, done)
                        if not begun:
                            finish(t - 1, 1 - p)
                        weigh(t, p, 2, done + 1)
                        if not final:
                            prelim(t + 1, 1 - p, 0, done + 1)
                        weigh(t, p, 3, done)
                        if not final:
                            prelim(t + 1, 1 - p, 1, done + 2)
                        weigh(t, p, 4, done)
                        form(t, p, 1)
                        if not final:
                            prelim(t + 1, 1 - p, 2, done + 3)
                        weigh(t, p, 5, done)
                        if not begun:
                            residual(t - 1)
                        if not final:
                            prelim(t + 1, 1 - p, 3, done + 5)
                        weigh(t, p, 6, done + 4 - (2 if final else 0))
                        weigh(t, p, 7, done)

                rounds(dve, NT // 2, body)
                finish(NT - 1, 1)
                residual(NT - 1)


def rotary(nc, env, a, tag):
    NT, NC_, T = env.NT, env.NC, env.NT * P
    HD, D, S = 16, 8, 8
    NB = NT // 2
    row_scales(nc, env, tag + "sc", None)
    with ExitStack() as outer:
        sb, ps, sem = scope(nc, outer, tag)
        wT, pT = sb("wT", [P, 3 * P]), sb("pT", [P, P])
        three = sb("three", [P, HD, P], BF16)
        wkq, qw = sb("wkq", [P, D]), sb("qw", [P, D])
        KK, QQ = sb("KK", [P, NT, P]), sb("QQ", [P, NT, P])
        V = sb("V", [P, NT, HD, D + 1])
        norm2 = sb("norm2", [P, 2, NT, HD])
        with ExitStack() as prep:
            psb, pps, psem = scope(nc, prep, tag + "p")
            w, pw = psb("w", [P, 3, P]), psb("pw", [P, P])
            ZT = psb("ZT", [P, T])
            zc = psb("zc", [P, 2, CH])
            rope = psb("rope", [P, 2, 2, P])
            load(nc, tag + "ld", [(w[:, :, :], a["W_kqv"].rearrange("(j p) c -> p j c", p=P)),
                                  (pw[:, :], a["W_proj"]),
                                  (rope[:, :, :, :], a["rope"]), (three[:, :, :], a["three"]),
                                  (wkq[:, :], a["k_norm_w"].rearrange("(o d) -> o d", o=1).broadcast_to([P, D])),
                                  (qw[:, :], a["q_norm_w"].rearrange("(o d) -> o d", o=1).broadcast_to([P, D]))])
            turn_weights(nc, env, tag + "t", [], [(w[:, j, :], wT[:, j * P:(j + 1) * P]) for j in range(3)]
                         + [(pw[:, :], pT[:, :])])
            front_pass(nc, env, tag + "f", False, ZT[:, :])
            t1, t2 = psb("t1", [P, 2, 2, 2 * P]), psb("t2", [P, 2, 2, 2 * P])
            sq = psb("sq", [P, 2, TPC, P])
            pk, pv = pps("pk", [P, 2, TPC, 2 * P]), pps("pv", [P, 2, TPC, P])
            copied, made, taken, vin, cosd, rotated, squared, normed = (psem(x) for x in (
                "copied", "made", "taken", "vin", "cosd", "rotated", "squared", "normed"))
            with nc.Block() as block:
                @block.gpsimd
                def _(pool):
                    nc.gpsimd.memset(V[:, :, :, D:D + 1], 1.0)
                    with pool.Fori(0, NC_ // 2) as it:
                        for p in range(2):
                            n = it * 2 + p
                            hold(pool, made, n + 1)
                            nc.gpsimd.tensor_copy(zc[:, p, :], ZT[:, bass.ds(n * CH, CH)]).then_inc(copied, 1)
                            for q in range(2):
                                m = 2 * n + q
                                pool.wait_ge(cosd, 3 * m + 3 + 12)
                                for z, dst in ((0, KK), (1, QQ)):
                                    ins = nc.gpsimd.tensor_tensor(dst[:, bass.ds(2 * m, 2), :], t1[:, q, :, z * P:(z + 1) * P],
                                                                  t2[:, q, :, z * P:(z + 1) * P], ALU.add)
                                ins.then_inc(rotated, 1)

                @block.tensor
                def _(pe):
                    pe.sem_inc(made, 2)
                    with pe.Fori(0, NC_ // 2) as it:
                        for p in range(2):
                            n = it * 2 + p
                            pe.wait_ge(copied, n + 1)
                            pe.wait_ge(cosd, 6 * n + 6)
                            pe.wait_ge(vin, n + 1)
                            for k in range(TPC):
                                z = zc[:, p, k * P:(k + 1) * P]
                                nc.tensor.matmul(pk[:, p, k, :], z, wT[:, 0:2 * P], start=True, stop=True)
                                ins = nc.tensor.matmul(pv[:, p, k, :], z, wT[:, 2 * P:3 * P], start=True, stop=True)
                            ins.then_inc(made, 1)

                @block.vector
                def _(dve):
                    dve.sem_inc(cosd, 12)
                    with dve.Fori(0, NC_ // 2) as it:
                        for p in range(2):
                            n = it * 2 + p
                            dve.wait_ge(made, n + 1 + 2)
                            for q in range(2):
                                m = 2 * n + q
                                dve.wait_ge(rotated, m)
                                for z in range(2):
                                    x = pk[:, p, 2 * q:2 * q + 2, z * P:(z + 1) * P]
                                    ins = nc.vector.tensor_tensor(t1[:, q, :, z * P:(z + 1) * P], x, rope[:, :, 0, :], ALU.mult)
                                ins.then_inc(cosd, 1)
                                for half in range(2):
                                    for z in range(2):
                                        def part(v, f):
                                            return v.rearrange("p t (h f d) -> p t h f d", f=2, d=D // 2)[:, :, :, f, :]
                                        x = part(pk[:, p, 2 * q:2 * q + 2, z * P:(z + 1) * P], 1 - half)
                                        ins = nc.vector.tensor_tensor(part(t2[:, q, :, z * P:(z + 1) * P], half), x,
                                                                      part(rope[:, :, 1, :], half), ALU.mult)
                                    ins.then_inc(cosd, 1)
                            for z in range(2):
                                dve.wait_ge(squared, 2 * n + z + 1)
                                nc.vector.tensor_reduce(norm2[:, z, bass.ds(n * TPC, TPC), :],
                                                        sq[:, z, :, :].rearrange("p t (h d) -> p t h d", d=D), AX,
                                                        ALU.add).then_inc(normed, 1)

                @block.scalar
                def _(act):
                    act.sem_inc(vin, 2)
                    with act.Fori(0, NC_ // 2) as it:
                        for p in range(2):
                            n = it * 2 + p
                            hold(act, made, n + 1 + 2)
                            for k in range(TPC):
                                ins = nc.scalar.copy(V[:, n * TPC + k, :, 0:D], pv[:, p, k, :].rearrange(
                                    "p (h d) -> p h d", d=D))
                            ins.then_inc(vin, 1)
                            act.wait_ge(rotated, 2 * n + 2)
                            hold(act, normed, 2 * n)
                            for z, src in ((0, KK), (1, QQ)):
                                nc.scalar.activation(sq[:, z, :, :], src[:, bass.ds(n * TPC, TPC), :], ACT.Square
                                                     ).then_inc(squared, 1)
        with ExitStack() as ctx:
            sb, ps, sem = scope(nc, ctx, tag + "n")
            rms = sb("rms", [P, 2, NT, HD])
            rooted, vec, done, weighed = sem("rooted"), sem("vec"), sem("done"), sem("weighed")
            block = ctx.enter_context(nc.Block())

            @block.scalar
            def _(act):
                nc.scalar.activation(rms[:, :, :, :], norm2[:, :, :, :], ACT.Sqrt, scale=1.0 / D).then_inc(rooted, 1)

            @block.vector
            def _(dve):
                link = Link(dve, vec)
                link(nc.vector.tensor_tensor(wkq[:, :], wkq[:, :], qw[:, :], ALU.mult))
                dve.wait_ge(rooted, 1)
                link(nc.vector.tensor_scalar(rms[:, :, :, :], rms[:, :, :, :], 1e-6, None, ALU.add))
                link(nc.vector.reciprocal(norm2[:, :, :, :], rms[:, :, :, :]))
                for z, x in ((0, KK), (1, QQ)):
                    v = x[:, :, :].rearrange("p t (h d) -> p (t h) d", d=D)
                    f = norm2[:, z, :, :].rearrange("p t (h o) -> p (t h) o", o=1).broadcast_to([P, NT * HD, D])
                    nc.vector.tensor_tensor(v, v, f, ALU.mult).then_inc(done, 1)
                dve.wait_ge(done, 1)
                v = KK[:, :, :].rearrange("p t (h d) -> p (t h) d", d=D)
                f = wkq[:, :].rearrange("p (o d) -> p o d", o=1).broadcast_to([P, NT * HD, D])
                link(nc.vector.scalar_tensor_tensor(v, v, float(D) ** -0.5, f, ALU.mult, ALU.mult))
                dve.wait_ge(done, 2)
        with ExitStack() as ctx:
            sb, ps, sem = scope(nc, ctx, tag + "a")
            KS, QS = sb("KS", [P, 2, 2 * HD * S * D], BF16), sb("QS", [P, 2, 2 * HD * S * D], BF16)
            rk, rq = sb("rk", [P, 2, 2 * P]), sb("rq", [P, 2, 2 * P])
            KT, QT = sb("KT", [P, 2, HD // 2, SEQ], BF16), sb("QT", [P, 2, HD // 2, SEQ], BF16)
            nm = sb("nm", [P, 2, HD])
            nr = sb("nr", [P, 2, HD])
            nb = sb("nb", [P, 2, 2, 64], BF16)
            nT = sb("nT", [P, 2, SEQ], BF16)
            pr = sb("pr", [P, 3, 3 * P])
            inv = sb("inv", [P, 2, HD])
            yt, yT = sb("yt", [P, 2, HD, D]), sb("yT", [P, SEQ])
            ptr = ps("ptr", [P, 2, 1024], BF16)
            psc, pst = ps("psc", [P, 2, 512]), ps("pst", [P, 2, 512])
            py, pout = ps("py", [P, 2, HD, 16]), ps("pout", [P, 512])
            (zeroed, kcast, qcast, krest, qrest, placed, t_in, scored, maxed, nmaxed, n_placed, n_in, shifted, expd, mixed,
             y_norm, y_placed, y_in, made, added, ainv) = (sem(x) for x in (
                "zeroed", "kcast", "qcast", "krest", "qrest", "placed", "tin", "scored", "maxed", "nmaxed",
                "nplaced", "nin", "shifted", "expd", "mixed", "ynorm", "yplaced", "yin", "made", "added", "ainv"))
            back = Back(nc, env, sb, ps, sem, tiles=2)
            block = ctx.enter_context(nc.Block())

            def first_head(u):
                g = 8 * (u // 3 % 2) + u // 6
                return g if u % 3 == 0 else g + 4 * (u % 3 - 1)

            def slots(buf, p):
                return buf[:, p, :].rearrange("p (g s d) -> p g s d", s=S, d=D)

            def spread(x, k):
                return x.rearrange("p (g o d) -> p g o d", o=1, d=D).broadcast_to([P, 2 * HD, k, D])

            def heads(x):
                return x.rearrange("p (g d) -> p g d", d=D)

            def steps(eng, first, second, tail):
                first(0, 0)
                with eng.Fori(0, NB // 2 - 1) as it:
                    second(it * 2, 0, True)
                    second(it * 2 + 1, 1, True)
                second(NB - 2, 0, True)
                second(NB - 1, 1, False)

            @block.scalar
            def _(act):
                def cast(n, p):
                    k = KK[:, bass.ds(2 * n, 2), :].rearrange("p t c -> p (t c)")
                    ks = slots(KS, p)
                    hold(act, placed, 4 * (n - 1) + 4)
                    nc.scalar.copy(ks[:, :, 0:3, :], spread(k, 3)).then_inc(kcast, 1)
                    act.wait_ge(krest, 2 * n + 1)
                    nc.scalar.copy(ks[:, :, 3:5, :], spread(rk[:, 0, :], 2)).then_inc(kcast, 1)
                    act.wait_ge(krest, 2 * n + 2)
                    nc.scalar.copy(ks[:, :, 5, :], heads(rk[:, 1, :])).then_inc(kcast, 1)

                def second(n, p, more):
                    for h in range(HD):
                        m = n * HD + h
                        act.wait_ge(shifted, m + 1)
                        act.wait_ge(mixed, m + 1)
                        nc.scalar.activation(pr[:, h % 2, :], pst[:, h % 2, 0:3 * P], ACT.Exp).then_inc(expd, 1)
                        if h == 1 and more:
                            cast(n + 1, 1 - p)
                    act.wait_ge(y_placed, n + 1)
                    nc.scalar.copy(yT[:, :], pout[:, 0:SEQ]).then_inc(y_in, 1)

                act.sem_inc(expd, 2)
                act.wait_ge(zeroed, 1)
                steps(act, cast, second, None)

            @block.gpsimd
            def _(pool):
                nc.gpsimd.memset(KS[:, :, :], 0.0).then_inc(zeroed, 1)
                nc.gpsimd.memset(QS[:, :, :], 0.0).then_inc(zeroed, 1)
                nc.gpsimd.memset(nb[:, :, :, :], 0.0).then_inc(zeroed, 1)

                def rest(n, p):
                    ks, qs = slots(KS, p), slots(QS, p)
                    k = KK[:, bass.ds(2 * n, 2), :].rearrange("p t (h d) -> p (t h) d", d=D)
                    q = QQ[:, bass.ds(2 * n, 2), :].rearrange("p t (h d) -> p (t h) d", d=D)
                    pool.wait_ge(kcast, 3 * n + 1)
                    nc.gpsimd.tensor_tensor(heads(rk[:, 0, :]), k, ks[:, :, 0, :], ALU.subtract).then_inc(krest, 1)
                    pool.wait_ge(qcast, 5 * n + 2)
                    nc.gpsimd.tensor_tensor(heads(rq[:, 0, :]), q, qs[:, :, 0, :], ALU.subtract).then_inc(qrest, 1)
                    pool.wait_ge(kcast, 3 * n + 2)
                    pool.wait_ge(krest, 2 * n + 1)
                    nc.gpsimd.tensor_tensor(heads(rk[:, 1, :]), heads(rk[:, 0, :]), ks[:, :, 3, :], ALU.subtract).then_inc(krest, 1)
                    pool.wait_ge(qcast, 5 * n + 4)
                    pool.wait_ge(qrest, 2 * n + 1)
                    nc.gpsimd.tensor_tensor(heads(rq[:, 1, :]), heads(rq[:, 0, :]), qs[:, :, 1, :], ALU.subtract).then_inc(qrest, 1)

                def second(n, p, more):
                    if more:
                        rest(n + 1, 1 - p)

                steps(pool, rest, second, None)

            @block.tensor
            def _(pe):
                def place(n, p, g):
                    m = 4 * n + g
                    if g == 0:
                        pe.wait_ge(kcast, 3 * n + 3)
                    if g == 2:
                        pe.wait_ge(qcast, 5 * n + 5)
                    pe.wait_ge(t_in, m + 1)
                    src = (KS if g < 2 else QS)[:, p, :].rearrange("p (t a c) -> p t a c", t=2, c=P)
                    for a_ in range(4):
                        for t in range(2):
                            ins = nc.tensor.transpose(ptr[:, g % 2, (a_ * 2 + t) * P:(a_ * 2 + t + 1) * P],
                                                      src[:, t, 4 * (g % 2) + a_, :], env.identb[:, :])
                    ins.then_inc(placed, 1)

                def rows_of(h):
                    return slice(64 * (h % 2), 64 * (h % 2) + 64)

                def score(n, p, u):
                    m = 12 * n + u
                    if u == 0:
                        pe.wait_ge(t_in, 4 * n + 4 + 2)
                    pe.wait_ge(maxed, m + 1)
                    B = psc[:, u % 2, :]
                    g = first_head(u)
                    if u % 3 == 0:
                        for k in range(4):
                            h = g + 2 * k
                            r_ = rows_of(h)
                            o = B[:, k * P:(k + 1) * P]
                            nc.tensor.matmul(o, env.identb[:, :], env.causal[:, :], start=True, stop=False)
                            ins = nc.tensor.matmul(o, QT[r_, p, h // 2, 0:P], KT[r_, p, h // 2, 0:P], start=False, stop=True)
                    else:
                        for k in range(2):
                            h = g + 2 * k
                            r_ = rows_of(h)
                            nc.tensor.matmul(B[:, k * SEQ + P:(k + 1) * SEQ], env.identb[:, :], env.causal[:, :],
                                             start=True, stop=True)
                            ins = nc.tensor.matmul(B[:, k * SEQ:(k + 1) * SEQ], QT[r_, p, h // 2, P:SEQ],
                                                   KT[r_, p, h // 2, :], start=False, stop=True, skip_group_check=True)
                    ins.then_inc(scored, 1)

                def turn_max(n, p):
                    pe.wait_ge(nmaxed, 5 * n + 5)
                    pe.wait_ge(t_in, 4 * n + 4 + 2)
                    for t in range(2):
                        ins = nc.tensor.transpose(ptr[:, 0, t * P:(t + 1) * P],
                                                  nb[:, t, :, :].rearrange("p s h -> p (s h)"), env.identb[:, :])
                    ins.then_inc(n_placed, 1)

                def shift(n, p, h):
                    m = n * HD + h
                    pe.wait_ge(expd, m + 1)
                    if h == 0:
                        pe.wait_ge(n_in, n + 1)
                    B = pst[:, h % 2, :]
                    r_ = rows_of(h)
                    one = three[r_, h, :]
                    for c0, c1, j0, i0 in ((0, SEQ, 0, 0), (SEQ, SEQ + P, P, P)):
                        nc.tensor.matmul(B[:, c0:c0 + P], env.identb[:, :], env.causalT[:, :], start=True, stop=True)
                        nc.tensor.matmul(B[:, c0:c1], one, nT[r_, p, i0:SEQ], start=False, stop=True, skip_group_check=True)
                        ins = nc.tensor.matmul(B[:, c0:c1], KT[r_, p, h // 2, j0:j0 + P], QT[r_, p, h // 2, i0:SEQ],
                                               start=False, stop=True, skip_group_check=True)
                    ins.then_inc(shifted, 1)

                def mix(n, p, h):
                    m = n * HD + h
                    pe.wait_ge(expd, m + 1 + 2)
                    if h == 0:
                        pe.wait_ge(y_norm, n)
                    e = pr[:, h % 2, :]
                    v0, v1 = V[:, 2 * n, h, :], V[:, 2 * n + 1, h, :]
                    nc.tensor.matmul(py[:, 0, h, 0:D + 1], e[:, 0:P], v0, start=True, stop=True)
                    nc.tensor.matmul(py[:, 1, h, 0:D + 1], e[:, P:2 * P], v0, start=True, stop=False)
                    nc.tensor.matmul(py[:, 1, h, 0:D + 1], e[:, 2 * P:3 * P], v1, start=False, stop=True).then_inc(mixed, 1)

                def first(n, p):
                    for g in range(4):
                        place(n, p, g)
                    for u in range(12):
                        score(n, p, u)
                    turn_max(n, p)

                def second(n, p, more):
                    A = []
                    if more:
                        A = [lambda g=g: place(n + 1, 1 - p, g) for g in range(4)]
                        A += [lambda u=u: score(n + 1, 1 - p, u) for u in range(12)]
                    for h in range(HD + 1):
                        if h < HD:
                            shift(n, p, h)
                        if h >= 3:
                            for _ in range(2):
                                if A:
                                    A.pop(0)()
                        if h >= 1:
                            mix(n, p, h - 1)
                    while A:
                        A.pop(0)()
                    pe.wait_ge(y_norm, n + 1)
                    pe.wait_ge(added, n)
                    for t in range(2):
                        ins = nc.tensor.transpose(pout[:, t * P:(t + 1) * P], yt[:, t, :, :].rearrange("p h d -> p (h d)"),
                                                  env.ident[:, :])
                    ins.then_inc(y_placed, 1)
                    if more:
                        turn_max(n + 1, 1 - p)
                    pe.wait_ge(y_in, n + 1)
                    for t in range(2):
                        ins = nc.tensor.matmul(pout[:, SEQ + t * P:SEQ + (t + 1) * P], yT[:, t * P:(t + 1) * P], pT[:, :],
                                               start=True, stop=True)
                    ins.then_inc(made, 1)

                pe.sem_inc(placed, 4)
                pe.sem_inc(mixed, 2)
                steps(pe, first, second, None)

            @block.vector
            def _(dve):
                def cast(n, p):
                    q = QQ[:, bass.ds(2 * n, 2), :].rearrange("p t (h d) -> p (t h) d", d=D)
                    qs = slots(QS, p)
                    q1 = QQ[:, bass.ds(2 * n, 2), :].rearrange("p t c -> p (t c)")
                    hold(dve, placed, 4 * (n - 1) + 4)
                    nc.vector.tensor_copy(qs[:, :, 0, :], q).then_inc(qcast, 1)
                    nc.vector.tensor_copy(qs[:, :, 3:6:2, :], spread(q1, 2)).then_inc(qcast, 1)
                    dve.wait_ge(qrest, 2 * n + 1)
                    nc.vector.tensor_copy(qs[:, :, 1, :], heads(rq[:, 0, :])).then_inc(qcast, 1)
                    nc.vector.tensor_copy(qs[:, :, 4, :], heads(rq[:, 0, :])).then_inc(qcast, 1)
                    dve.wait_ge(qrest, 2 * n + 2)
                    nc.vector.tensor_copy(qs[:, :, 2, :], heads(rq[:, 1, :])).then_inc(qcast, 1)

                def maxima(n, p):
                    for g in range(4):
                        dve.wait_ge(placed, 4 * n + g + 1 + 4)
                        dst = (KT if g < 2 else QT)[:, p, 4 * (g % 2):4 * (g % 2) + 4, :]
                        nc.vector.tensor_copy(dst, ptr[:, g % 2, :].rearrange("p (a c) -> p a c", a=4)).then_inc(t_in, 1)
                    for u in range(12):
                        g = first_head(u)
                        dve.wait_ge(scored, 12 * n + u + 1)
                        if u % 3 == 0:
                            dst, src = nm[:, 0, g:g + 7:2], psc[:, u % 2, :].rearrange("p (k c) -> p k c", k=4)
                        else:
                            dst, src = nm[:, 1, g:g + 3:2], psc[:, u % 2, :].rearrange("p (k c) -> p k c", k=2)
                        nc.vector.tensor_reduce(dst, src, AX, ALU.max, negate=True).then_inc(maxed, 1)
                    dve.wait_ge(maxed, 12 * n + 12 + 2)
                    dve.wait_ge(n_placed, n)
                    link = Link(dve, nmaxed, 5 * n)
                    def both(x):
                        return x.rearrange("p t (o h) -> p t o h", o=1).broadcast_to([P, 2, 2, HD])

                    link(nc.vector.tensor_copy(nb[:, :, :, 0:HD], both(nm[:, :, :])))
                    link(nc.vector.tensor_tensor(nr[:, :, :], nm[:, :, :], nb[:, :, 0, 0:HD], ALU.subtract))
                    link(nc.vector.tensor_copy(nb[:, :, :, HD:2 * HD], both(nr[:, :, :])))
                    link(nc.vector.tensor_tensor(nm[:, :, :], nr[:, :, :], nb[:, :, 0, HD:2 * HD], ALU.subtract))
                    link(nc.vector.tensor_copy(nb[:, :, :, 2 * HD:3 * HD], both(nm[:, :, :])))

                def max_in(n, p):
                    dve.wait_ge(n_placed, n + 1)
                    nc.vector.tensor_copy(nT[:, p, :], ptr[:, 0, 0:SEQ]).then_inc(n_in, 1)

                def first(n, p):
                    cast(n, p)
                    maxima(n, p)
                    max_in(n, p)

                def second(n, p, more):
                    if more:
                        cast(n + 1, 1 - p)
                        maxima(n + 1, 1 - p)
                    dve.wait_ge(mixed, n * HD + HD + 2)
                    nc.vector.reciprocal(inv[:, :, :], py[:, :, :, D]).then_inc(ainv, 1)
                    dve.wait_ge(ainv, 2 * n + 1)
                    for t in range(2):
                        f = inv[:, t, :].rearrange("p (h o) -> p h o", o=1).broadcast_to([P, HD, D])
                        ins = nc.vector.tensor_tensor(yt[:, t, :, :], py[:, t, :, 0:D], f, ALU.mult)
                    ins.then_inc(y_norm, 1)
                    dve.sem_inc(ainv, 1)
                    if more:
                        max_in(n + 1, 1 - p)
                    dve.wait_ge(made, n + 1)
                    back.dve(dve, n, pout[:, SEQ:2 * SEQ].rearrange("p (k c) -> p k c", k=2), y=False)
                    dve.sem_inc(added, 1)

                dve.sem_inc(t_in, 2)
                dve.sem_inc(maxed, 2)
                dve.wait_ge(zeroed, 3)
                steps(dve, first, second, None)


def state_space(nc, env, a, tag):
    NT, NC_, T = env.NT, env.NC, env.NT * P
    DS, TAPS, EPS = 64, 4, 1e-4
    NB, GH = NT // 2, NC_ // 2
    row_scales(nc, env, tag + "sc", None)
    with ExitStack() as outer:
        sb, ps, sem = scope(nc, outer, tag)
        wT = sb("wT", [P, 3, DS])
        outT = sb("outT", [P, P])
        cw, cb = sb("cw", [P, TAPS]), sb("cb", [P, 1])
        bias = sb("bias", [P, 3])
        A, near, rA = sb("A", [P, 1]), sb("near", [P, 1]), sb("rA", [P, 1])
        ob, ones = sb("ob", [1, P]), sb("ones", [1, P])
        ZT, XC = sb("ZT", [P, T]), sb("XC", [P, T])
        with ExitStack() as prep:
            psb, pps, psem = scope(nc, prep, tag + "p")
            wd = psb("wd", [DS, P])
            wbc = psb("wbc", [DS, 2, 2, P])
            wm = psb("wm", [DS, 2, P])
            ow = psb("ow", [P, 2, DS])
            bb = psb("bb", [P, 2, 2])
            t = psb("t", [P, 4])
            pw, pb = a["in_proj_w"], a["in_proj_b"]
            loads = [(wd[:, :], pw[0:DS, :]),
                     (wbc[:, :, :, :], pw[DS:5 * DS, :].rearrange("(z n g) c -> n z g c", z=2, g=2)),
                     (cw[:, :], a["conv_w"].rearrange("c o k -> c (o k)")),
                     (cb[:, :], a["conv_b"].rearrange("(p o) -> p o", o=1)),
                     (ob[:, :], a["out_proj_b"].rearrange("(o d) -> o d", o=1))]
            for half in range(2):
                r_ = slice(half * DS, (half + 1) * DS)
                loads += [(bias[r_, 0:1], pb[0:DS].rearrange("(p o) -> p o", o=1)),
                          (bb[r_, :, :], pb[DS:5 * DS].rearrange("(z n g) -> n z g", z=2, g=2)),
                          (A[r_, :], a["A_log"].rearrange("(p o) -> p o", o=1)),
                          (ow[:, half, :], a["out_proj_w"])]
            load(nc, tag + "ld", loads)
            vec, ex = psem("vec"), psem("ex")
            with nc.Block() as block:
                @block.scalar
                def _(act):
                    nc.scalar.activation(t[:, 0:1], A[:, :], ACT.Exp).then_inc(ex, 1)

                @block.vector
                def _(dve):
                    link = Link(dve, vec)
                    link(nc.vector.memset(ones[:, :], 1.0))
                    for z in range(2):
                        link(nc.vector.tensor_tensor(wm[:, z, :], wbc[:, z, 0, :], wbc[:, z, 1, :], ALU.add))
                        link(nc.vector.tensor_scalar(wm[:, z, :], wm[:, z, :], 0.5, None, ALU.mult))
                        link(nc.vector.tensor_tensor(bias[:, 1 + z:2 + z], bb[:, z, 0:1], bb[:, z, 1:2], ALU.add))
                        link(nc.vector.tensor_scalar(bias[:, 1 + z:2 + z], bias[:, 1 + z:2 + z], 0.5, None, ALU.mult))
                    dve.wait_ge(ex, 1)
                    link(nc.vector.tensor_scalar(near[:, :], t[:, 0:1], EPS, None, ALU.is_lt))
                    link(nc.vector.tensor_scalar(A[:, :], t[:, 0:1], -1.0, None, ALU.mult))
                    link(nc.vector.tensor_tensor(t[:, 1:2], A[:, :], near[:, :], ALU.subtract))
                    link(nc.vector.reciprocal(t[:, 2:3], t[:, 1:2]))
                    link(nc.vector.tensor_scalar(t[:, 3:4], near[:, :], -1.0, 1.0, ALU.mult, ALU.add))
                    link(nc.vector.tensor_tensor(rA[:, :], t[:, 2:3], t[:, 3:4], ALU.mult))
            turn_weights(nc, env, tag + "t", [], [(wd[:, :], wT[:, 0, :])]
                         + [(wm[:, z, :], wT[:, 1 + z, :]) for z in range(2)]
                         + [(ow[:, :, :].rearrange("p a n -> p (a n)"), outT[:, :])])
        front_pass(nc, env, tag + "f", False, ZT[:, :])
        with ExitStack() as ctx:
            sb, ps, sem = scope(nc, ctx, tag + "c")
            vec = sem("vec")
            block = ctx.enter_context(nc.Block())
            L = SEQ - 1

            @block.vector
            def _(dve):
                link = Link(dve, vec)
                z = ZT[:, :].rearrange("p (s t) -> p s t", t=SEQ)
                x = XC[:, :].rearrange("p (s t) -> p s t", t=SEQ)
                link(nc.vector.memset(x[:, :, L:SEQ], 0.0))
                link(nc.vector.tensor_scalar(x[:, :, 0:L], z[:, :, 0:L], cw[:, 1:2], cb[:, 0:1], ALU.mult, ALU.add))
                for k, lo, hi in ((0, 1, L), (2, 0, L), (3, 0, L - 1)):
                    link(nc.vector.scalar_tensor_tensor(x[:, :, lo:hi], z[:, :, lo + k - 1:hi + k - 1], cw[:, k:k + 1],
                                                        x[:, :, lo:hi], ALU.mult, ALU.add))
        with ExitStack() as ctx:
            sb, ps, sem = scope(nc, ctx, tag + "s")
            d, l, e, w, c, ab, q, h_, y = (sb(k, [P, CH]) for k in ("d", "l", "e", "w", "c", "ab", "q", "h", "y"))
            pp, po = ps("pp", [P, 3, 512]), ps("po", [P, 2, 512])
            made, acts, vec, outs, added = sem("made"), sem("acts"), sem("vec"), sem("outs"), sem("added")
            back = Back(nc, env, sb, ps, sem)
            block = ctx.enter_context(nc.Block())
            STEPS = 15

            @block.tensor
            def _(pe):
                for g in range(GH):
                    pe.wait_ge(vec, STEPS * g)
                    for z in range(3):
                        for half in range(2):
                            n = g + half * GH
                            ins = nc.tensor.matmul(pp[half * DS:(half + 1) * DS, z, :], wT[:, z, :],
                                                   XC[:, n * CH:(n + 1) * CH], start=True, stop=True)
                    ins.then_inc(made, 1)
                    pe.wait_ge(vec, STEPS * g + STEPS)
                    pe.wait_ge(added, 2 * g)
                    for half in range(2):
                        r_ = slice(half * DS, (half + 1) * DS)
                        for k in range(TPC):
                            o = po[:, half, k * P:(k + 1) * P]
                            nc.tensor.matmul(o, ones[:, :], ob[:, :], start=True, stop=False)
                            ins = nc.tensor.matmul(o, y[r_, k * P:(k + 1) * P], outT[r_, :], start=False, stop=True)
                        ins.then_inc(outs, 1)

            @block.scalar
            def _(act):
                for g in range(GH):
                    link = Link(act, acts, 5 * g)
                    act.wait_ge(made, g + 1)
                    link(nc.scalar.activation(d[:, :], pp[:, 0, :], ACT.Identity, bias=bias[:, 0:1]))
                    link(nc.scalar.activation(l[:, :], d[:, :], ACT.Abs))
                    link(nc.scalar.activation(e[:, :], l[:, :], ACT.Exp, scale=-1.0))
                    link(nc.scalar.activation(l[:, :], e[:, :], ACT.Ln, bias=1.0))
                    act.wait_ge(vec, STEPS * g + 4)
                    link(nc.scalar.activation(ab[:, :], d[:, :], ACT.Exp, scale=A[:, 0:1]))

            @block.vector
            def _(dve):
                for g in range(GH):
                    link = Link(dve, vec, STEPS * g)
                    dve.wait_ge(acts, 5 * g + 3)
                    link(nc.vector.tensor_scalar(w[:, :], e[:, :], 1.0, -1.0, ALU.add, ALU.add))
                    link(nc.vector.tensor_tensor(c[:, :], e[:, :], w[:, :], ALU.subtract))
                    dve.wait_ge(acts, 5 * g + 4)
                    link(nc.vector.scalar_tensor_tensor(l[:, :], d[:, :], 0.0, l[:, :], ALU.max, ALU.add))
                    link(nc.vector.tensor_tensor(d[:, :], l[:, :], c[:, :], ALU.add))
                    link(nc.vector.tensor_scalar(w[:, :], d[:, :], A[:, 0:1], None, ALU.mult))
                    link(nc.vector.tensor_scalar(q[:, :], w[:, :], 1.0 / 6.0, 0.5, ALU.mult, ALU.add))
                    link(nc.vector.tensor_tensor(c[:, :], q[:, :], w[:, :], ALU.mult))
                    link(nc.vector.tensor_scalar(q[:, :], c[:, :], 1.0, near[:, 0:1], ALU.add, ALU.mult))
                    dve.wait_ge(acts, 5 * g + 5)
                    link(nc.vector.tensor_scalar(w[:, :], ab[:, :], 1.0, rA[:, 0:1], ALU.subtract, ALU.mult))
                    link(nc.vector.tensor_tensor(c[:, :], w[:, :], q[:, :], ALU.add))
                    link(nc.vector.scalar_tensor_tensor(q[:, :], pp[:, 1, :], bias[:, 1:2], c[:, :], ALU.add, ALU.mult))
                    for s in range(SPC):
                        cols = slice(s * SEQ, (s + 1) * SEQ)
                        link(nc.vector.tensor_tensor_scan(h_[:, cols], ab[:, cols], q[:, cols], 0.0, ALU.mult, ALU.add))
                    dve.wait_ge(outs, 2 * g)
                    link(nc.vector.scalar_tensor_tensor(y[:, :], pp[:, 2, :], bias[:, 2:3], h_[:, :], ALU.add, ALU.mult))
                    link(nc.vector.tensor_scalar(w[:, 0:1], w[:, 0:1], 1.0, None, ALU.mult))
                    for half in range(2):
                        dve.wait_ge(outs, 2 * g + half + 1)
                        back.dve(dve, g + half * GH, po[:, half, :].rearrange("p (k c) -> p k c", k=TPC), y=False,
                                 turn=2 * g + half)
                        dve.sem_inc(added, 1)


def store(nc, env, out):
    with ExitStack() as ctx:
        stored = ctx.enter_context(nc.semaphore("stored"))
        block = ctx.enter_context(nc.Block())

        @block.sync
        def _(sp):
            sp.dma_start(out.rearrange("b (s p) c -> p (b s) c", p=P), env.X[:, :, :]).then_inc(stored, 16)
            sp.wait_ge(stored, 16)


STAGES = ("mamba", "experts", "attention", "experts", "rotary", "product_keys", "state_space", "product_keys")


def hybrid(nc, args, out, stages=STAGES):
    Lent.handles = []
    env = Env()
    nb = args["L0_attn_a_x"].shape[0]
    env.NT = nb * SEQ // P
    env.NC = env.NT // TPC
    with ExitStack() as ctx:
        sb, ps, sem = scope(nc, ctx, "g")
        env.X = sb("X", [P, env.NT, P])
        env.stats = sb("stats", [P, env.NT, 6])
        env.mean, env.rstd = sb("mean", [P, env.NT]), sb("rstd", [P, env.NT])
        env.keep, env.shift = sb("keep", [P, env.NT]), sb("shift", [P, env.NT])
        env.root, env.rnorm = sb("root", [P, env.NT]), sb("rnorm", [P, env.NT])
        env.ident = sb("ident", [P, P])
        env.sel = sb("sel", [96, 32, P], BF16)
        env.ranks = sb("ranks", [P, 2, P], BF16)
        env.steps = sb("steps", [P, 2, 40])
        env.sorted_rows = nc.dram_tensor("sorted_rows", ((env.NT + 8) * P, P), F32, kind="Internal").ap()
        env.sorted_out = nc.dram_tensor("sorted_out", ((env.NT + 8) * P, P), F32, kind="Internal").ap()
        env.sorted_rows_written = False
        env.firsts = sb("firsts", [P, TPC, 8])
        env.identb = sb("identb", [P, P], BF16)
        env.causal = sb("causal", [P, P], BF16)
        env.causalT = sb("causalT", [P, P], BF16)
        turn_weights(nc, env, "const", [(env.causalT[:, :], args["c_causalT"]), 
                      (env.identb[:, :], args["c_identb"]), (env.causal[:, :], args["c_causal"]),
                      (env.ident[:, :], args["c_ident"]), (env.sel[:, :, :], args["c_sel"]),
                      (env.ranks[:, :, :], args["c_ranks"]), (env.steps[:, :, :], args["c_steps"]), (env.firsts[:, :, :], args["c_firsts"])], [])
        first_stats(nc, env, args["L0_attn_a_x"])
        def of(prefix):
            return {k[len(prefix):]: v for k, v in args.items() if k.startswith(prefix)}

        for i, s in enumerate(stages):
            if s == "attention":
                attention(nc, env, of("L0_attn_b_"), f"b{i}")
            if s == "rotary":
                rotary(nc, env, dict(of("L1_attn_a_"), rope=args["c_rope"], three=args["c_three"]), f"r{i}")
            if s == "state_space":
                state_space(nc, env, of("L1_attn_b_"), f"s{i}")
            if s == "product_keys":
                product_keys(nc, env, of("L1_ffn_"), f"k{i}")
            if s == "experts":
                experts(nc, env, of("L0_ffn_"), f"e{i}")
            if s == "mamba":
                mamba(nc, env, of("L0_attn_a_"))
            sweep(nc)
        store(nc, env, out)


def shape_constants():
    bf = mybir.dt.np(BF16)
    sel = np.zeros((96, 32, P), bf)
    for part in range(3):
        for s in range(32):
            sel[32 * part + s, s, :] = 1
    ranks = np.ones((P, 2, P), bf)
    ranks[:, 0, :] = np.triu(np.ones((P, P)), 1).astype(bf)
    steps = np.tile(np.stack([np.arange(40) * P, np.arange(40)]).astype(np.float32), (P, 1, 1))
    firsts = np.tile(np.arange(8, 0, -1, dtype=np.float32), (P, TPC, 1))
    causal = np.where(np.arange(P)[None, :] > np.arange(P)[:, None], np.float32(-1e30), np.float32(0)).astype(bf)
    three = np.zeros((P, 16, P), bf)
    for half in range(2):
        for part in range(3):
            for h in range(16):
                three[64 * half + 16 * part + h, h, :] = 1
    inv = (np.float32(1.0) / np.power(np.float32(10000.0), np.arange(0, 8, 2, dtype=np.float32) / np.float32(8)))
    freqs = (np.arange(SEQ, dtype=np.float32)[:, None] * inv[None, :].astype(np.float32)).astype(np.float32)
    cos, sin = np.cos(freqs), np.sin(freqs)
    one = np.stack([np.concatenate([cos, cos], 1), np.concatenate([-sin, sin], 1)], 1)
    rope = np.tile(one, (1, 1, 16)).reshape(2, P, 2, P).transpose(1, 0, 2, 3)
    return {"c_three": three, "c_rope": np.ascontiguousarray(rope.astype(np.float32)), "c_causalT": np.ascontiguousarray(causal.T), "c_identb": np.eye(P, dtype=bf), "c_causal": causal, "c_ranks": ranks, "c_steps": steps, "c_firsts": firsts, "c_ident": np.eye(P, dtype=np.float32), "c_sel": sel}


def hybrid_layers_kernel(nc, *operands):
    hybrid(nc, dict(zip(_INS + _TABLES, operands[:-1])), operands[-1])


_INS = ['L0_attn_a_x', 'L0_attn_a_norm_g', 'L0_attn_a_norm_b', 'L0_attn_a_in_w', 'L0_attn_a_conv_w',
        'L0_attn_a_conv_b', 'L0_attn_a_xproj_w', 'L0_attn_a_dt_w', 'L0_attn_a_dt_b', 'L0_attn_a_A_log',
        'L0_attn_a_D', 'L0_attn_a_out_w', 'L0_attn_b_gamma', 'L0_attn_b_w_qkv', 'L0_attn_b_w_out',
        'L0_ffn_centroids', 'L0_ffn_gamma', 'L0_ffn_beta', 'L0_ffn_W1', 'L0_ffn_b1', 'L0_ffn_W2',
        'L0_ffn_b2', 'L1_attn_a_W_kqv', 'L1_attn_a_W_proj', 'L1_attn_a_q_norm_w', 'L1_attn_a_k_norm_w',
        'L1_attn_b_conv_w', 'L1_attn_b_conv_b', 'L1_attn_b_in_proj_w', 'L1_attn_b_in_proj_b',
        'L1_attn_b_A_log', 'L1_attn_b_out_proj_w', 'L1_attn_b_out_proj_b', 'L1_ffn_w_q', 'L1_ffn_keys',
        'L1_ffn_expert_down', 'L1_ffn_expert_up', 'L1_ffn_norm_w']
_TABLES = ['c_ident', 'c_identb', 'c_sel', 'c_ranks', 'c_steps', 'c_three', 'c_firsts', 'c_causal', 'c_causalT', 'c_rope']
_OUTS = [((16, 256, 128), 'float32')]


def kernel(**inputs):
    import numpy as _np
    import concourse.bacc as _bacc
    from concourse import mybir as _mybir
    from concourse.bass_utils import run_bass_kernel_spmd as _run

    nc = _bacc.Bacc("TRN2", target_bir_lowering=False, num_devices=1)
    tables = shape_constants()
    arrays, args = {}, []
    for name in _INS + _TABLES:
        a = _np.ascontiguousarray(inputs[name] if name in inputs else tables[name])
        arrays[f"in_{name}_dram"] = a
        args.append(nc.dram_tensor(f"in_{name}_dram", a.shape, _mybir.dt.from_np(a.dtype), kind="ExternalInput").ap())
    for i, (shape, dtype) in enumerate(_OUTS):
        dt = _mybir.dt.from_np(_np.dtype(dtype))
        args.append(nc.dram_tensor(f"out_{i}_dram", shape, dt, kind="ExternalOutput").ap())
    hybrid_layers_kernel(nc, *args)
    r = _run(nc, [arrays], core_ids=[0])
    got = tuple(r.results[0][f"out_{i}_dram"] for i in range(len(_OUTS)))
    return got[0]
```

```python
from contextlib import ExitStack

import numpy as np

import concourse.bass as bass
from concourse import mybir

P = 128
TPC = 4
CH = TPC * P
SEQ = 256
SPC = CH // SEQ

F32 = mybir.dt.float32
BF16 = mybir.dt.bfloat16
I32 = mybir.dt.int32
ALU = mybir.AluOpType
ACT = mybir.ActivationFunctionType
AX = mybir.AxisListType.X


class Env:
    pass


class Lent:
    handles = []


def sweep(nc):
    nc.clear_and_free_semaphores(Lent.handles)
    Lent.handles = []
    nc.all_engine_barrier()


class Link:

    def __init__(self, eng, sem, base=0):
        self.eng, self.sem, self.base, self.n = eng, sem, base, 0

    def __call__(self, ins):
        ins.then_inc(self.sem, 1)
        self.n += 1
        self.eng.wait_ge(self.sem, self.base + self.n)

    def inc(self, ins):
        ins.then_inc(self.sem, 1)
        self.n += 1

    def wait(self, back=0):
        self.eng.wait_ge(self.sem, self.base + self.n - back)


def hold(eng, sem, value):
    if not (isinstance(value, int) and value <= 0):
        eng.wait_ge(sem, value)
        eng.nop(nofuse=True)


def need(eng, sem, value):
    if not (isinstance(value, int) and value <= 0):
        eng.wait_ge(sem, value)


def rounds(eng, count, body):
    body(0, True, count == 1)
    if count > 2:
        with eng.Fori(1, count - 1) as it:
            body(it, False, False)
    if count > 1:
        body(count - 1, False, True)


def scope(nc, ctx, tag):
    def sb(name, shape, dt=F32):
        return ctx.enter_context(nc.sbuf_tensor(f"{tag}_{name}", shape, dt))

    def ps(name, shape, dt=F32):
        return ctx.enter_context(nc.psum_tensor(f"{tag}_{name}", shape, dt))

    def sem(name):
        handle = nc.alloc_semaphore(name=f"{tag}_{name}")
        Lent.handles.append(handle)
        return handle

    return sb, ps, sem


def turn_weights(nc, tag, ident, turns):
    BANKS = 8
    with ExitStack() as ctx:
        _, ps, sem = scope(nc, ctx, tag)
        turned = ps("turned", [P, BANKS, 512])
        placed = sem("placed")
        evacuated = (sem("evacuated_dve"), sem("evacuated_act"))
        block = ctx.enter_context(nc.Block())

        @block.tensor
        def _(pe):
            for j, (src, dst) in enumerate(turns):
                p, f = src.shape[0], dst.shape[0]
                if j >= BANKS:
                    pe.wait_ge(evacuated[j % 2], (j - BANKS) // 2 + 1)
                nc.tensor.transpose(turned[0:f, j % BANKS, 0:p], src, ident[0:p, 0:p]).then_inc(placed, 1)

        def evacuate(eng, copy, z):
            for j, (src, dst) in enumerate(turns):
                if j % 2 == z:
                    eng.wait_ge(placed, j + 1)
                    copy(dst, turned[0:dst.shape[0], j % BANKS, 0:src.shape[0]]).then_inc(evacuated[z], 1)
            if len(turns) > z:
                eng.wait_ge(evacuated[z], (len(turns) + 1 - z) // 2)

        @block.vector
        def _(dve):
            evacuate(dve, nc.vector.tensor_copy, 0)

        @block.scalar
        def _(act):
            evacuate(act, nc.scalar.copy, 1)


def row_scales(nc, env, tag, second, loads=(), later=None):
    NT = env.NT
    with ExitStack() as ctx:
        sb, _, sem = scope(nc, ctx, tag)
        tmp = sb("tmp", [P, 5, NT])
        rooted, vec, loaded = sem("rooted"), sem("vec"), sem("loaded")
        block = ctx.enter_context(nc.Block())

        @block.sync
        def _(sp):
            for dst, src in loads:
                sp.dma_start(dst, src, allow_slow_non_contiguous=True).then_inc(loaded, 16)
            if later:
                for dst, src in later[1]:
                    sp.dma_start(dst, src, allow_slow_non_contiguous=True).then_inc(later[0], 16)
            if loads:
                sp.wait_ge(loaded, 16 * len(loads))

        st, t0, t1, t2, t3, t4 = env.stats, tmp[:, 0, :], tmp[:, 1, :], tmp[:, 2, :], tmp[:, 3, :], tmp[:, 4, :]

        @block.vector
        def _(dve):
            link = Link(dve, vec)
            link.inc(nc.vector.tensor_tensor(t0, st[:, :, 1], st[:, :, 4], ALU.add))
            link.inc(nc.vector.tensor_tensor(t1, st[:, :, 1], st[:, :, 4], ALU.subtract))
            link.inc(nc.vector.tensor_tensor(t2, st[:, :, 2], st[:, :, 5], ALU.add))
            link.wait()
            link.inc(nc.vector.tensor_scalar(env.mean[:, :], t0, 0.5, None, ALU.mult))
            link(nc.vector.scalar_tensor_tensor(t3, t1, 0.25, t1, ALU.mult, ALU.mult))
            link(nc.vector.scalar_tensor_tensor(t0, t2, 1.0 / P, t3, ALU.mult, ALU.add))
            link(nc.vector.tensor_scalar(t1, t0, 1e-5, None, ALU.add))
            dve.wait_ge(rooted, 1)
            link(nc.vector.reciprocal(env.rstd[:, :], t2))
            link.inc(nc.vector.tensor_scalar(env.keep[:, :], env.rstd[:, :], 1.0, None, ALU.add))
            link(nc.vector.scalar_tensor_tensor(env.shift[:, :], env.mean[:, :], -1.0, env.rstd[:, :],
                                                ALU.mult, ALU.mult))
            if second:
                k, eps, floor, gain = second
                link(nc.vector.tensor_tensor(t1, t0, env.rstd[:, :], ALU.mult))
                link(nc.vector.tensor_tensor(t3, t1, env.rstd[:, :], ALU.mult))
                link(nc.vector.tensor_scalar(t1, t3, float(k), float(eps), ALU.mult, ALU.add))
                dve.wait_ge(rooted, 2)
                link(nc.vector.tensor_scalar(t4, t2, float(floor), None, ALU.max))
                link(nc.vector.reciprocal(t3, t4))
                link.inc(nc.vector.tensor_scalar(env.root[:, :], t4, 1.0 / gain, None, ALU.mult))
                link(nc.vector.scalar_tensor_tensor(env.rnorm[:, :], t3, float(gain), env.rstd[:, :],
                                                    ALU.mult, ALU.mult))

        @block.scalar
        def _(act):
            act.wait_ge(vec, 7)
            nc.scalar.activation(t2, t1, ACT.Sqrt).then_inc(rooted, 1)
            if second:
                act.wait_ge(vec, 13)
                nc.scalar.activation(t2, t1, ACT.Sqrt).then_inc(rooted, 1)
            act.wait_ge(rooted, 2 if second else 1)


def launch(nc, env, x_dram, tables):
    NT, PARTS = env.NT, 8
    G = NT // PARTS
    with ExitStack() as ctx:
        _, _, sem = scope(nc, ctx, "first")
        loaded = [sem(f"loaded{q}") for q in range(PARTS)]
        tabled, done = sem("tabled"), sem("done")
        block = ctx.enter_context(nc.Block())
        rows = x_dram.rearrange("b (s p) c -> p (b s) c", p=P)

        @block.sync
        def _(sp):
            for q in range(PARTS):
                sp.dma_start(env.X[:, q * G:(q + 1) * G, :], rows[:, q * G:(q + 1) * G, :]).then_inc(loaded[q], 16)

        @block.scalar
        def _(act):
            for dst, src in tables:
                act.dma_start(dst, src).then_inc(tabled, 16)
            act.wait_ge(tabled, 16 * len(tables))

        @block.vector
        def _(dve):
            for q in range(PARTS):
                dve.wait_ge(loaded[q], 16)
                for i in range(q * G, (q + 1) * G):
                    nc.vector.bn_stats(env.stats[:, i, :], env.X[:, i, :]).then_inc(done, 1)
            dve.wait_ge(done, NT)


class Front:

    def __init__(self, nc, env, sb, ps, sem, inner, out, banks=1):
        self.nc, self.env, self.inner, self.out, self.banks = nc, env, inner, out, banks
        self.rows = sb("rows", [P, 2, TPC, P])
        self.tp = ps("front", [P, banks, 512])
        self.normed, self.turned, self.written = sem("normed"), sem("turned"), sem("written")

    def dve(self, eng, n, p):
        e, nc = self.env, self.nc
        eng.wait_ge(self.turned, n + 1)
        r = e.rnorm if self.inner else e.rstd
        for k in range(TPC):
            t = n * TPC + k
            ins = nc.vector.tensor_scalar(self.rows[:, p, k, :], e.X[:, t, :], e.mean[:, bass.ds(t, 1)],
                                          r[:, bass.ds(t, 1)], ALU.subtract, ALU.mult)
        ins.then_inc(self.normed, 1)

    def credit(self, pe):
        pe.sem_inc(self.turned, 2)

    def credit_act(self, act):
        act.sem_inc(self.written, self.banks)

    def pe(self, eng, n, p):
        eng.wait_ge(self.normed, n + 1)
        eng.wait_ge(self.written, n + 1)
        for k in range(TPC):
            ins = self.nc.tensor.transpose(self.tp[:, p % self.banks, k * P:(k + 1) * P],
                                           self.rows[:, p, k, :], self.env.ident[:, :])
        ins.then_inc(self.turned, 1)

    def act(self, eng, n, p):
        eng.wait_ge(self.turned, n + 3)
        self.nc.scalar.copy(self.out(p), self.tp[:, p % self.banks, :]).then_inc(self.written, 1)

    def wait(self, eng, n):
        eng.wait_ge(self.written, n + 1 + self.banks)


class Back:

    def __init__(self, nc, env, sb, ps, sem, tiles=TPC, y=False):
        self.nc, self.env, self.tiles, self.y = nc, env, tiles, y
        self.kept = sb("kept", [P, tiles, P]) if y else None
        self.chain = sem("back")
        self.steps = 3 if y else 2

    def dve(self, eng, n, out, gain=None, turn=None):
        e, nc, G, kept = self.env, self.nc, self.tiles, self.kept
        chain = Link(eng, self.chain, self.steps * (n if turn is None else turn))
        if self.y:
            for k in range(G):
                t = n * G + k
                ins = nc.vector.tensor_scalar(kept[:, k, :], e.X[:, t, :], e.keep[:, bass.ds(t, 1)],
                                              e.shift[:, bass.ds(t, 1)], ALU.mult, ALU.add)
            chain(ins)
        if gain is None:
            dst = e.X[:, bass.ds(n * G, G), :]
            ins = nc.vector.tensor_tensor(dst, kept[:, :, :] if self.y else dst, out, ALU.add)
        else:
            for k in range(G):
                t = n * G + k
                dst = e.X[:, t, :]
                ins = nc.vector.scalar_tensor_tensor(dst, out[:, k, :], gain[:, bass.ds(t, 1)],
                                                     kept[:, k, :] if self.y else dst, ALU.mult, ALU.add)
        chain(ins)
        for k in range(G):
            t = n * G + k
            ins = nc.vector.bn_stats(e.stats[:, t, :], e.X[:, t, :])
        chain(ins)


def mamba(nc, env, a):
    NC_, T = env.NC, env.NT * P
    DI, DS, DTR, TAPS = 256, 16, 64, 4
    H = DI // P
    with ExitStack() as outer:
        sb, ps, sem = scope(nc, outer, "m")
        outT = sb("outT", [P, H, P])
        A = sb("A", [P, H, DS])
        convb, dtb, Dd = sb("convb", [P, H]), sb("dtb", [P, H]), sb("Dd", [P, H])
        g, b = sb("g", [P, 1]), sb("b", [P, 1])
        diagD = sb("diagD", [P, H, P])
        u = sb("u", [P, H, T])
        sz = sb("sz", [P, H, T])
        delta = sb("delta", [P, H, T])
        du = sb("du", [P, H, T])
        bc = sb("bc", [96, T], BF16)
        projections = ExitStack()
        sb, _, _ = scope(nc, projections, "mw")
        wconv = sb("wconv", [P, TAPS, DI])
        wz = sb("wz", [P, DI])
        xprojT = sb("xprojT", [P, H, DTR + 2 * DS])
        dtT = sb("dtT", [DTR, DI])
        with ExitStack() as prep:
            psb, _, psem = scope(nc, prep, "mp")
            in_w = psb("in_w", [P, 4, P])
            scaled = psb("scaled", [P, TAPS, H, P])
            cw = psb("cw", [P, H, TAPS])
            xp = psb("xp", [DTR + 2 * DS, DI])
            dtw = psb("dtw", [P, H, DTR])
            ow = psb("ow", [P, DI])
            row_scales(nc, env, "m_sc", (1.0, 1e-5, 0.0, 1.0), [
                (in_w[:, :, :], a["in_w"].rearrange("(j p) c -> p j c", p=P)),
                (cw[:, :, :], a["conv_w"].rearrange("(h p) o k -> p h (o k)", p=P)),
                (xp[:, :], a["xproj_w"]),
                (dtw[:, :, :], a["dt_w"].rearrange("(h p) r -> p h r", p=P)),
                (ow[:, :], a["out_w"]),
                (A[:, :, :], a["A_log"].rearrange("(h p) s -> p h s", p=P)),
                (convb[:, :], a["conv_b"].rearrange("(h p) -> p h", p=P)),
                (dtb[:, :], a["dt_b"].rearrange("(h p) -> p h", p=P)),
                (Dd[:, :], a["D"].rearrange("(h p) -> p h", p=P)),
                (g[:, :], a["norm_g"].rearrange("(p o) -> p o", o=1)),
                (b[:, :], a["norm_b"].rearrange("(p o) -> p o", o=1))])
            mt, ma_ = psem("mt"), psem("ma")
            with nc.Block() as block:
                @block.vector
                def _(dve):
                    for k in range(TAPS):
                        for h in range(H):
                            nc.vector.tensor_scalar(scaled[:, k, h, :], in_w[:, h, :], cw[:, h, k:k + 1], None,
                                                    ALU.mult).then_inc(mt, 1)
                    for h in range(H):
                        nc.vector.tensor_scalar(diagD[:, h, :], env.ident[:, :], Dd[:, h:h + 1], None,
                                                ALU.mult).then_inc(mt, 1)
                    dve.wait_ge(mt, 10)

                @block.scalar
                def _(act):
                    nc.scalar.activation(A[:, :, :], A[:, :, :], ACT.Exp).then_inc(ma_, 1)
                    act.wait_ge(ma_, 1)
                    nc.scalar.mul(A[:, :, :], A[:, :, :], -1.0).then_inc(ma_, 1)
                    act.wait_ge(ma_, 2)
            turn_weights(nc, "m_t", env.ident,
                         [(scaled[:, k, h, :], wconv[:, k, h * P:(h + 1) * P]) for k in range(TAPS) for h in range(H)]
                         + [(in_w[:, 2 + h, :], wz[:, h * P:(h + 1) * P]) for h in range(H)]
                         + [(xp[:, h * P:(h + 1) * P], xprojT[:, h, :]) for h in range(H)]
                         + [(dtw[:, h, :], dtT[:, h * P:(h + 1) * P]) for h in range(H)]
                         + [(ow[:, h * P:(h + 1) * P], outT[:, h, :]) for h in range(H)])

        with ExitStack() as ctx:
            sb, ps, sem = scope(nc, ctx, "ma")
            PAD = TAPS - 1
            zc = sb("zc", [P, 2, SPC, PAD + SEQ])
            dr = sb("dr", [DTR, CH])
            bcf = sb("bcf", [2 * DS, 2, CH])
            pj = ps("pj", [P, 4, 512])
            pd = ps("pd", [P, 3, 512])
            padded, proj, gated, small, draw_, drd, split, entered = (sem(x) for x in (
                "padded", "proj", "gated", "small", "dtraw", "drd", "split", "entered"))
            front = Front(nc, env, sb, ps, sem, True, None)
            block = ctx.enter_context(nc.Block())

            def chunks(eng, now, ahead=None, behind=None):
                def body(it, first, last):
                    for p in range(2):
                        n = it * 2 + p
                        if ahead and not (last and p):
                            ahead(n + 1, 1 - p)
                        now(n, p)
                        if behind and not (first and p == 0):
                            behind(n - 1, 1 - p)

                if ahead:
                    ahead(0, 0)
                rounds(eng, NC_ // 2, body)
                if behind:
                    behind(NC_ - 1, 1)

            @block.gpsimd
            def _(pool):
                nc.gpsimd.memset(zc[:, :, :, 0:PAD], 0.0).then_inc(padded, 1)

            @block.vector
            def _(dve):
                def enter(n, p):
                    need(dve, front.turned, n + 3)
                    need(dve, proj, 4 * (n - 1))
                    nc.vector.tensor_scalar(zc[:, p, :, PAD:PAD + SEQ],
                                            front.tp[:, 0, :].rearrange("p (s t) -> p s t", s=SPC),
                                            g[:, 0:1], b[:, 0:1], ALU.mult, ALU.add).then_inc(entered, 1)

                def steps(n, p):
                    cols = bass.ds(n * CH, CH)
                    need(dve, small, 2 * n + 2)
                    link = Link(dve, split, n * 5)
                    link(nc.vector.tensor_copy(bc[0:32, cols], bcf[:, 0, :]))
                    link(nc.vector.tensor_tensor(bcf[:, 1, :], bcf[:, 0, :], bc[0:32, cols], ALU.subtract))
                    link(nc.vector.tensor_copy(bc[32:64, cols], bcf[:, 1, :]))
                    link(nc.vector.tensor_tensor(bcf[:, 0, :], bcf[:, 1, :], bc[32:64, cols], ALU.subtract))
                    link(nc.vector.tensor_copy(bc[64:96, cols], bcf[:, 0, :]))
                    for h in range(H):
                        need(dve, draw_, 3 * n + 2 + h)
                        nc.vector.tensor_scalar(delta[:, h, cols], pd[:, 1 + h, :], dtb[:, h:h + 1], None,
                                                ALU.add).then_inc(drd, 1)

                def body(it, first, last):
                    for p in range(2):
                        n = it * 2 + p
                        if not last:
                            front.dve(dve, n + 2, p)
                        if not (last and p):
                            enter(n + 1, 1 - p)
                        if not (first and p == 0):
                            steps(n - 1, 1 - p)

                front.dve(dve, 0, 0)
                front.dve(dve, 1, 1)
                enter(0, 0)
                rounds(dve, NC_ // 2, body)
                steps(NC_ - 1, 1)

            @block.tensor
            def _(pe):
                def turn(n, p):
                    need(pe, front.normed, n + 1)
                    need(pe, entered, n)
                    for k in range(TPC):
                        ins = nc.tensor.transpose(front.tp[:, 0, k * P:(k + 1) * P], front.rows[:, p, k, :], env.ident[:, :])
                    ins.then_inc(front.turned, 1)

                def convolve(n, p):
                    need(pe, entered, n + 1)
                    for h in range(H):
                        need(pe, gated, 4 * (n - 1) + 1 + h)
                        for k in range(TAPS):
                            ins = nc.tensor.matmul(pj[:, h, :], wconv[:, k, h * P:(h + 1) * P],
                                                   zc[:, p, :, k:k + SEQ], start=(k == 0), stop=(k == TAPS - 1))
                        ins.then_inc(proj, 1)
                    for h in range(H):
                        need(pe, gated, 4 * (n - 1) + 3 + h)
                        nc.tensor.matmul(pj[:, 2 + h, :], wz[:, h * P:(h + 1) * P],
                                         zc[:, p, :, PAD:PAD + SEQ], start=True, stop=True).then_inc(proj, 1)

                def steps(n, p):
                    need(pe, small, 2 * n)
                    hold(pe, gated, 4 * n + 2)
                    for h in range(H):
                        ins = nc.tensor.matmul(pd[0:96, 0, :], xprojT[:, h, :], u[:, h, bass.ds(n * CH, CH)],
                                               start=(h == 0), stop=(h == H - 1))
                    ins.then_inc(draw_, 1)
                    need(pe, small, 2 * n + 1)
                    for h in range(H):
                        need(pe, drd, 2 * (n - 1) + h + 1)
                        nc.tensor.matmul(pd[:, 1 + h, :], dtT[:, h * P:(h + 1) * P], dr[:, :],
                                         start=True, stop=True).then_inc(draw_, 1)

                front.credit(pe)
                pe.wait_ge(padded, 1)
                chunks(pe, convolve, ahead=turn, behind=steps)

            @block.scalar
            def _(act):
                def gates(n, p):
                    cols = bass.ds(n * CH, CH)
                    for h in range(H):
                        hold(act, proj, 4 * n + 1 + h)
                        nc.scalar.activation(u[:, h, cols], pj[:, h, :], ACT.Silu,
                                             bias=convb[:, h:h + 1]).then_inc(gated, 1)
                    for h in range(H):
                        hold(act, proj, 4 * n + 3 + h)
                        nc.scalar.activation(sz[:, h, cols], pj[:, 2 + h, :], ACT.Silu).then_inc(gated, 1)

                def steps(n, p):
                    need(act, draw_, 3 * n + 1)
                    nc.scalar.copy(dr[:, :], pd[0:DTR, 0, :]).then_inc(small, 1)
                    need(act, split, 5 * n)
                    nc.scalar.copy(bcf[:, 0, :], pd[DTR:DTR + 2 * DS, 0, :]).then_inc(small, 1)

                chunks(act, gates, behind=steps)

        projections.close()

        with ExitStack() as ctx:
            sb, ps, sem = scope(nc, ctx, "mb")
            e = sb("e", [P, 2, H, CH])
            l = sb("l", [P, 2, H, CH])
            w = sb("w", [P, 2, H, CH])
            logs, vec, rest, done = sem("logs"), sem("vec"), sem("rest"), sem("done")
            block = ctx.enter_context(nc.Block())

            @block.scalar
            def _(act):
                def body(it, first, last):
                    link = Link(act, logs, 6 * it)
                    for p in range(2):
                        n = it * 2 + p
                        hold(act, vec, 3 * (n - 1))
                        link(nc.scalar.activation(l[:, p, :, :], delta[:, :, bass.ds(n * CH, CH)], ACT.Abs))
                        link(nc.scalar.activation(e[:, p, :, :], l[:, p, :, :], ACT.Exp, scale=-1.0))
                    for p in range(2):
                        link(nc.scalar.activation(l[:, p, :, :], e[:, p, :, :], ACT.Ln, bias=1.0))

                rounds(act, NC_ // 2, body)

            @block.gpsimd
            def _(pool):
                def body(it, first, last):
                    for p in range(2):
                        n = it * 2 + p
                        cols = bass.ds(n * CH, CH)
                        need(pool, vec, 3 * n + 1)
                        nc.gpsimd.tensor_tensor(w[:, p, :, :], e[:, p, :, :], w[:, p, :, :], ALU.subtract).then_inc(rest, 1)
                        hold(pool, vec, 3 * n + 3)
                        nc.gpsimd.tensor_tensor(du[:, :, cols], delta[:, :, cols], u[:, :, cols], ALU.mult).then_inc(done, 1)

                rounds(pool, NC_ // 2, body)
                pool.wait_ge(done, NC_)

            @block.vector
            def _(dve):
                def body(it, first, last):
                    for p in range(2):
                        n = it * 2 + p
                        d = delta[:, :, bass.ds(n * CH, CH)]
                        need(dve, logs, 6 * it + 2 * p + 2)
                        nc.vector.tensor_scalar(w[:, p, :, :], e[:, p, :, :], 1.0, -1.0, ALU.add, ALU.add).then_inc(vec, 1)
                        need(dve, logs, 6 * it + 5 + p)
                        nc.vector.scalar_tensor_tensor(l[:, p, :, :], d, 0.0, l[:, p, :, :], ALU.max, ALU.add).then_inc(vec, 1)
                        need(dve, vec, 3 * n + 2)
                        need(dve, rest, n + 1)
                        nc.vector.tensor_tensor(d, l[:, p, :, :], w[:, p, :, :], ALU.add).then_inc(vec, 1)

                rounds(dve, NC_ // 2, body)

        with ExitStack() as ctx:
            sb, ps, sem = scope(nc, ctx, "mc")
            RD, RB, RH, LAG = 2, 4, 8, 3
            dA = sb("dA", [P, RD, SPC, SEQ])
            h_ = sb("h", [P, RB, CH])
            cs = sb("cs", [P, 2, CH])
            hc = sb("hc", [P, RH, CH])
            Bp, Cp = ps("B", [P, 2, 512]), ps("C", [P, 2, 512])
            RI = 4
            dbu = sb("dbu", [P, RI, CH])
            yp = ps("y", [P, H, 512])
            zeroed, bcast, cdone, decay, inject, scanned, outs, summed, y_out, moved = (sem(x) for x in (
                "zeroed", "bcast", "cdone", "decay", "inject", "scanned", "outs", "summed", "yout", "moved"))
            block = ctx.enter_context(nc.Block())
            Q = DS * H

            @block.tensor
            def _(pe):
                def spread(n, s):
                    g = n * DS + s
                    cols = bass.ds(n * CH, CH)
                    need(pe, inject, H * (g - 1))
                    need(pe, cdone, g - 1)
                    nc.tensor.matmul(Bp[:, s % 2, :], env.sel[:, s, :], bc[:, cols], start=True, stop=True)
                    nc.tensor.matmul(Cp[:, s % 2, :], env.sel[:, DS + s, :], bc[:, cols],
                                     start=True, stop=True).then_inc(bcast, 1)

                def sum_up(n, s):
                    for h in range(H):
                        q = s * H + h
                        need(pe, outs, n * Q + q + 1)
                        if s == 0:
                            need(pe, y_out, H * n)
                        nc.tensor.matmul(yp[:, h, :], env.ident[:, :], hc[:, q % RH, :], start=(s == 0), stop=False,
                                         ).then_inc(summed, 1)
                    if s == DS - 1:
                        for h in range(H):
                            nc.tensor.matmul(yp[:, h, :], diagD[:, h, :], u[:, h, bass.ds(n * CH, CH)], start=False,
                                             stop=True).then_inc(moved, 1)

                def body(n, first, last):
                    for s in range(DS):
                        spread(n, s)
                        if s >= LAG:
                            sum_up(n, s - LAG)
                        elif not first:
                            sum_up(n - 1, s - LAG + DS)

                rounds(pe, NC_, body)
                for s in range(DS - LAG, DS):
                    sum_up(NC_ - 1, s)

            @block.scalar
            def _(act):
                act.wait_ge(zeroed, 1)

                def body(n, first, last):
                    for s in range(DS):
                        for h in range(H):
                            q = s * H + h
                            hold(act, scanned, n * Q + q + 1 - RD)
                            d = delta[:, h, bass.ds(n * CH, CH)].rearrange("p (s t) -> p s t", s=SPC)
                            nc.scalar.activation(dA[:, q % RD, :, 1:SEQ], d[:, :, 1:SEQ], ACT.Exp,
                                                 scale=A[:, h, s:s + 1]).then_inc(decay, 1)
                        need(act, bcast, n * DS + s + 1)
                        need(act, outs, H * (n * DS + s - 1))
                        nc.scalar.copy(cs[:, s % 2, :], Cp[:, s % 2, :]).then_inc(cdone, 1)

                rounds(act, NC_, body)

            @block.vector
            def _(dve):
                def bring(n, q):
                    s, h = q // H, q % H
                    need(dve, bcast, n * DS + s + 1)
                    need(dve, scanned, n * Q + q + 1 - RI)
                    nc.vector.tensor_tensor(dbu[:, q % RI, :], du[:, h, bass.ds(n * CH, CH)], Bp[:, s % 2, :],
                                            ALU.mult).then_inc(inject, 1)

                def gate(n):
                    for h in range(H):
                        need(dve, moved, H * n + 1 + h)
                        z = sz[:, h, bass.ds(n * CH, CH)]
                        nc.vector.tensor_tensor(z, z, yp[:, h, :], ALU.mult).then_inc(y_out, 1)

                def body(n, first, last):
                    for q in range(Q):
                        if q + 1 < Q:
                            bring(n, q + 1)
                        elif not last:
                            bring(n + 1, 0)
                        if q == LAG * H and not first:
                            gate(n - 1)
                        need(dve, inject, n * Q + q + 1)
                        need(dve, decay, n * Q + q + 1)
                        need(dve, outs, n * Q + q + 1 - RB)
                        nc.vector.tensor_tensor_scan(h_[:, q % RB, :], dA[:, q % RD, :, :].rearrange("p s t -> p (s t)"),
                                                     dbu[:, q % RI, :], 0.0, ALU.mult, ALU.add).then_inc(scanned, 1)

                bring(0, 0)
                rounds(dve, NC_, body)
                gate(NC_ - 1)

            @block.gpsimd
            def _(pool):
                nc.gpsimd.memset(dA[:, :, :, 0:1], 0.0).then_inc(zeroed, 1)

                def body(n, first, last):
                    for q in range(Q):
                        s = q // H
                        need(pool, scanned, n * Q + q + 1)
                        need(pool, cdone, n * DS + s + 1)
                        need(pool, summed, n * Q + q + 1 - RH)
                        nc.gpsimd.tensor_tensor(hc[:, q % RH, :], h_[:, q % RB, :], cs[:, s % 2, :],
                                                ALU.mult).then_inc(outs, 1)

                rounds(pool, NC_, body)

        channels_out(nc, env, "md", H, lambda h: outT[:, h, :], lambda h, n: sz[:, h, bass.ds(n * CH, CH)])


def channels_out(nc, env, tag, K, weight, act_of):
    with ExitStack() as ctx:
        sb, ps, sem = scope(nc, ctx, tag)
        po, pt = ps("po", [P, 2, 512]), ps("pt", [P, 2, 512])
        oT = sb("oT", [P, 2, CH])
        made, held, turned, added = sem("made"), sem("held"), sem("turned"), sem("added")
        back = Back(nc, env, sb, ps, sem, y=True)
        block = ctx.enter_context(nc.Block())

        @block.tensor
        def _(pe):
            with pe.Fori(0, env.NC // 2) as it:
                for p in range(2):
                    n = it * 2 + p
                    pe.wait_ge(held, n + 1)
                    for k in range(K):
                        ins = nc.tensor.matmul(po[:, p, :], weight(k), act_of(k, n), start=(k == 0), stop=(k == K - 1))
                    ins.then_inc(made, 1)
                    pe.wait_ge(held, n + 3)
                    pe.wait_ge(added, n + 1)
                    for k in range(TPC):
                        ins = nc.tensor.transpose(pt[:, p, k * P:(k + 1) * P], oT[:, p, k * P:(k + 1) * P], env.ident[:, :])
                    ins.then_inc(turned, 1)

        @block.scalar
        def _(act):
            act.sem_inc(held, 2)
            with act.Fori(0, env.NC // 2) as it:
                for p in range(2):
                    n = it * 2 + p
                    act.wait_ge(made, n + 1)
                    act.wait_ge(added, n + 1)
                    nc.scalar.copy(oT[:, p, :], po[:, p, :]).then_inc(held, 1)

        @block.vector
        def _(dve):
            dve.sem_inc(added, 2)
            with dve.Fori(0, env.NC // 2) as it:
                for p in range(2):
                    n = it * 2 + p
                    dve.wait_ge(turned, n + 1)
                    back.dve(dve, n, pt[:, p, :].rearrange("p (k c) -> p k c", k=TPC))
                    dve.sem_inc(added, 1)


def front_pass(nc, env, tag, inner, ZT, scale=None, bias=None):
    with ExitStack() as ctx:
        sb, ps, sem = scope(nc, ctx, tag)
        rows = sb("rows", [P, 2, TPC, P])
        tp = ps("tp", [P, 2, 512])
        normed, turned, written = sem("normed"), sem("turned"), sem("written")
        block = ctx.enter_context(nc.Block())
        r = env.rnorm if inner else env.rstd

        @block.vector
        def _(dve):
            with dve.Fori(0, env.NC // 2) as it:
                for p in range(2):
                    n = it * 2 + p
                    dve.wait_ge(turned, n + 1)
                    for k in range(TPC):
                        t = n * TPC + k
                        ins = nc.vector.tensor_scalar(rows[:, p, k, :], env.X[:, t, :], env.mean[:, bass.ds(t, 1)],
                                                      r[:, bass.ds(t, 1)], ALU.subtract, ALU.mult)
                    ins.then_inc(normed, 1)

        @block.tensor
        def _(pe):
            pe.sem_inc(turned, 2)
            with pe.Fori(0, env.NC // 2) as it:
                for p in range(2):
                    n = it * 2 + p
                    pe.wait_ge(written, n + 1)
                    pe.wait_ge(normed, n + 1)
                    for k in range(TPC):
                        ins = nc.tensor.transpose(tp[:, p, k * P:(k + 1) * P], rows[:, p, k, :], env.ident[:, :])
                    ins.then_inc(turned, 1)

        @block.scalar
        def _(act):
            act.sem_inc(written, 2)
            with act.Fori(0, env.NC // 2) as it:
                for p in range(2):
                    n = it * 2 + p
                    hold(act, turned, n + 3)
                    dst = ZT[:, bass.ds(n * CH, CH)]
                    kw = {k: v for k, v in (("scale", scale), ("bias", bias)) if v is not None}
                    if kw:
                        nc.scalar.activation(dst, tp[:, p, :], ACT.Identity, **kw).then_inc(written, 1)
                    else:
                        nc.scalar.copy(dst, tp[:, p, :]).then_inc(written, 1)


def experts(nc, env, a, tag):
    NT = env.NT
    E, F = 8, 512
    J = F // P
    NJ = (NT + E - 1 + 1) // 2 * 2
    with ExitStack() as outer:
        sb, _, sem = scope(nc, outer, tag)
        w1T = sb("w1T", [P, E, F])
        w2T = sb("w2T", [P, E, F])
        b1 = sb("b1", [P, E, J])
        b2 = sb("b2", [1, E, P])
        byexpert = sb("byexpert", [P, 3, E])
        centT, gT, bT = byexpert[:, 0, :], byexpert[:, 1, :], byexpert[:, 2, :]
        alpha = sb("alpha", [P, NT])
        ones = sb("ones", [1, P])
        slot = sb("slot", [P, NT], I32)
        expert = sb("expert", [P, NJ], I32)
        ZS = sb("ZS", [P, NJ, P])
        YS = sb("YS", [P, NJ, P])
        with ExitStack() as ctx:
            sb, ps, sem = scope(nc, ctx, tag + "p")
            w1, w2 = sb("w1", [P, E, J, P]), sb("w2", [P, E, F])
            hot = sb("hot", [P, NT, E], BF16)
            fetched = sem("fetched")
            weights = []
            for e in range(E):
                weights += [(w1[:, e, :, :], a["W1"][e].rearrange("(j p) c -> p j c", p=P)), (w2[:, e, :], a["W2"][e])]
            rows1, rows3 = sb("rows1", [E * J, P]), sb("rows3", [3 * E, P])
            row_scales(nc, env, tag + "sc", (1.0, 1e-5, 0.0, 1.0), [
                (rows1[:, :], a["b1"].rearrange("e (j p) -> (e j) p", p=P)),
                (b2[:, :, :], a["b2"].rearrange("(o e) c -> o e c", o=1)),
                (rows3[0:E, :], a["centroids"]), (rows3[E:2 * E, :], a["gamma"]), (rows3[2 * E:3 * E, :], a["beta"])],
                later=(fetched, weights))
            turn_weights(nc, tag + "t", env.ident, [(rows3[:, :], byexpert[:, :, :].rearrange("p a e -> p (a e)")),
                                                    (rows1[:, :], b1[:, :, :].rearrange("p e j -> p (e j)"))])
            choose(nc, env, tag, centT, hot, alpha)
            turns = []
            for e in range(E):
                turns += [(w1[:, e, j, :], w1T[:, e, j * P:(j + 1) * P]) for j in range(J)]
                turns += [(w2[:, e, j * P:(j + 1) * P], w2T[:, e, j * P:(j + 1) * P]) for j in range(J)]
            place(nc, env, tag, hot, slot, expert, ZS, YS, ones, NJ, (fetched, 16 * len(weights), turns, w1T, b1, gT, bT))
        sorted_experts(nc, env, tag, ZS, YS, w1T, w2T, b1, b2, ones, expert, NJ)
        collect(nc, env, tag, YS, slot, alpha, NJ)


def choose(nc, env, tag, centT, hot, alpha):
    NT, NC_ = env.NT, env.NC
    E = 8
    with ExitStack() as ctx:
        sb, ps, sem = scope(nc, ctx, tag + "r")
        zc = sb("zc", [P, 2, CH])
        sc, best = sb("sc", [P, NT, E]), sb("best", [P, NT, E])
        mx, m2, arg = sb("mx", [P, NT]), sb("m2", [P, NT]), sb("arg", [P, NT])
        psc = ps("psc", [P, NT, E])
        front = Front(nc, env, sb, ps, sem, True, lambda p: zc[:, p, :], banks=2)
        scored, vec, gated = sem("scored"), sem("vec"), sem("gated")
        block = ctx.enter_context(nc.Block())

        @block.tensor
        def _(pe):
            front.credit(pe)
            with pe.Fori(0, NC_ // 2) as it:
                for p in range(2):
                    front.pe(pe, it * 2 + p, p)
                for p in range(2):
                    n = it * 2 + p
                    front.wait(pe, n)
                    for k in range(TPC):
                        ins = nc.tensor.matmul(psc[:, n * TPC + k, :], zc[:, p, k * P:(k + 1) * P],
                                               centT, start=True, stop=True)
                    ins.then_inc(scored, 1)

        @block.scalar
        def _(act):
            front.credit_act(act)

            def body(it, first, last):
                for p in range(2):
                    n = it * 2 + p
                    need(act, scored, n - 1)
                    front.act(act, n, p)

            rounds(act, NC_ // 2, body)
            act.wait_ge(vec, 7)
            nc.scalar.activation(alpha[:, :], arg[:, :], ACT.Sigmoid).then_inc(gated, 1)
            act.wait_ge(gated, 1)

        @block.vector
        def _(dve):
            with dve.Fori(0, NC_ // 2) as it:
                for p in range(2):
                    front.dve(dve, it * 2 + p, p)
            link = Link(dve, vec)
            dve.wait_ge(scored, NC_)
            link(nc.vector.tensor_copy(sc[:, :, :], psc[:, :, :]))
            link(nc.vector.tensor_reduce(mx[:, :], sc[:, :, :], AX, ALU.max))

            def over(x):
                return x.rearrange("p (k o) -> p k o", o=1).broadcast_to([P, NT, E])

            link(nc.vector.tensor_tensor(best[:, :, :], sc[:, :, :], over(mx[:, :]), ALU.is_equal))
            link(nc.vector.tensor_tensor(sc[:, :, :], best[:, :, :], env.firsts[:, 0:1, :].broadcast_to([P, NT, E]), ALU.mult))
            link(nc.vector.tensor_reduce(m2[:, :], sc[:, :, :], AX, ALU.max))
            link(nc.vector.tensor_tensor(hot[:, :, :], sc[:, :, :], over(m2[:, :]), ALU.is_equal))
            link(nc.vector.tensor_tensor(arg[:, :], mx[:, :], env.root[:, :], ALU.mult))


def place(nc, env, tag, hot, slot, expert, ZS, rows, ones, NJ, weights):
    NT = env.NT
    E, J, BANKS = 8, 4, 4
    fetched, landed, turns, w1T, b1, gT, bT = weights
    with ExitStack() as ctx:
        sb, ps, sem = scope(nc, ctx, tag + "l")
        per, incl, at = sb("per", [P, E, NT]), sb("incl", [P, E, NT]), sb("at", [P, E, NT])
        keep = sb("keep", [P, E, NT])
        above = sb("above", [P, E, NT])
        tiles, ends, one8, first = sb("tiles", [P, E]), sb("ends", [P, E]), sb("one8", [P, E]), sb("first", [P, E])
        below = sb("below", [P, NJ, E - 1])
        slotf, expertf = sb("slotf", [P, NT]), sb("expertf", [P, NJ])
        counts, turned, shifts = ps("counts", [P, 2, 512]), ps("turned", [P, BANKS, 512]), ps("shifts", [P, E, J, E])
        counted, set_, vec, formed, scattered, loaded, cleared, placed, evacuated, shifted, folded = (sem(x) for x in (
            "counted", "set", "vec", "formed", "scattered", "loaded", "cleared", "placed", "evacuated", "shifted",
            "folded"))
        block = ctx.enter_context(nc.Block())
        CLEAR = not env.sorted_rows_written
        env.sorted_rows_written = True
        GROUPS = 4

        @block.tensor
        def _(pe):
            h = hot[:, :, :].rearrange("p t e -> p (t e)")
            for k in range(2):
                ins = nc.tensor.matmul(counts[:, k, 0:NT * E], env.ranks[:, k, :], h, start=True, stop=True)
            ins.then_inc(counted, 1)
            pe.wait_ge(fetched, landed)
            for j, (src, dst) in enumerate(turns):
                need(pe, evacuated, j + 1 - BANKS)
                nc.tensor.transpose(turned[:, j % BANKS, 0:P], src, env.ident[:, :]).then_inc(placed, 1)
            pe.wait_ge(evacuated, len(turns))
            for e in range(E):
                for j in range(J):
                    ins = nc.tensor.matmul(shifts[:, e, j, :], w1T[:, e, j * P:(j + 1) * P], bT, start=True, stop=True)
            ins.then_inc(shifted, 1)

        @block.scalar
        def _(act):
            for j, (src, dst) in enumerate(turns):
                act.wait_ge(placed, j + 1)
                nc.scalar.copy(dst, turned[:, j % BANKS, 0:P]).then_inc(evacuated, 1)

        @block.gpsimd
        def _(pool):
            nc.gpsimd.memset(keep[:, :, :], 1.0)
            nc.gpsimd.memset(one8[:, :], 1.0)
            nc.gpsimd.memset(ones[:, :], 1.0)
            nc.gpsimd.memset(ZS[:, :, :], 0.0).then_inc(set_, 1)
            pool.wait_ge(set_, 1)
            nc.gpsimd.memset(keep[:, :, 0:1], 0.0).then_inc(set_, 1)
            pool.wait_ge(vec, 12)
            if CLEAR:
                pool.wait_ge(cleared, 16)
            for t in range(NT):
                pool.wait_ge(formed, t + 1)
                nc.gpsimd.indirect_dma_start(env.sorted_rows[:, :], bass.IndirectOffsetOnAxis(slot[:, t:t + 1], 0),
                                             rows[:, t, :], None).then_inc(scattered, 16)

        @block.vector
        def _(dve):
            link = Link(dve, vec)
            def ei(x):
                return x.rearrange("p (t e) -> p e t", e=E)

            def over(x, n):
                return x.rearrange("p (e o) -> p e o", o=1).broadcast_to([P, E, n])

            dve.wait_ge(counted, 1)
            dve.wait_ge(set_, 2)
            link(nc.vector.tensor_copy(per[:, :, :], ei(counts[:, 1, 0:NT * E])))
            link(nc.vector.tensor_tensor_scan(incl[:, :, :].rearrange("p e t -> p (e t)"),
                                              keep[:, :, :].rearrange("p e t -> p (e t)"),
                                              per[:, :, :].rearrange("p e t -> p (e t)"), 0.0, ALU.mult, ALU.add))
            link.inc(nc.vector.tensor_tensor(at[:, :, :], incl[:, :, :], per[:, :, :], ALU.subtract))
            link(nc.vector.tensor_tensor(above[:, :, :], incl[:, :, NT - 1:NT].broadcast_to([P, E, NT]),
                                         env.steps[:, 0:1, 0:NT].broadcast_to([P, E, NT]), ALU.is_gt))
            link(nc.vector.tensor_reduce(tiles[:, :], above[:, :, :], AX, ALU.add))
            link(nc.vector.tensor_tensor_scan(ends[:, :], one8[:, :], tiles[:, :], 0.0, ALU.mult, ALU.add))
            link(nc.vector.tensor_tensor(first[:, :], ends[:, :], tiles[:, :], ALU.subtract))
            link(nc.vector.scalar_tensor_tensor(at[:, :, :], over(first[:, :], NT), float(P), at[:, :, :],
                                                ALU.mult, ALU.add))
            link(nc.vector.tensor_tensor(at[:, :, :], at[:, :, :], ei(counts[:, 0, 0:NT * E]), ALU.add))
            link(nc.vector.tensor_tensor(at[:, :, :], at[:, :, :], hot[:, :, :].rearrange("p t e -> p e t"), ALU.mult))
            link(nc.vector.tensor_reduce(slotf[:, :], at[:, :, :].rearrange("p e t -> p t e"), AX, ALU.add))
            link(nc.vector.tensor_copy(slot[:, :], slotf[:, :]))
            with dve.Fori(0, NT) as t:
                nc.vector.tensor_scalar(rows[:, t, :], env.X[:, t, :], env.mean[:, bass.ds(t, 1)],
                                        env.rnorm[:, bass.ds(t, 1)], ALU.subtract, ALU.mult).then_inc(formed, 1)
            e_ = ends[:, 0:E - 1].rearrange("p (o e) -> p o e", o=1).broadcast_to([P, NJ, E - 1])
            j_ = env.steps[:, 1, 0:NJ].rearrange("p (j o) -> p j o", o=1).broadcast_to([P, NJ, E - 1])
            link(nc.vector.tensor_tensor(below[:, :, :], e_, j_, ALU.is_le))
            link(nc.vector.tensor_reduce(expertf[:, :], below[:, :, :], AX, ALU.add))
            link(nc.vector.tensor_copy(expert[:, :], expertf[:, :]))
            dve.wait_ge(shifted, 1)
            for e in range(E):
                nc.vector.tensor_tensor(b1[:, e, :], b1[:, e, :], shifts[:, e, :, e], ALU.add).then_inc(folded, 1)
                nc.vector.tensor_scalar(w1T[:, e, :], w1T[:, e, :], gT[:, e:e + 1], None, ALU.mult).then_inc(folded, 1)
            dve.wait_ge(folded, 2 * E)
            dve.wait_ge(formed, NT)

        @block.sync
        def _(sp):
            view = env.sorted_rows.rearrange("(j p) c -> p j c", p=P)
            sp.wait_ge(set_, 1)
            if CLEAR:
                sp.dma_start(view, ZS[:, :, :]).then_inc(cleared, 16)
                sp.wait_ge(cleared, 16)
            sp.wait_ge(scattered, 16 * NT)
            for g in range(GROUPS):
                js = slice(NJ * g // GROUPS, NJ * (g + 1) // GROUPS)
                sp.dma_start(ZS[:, js, :], view[:, js, :]).then_inc(loaded, 16)
            sp.wait_ge(loaded, 16 * GROUPS)


def sorted_experts(nc, env, tag, ZS, YS, w1T, w2T, b1, b2, ones, expert, NJ):
    E, F = 8, 512
    J = F // P
    with ExitStack() as ctx:
        sb, ps, sem = scope(nc, ctx, tag + "e")
        zs, zT = sb("zs", [P, 2, P]), sb("zT", [P, 2, P])
        w1s, w2s = sb("w1s", [P, 2, F]), sb("w2s", [P, 2, F])
        b1s, b2s = sb("b1s", [P, 2, J]), sb("b2s", [1, 2, P])
        hid = sb("hid", [P, 2, J, P])
        pz, ph, po = ps("pz", [P, 2, 512]), ps("ph", [P, 2, 2, 512]), ps("po", [P, 2, 512])
        zcopied, turned, z_in, staged1, staged2, made, relu_a, relu_d, summed, kept, stored = (sem(x) for x in (
            "zcopied", "turned", "zin", "staged1", "staged2", "made", "relua", "relud", "summed", "kept", "stored"))
        block = ctx.enter_context(nc.Block())

        @block.tensor
        def _(pe):
            def turn(j, p):
                need(pe, zcopied, j + 1)
                need(pe, z_in, j - 1)
                nc.tensor.transpose(pz[:, p, 0:P], zs[:, p, :], env.ident[:, :]).then_inc(turned, 1)

            def first(j, p):
                need(pe, staged1, j + 1)
                need(pe, z_in, j + 1)
                need(pe, relu_a, j - 1)
                need(pe, relu_d, j - 1)
                for k in range(J):
                    ins = nc.tensor.matmul(ph[:, p, k // 2, (k % 2) * P:(k % 2 + 1) * P], w1s[:, p, k * P:(k + 1) * P],
                                           zT[:, p, :], start=True, stop=True)
                    if k % 2:
                        ins.then_inc(made, 1)

            def second(j, p):
                need(pe, relu_a, j + 1)
                need(pe, relu_d, j + 1)
                need(pe, staged2, j + 1)
                need(pe, kept, j - 1)
                for k in range(J):
                    nc.tensor.matmul(po[:, p, 0:P], hid[:, p, k, :], w2s[:, p, k * P:(k + 1) * P],
                                     start=(k == 0), stop=False)
                nc.tensor.matmul(po[:, p, 0:P], ones[:, :], b2s[:, p, :], start=False, stop=True).then_inc(summed, 1)

            def body(it, begin, last):
                for p in range(2):
                    j = it * 2 + p
                    if not (last and p):
                        turn(j + 1, 1 - p)
                    first(j, p)
                    if not (begin and p == 0):
                        second(j - 1, 1 - p)

            turn(0, 0)
            rounds(pe, NJ // 2, body)
            second(NJ - 1, 1)

        def relu(eng, j, p, half):
            for k in (2 * half, 2 * half + 1):
                src = ph[:, p, half, (k % 2) * P:(k % 2 + 1) * P]
                if half:
                    ins = nc.vector.tensor_scalar(hid[:, p, k, :], src, b1s[:, p, k:k + 1], 0.0, ALU.add, ALU.max)
                else:
                    ins = nc.scalar.activation(hid[:, p, k, :], src, ACT.Relu, bias=b1s[:, p, k:k + 1])
            return ins

        @block.scalar
        def _(act):
            def bring(j, p):
                hold(act, turned, j - 1)
                nc.scalar.copy(zs[:, p, :], ZS[:, j, :]).then_inc(zcopied, 1)

            def stage(j, p):
                e = act.value_load(expert[0:1, bass.ds(j, 1)], min_val=0, max_val=E - 1)
                hold(act, summed, j - 1)
                nc.scalar.copy(b2s[:, p, :], b2[:, e, :])
                nc.scalar.copy(w2s[:, p, :], w2T[:, e, :]).then_inc(staged2, 1)

            def enter(j, p):
                need(act, turned, j + 1)
                need(act, made, 2 * (j - 1))
                nc.scalar.copy(zT[:, p, :], pz[:, p, 0:P]).then_inc(z_in, 1)

            def body(it, begin, last):
                for p in range(2):
                    j = it * 2 + p
                    if not last:
                        bring(j + 2, p)
                    if not (last and p):
                        enter(j + 1, 1 - p)
                    need(act, made, 2 * j + 1)
                    need(act, summed, j - 1)
                    relu(act, j, p, 0).then_inc(relu_a, 1)
                    stage(j, p)

            bring(0, 0)
            bring(1, 1)
            enter(0, 0)
            rounds(act, NJ // 2, body)

        @block.vector
        def _(dve):
            def stage(j, p):
                e = dve.value_load(expert[0:1, bass.ds(j, 1)], min_val=0, max_val=E - 1)
                need(dve, relu_a, j - 1)
                need(dve, relu_d, j - 1)
                hold(dve, made, 2 * (j - 1))
                nc.vector.tensor_copy(b1s[:, p, :], b1[:, e, :])
                nc.vector.tensor_copy(w1s[:, p, :], w1T[:, e, :]).then_inc(staged1, 1)

            def keep(j, p):
                hold(dve, summed, j + 1)
                nc.vector.tensor_copy(YS[:, j, :], po[:, p, 0:P]).then_inc(kept, 1)

            def body(it, begin, last):
                for p in range(2):
                    j = it * 2 + p
                    if not (last and p):
                        stage(j + 1, 1 - p)
                    need(dve, made, 2 * j + 2)
                    need(dve, summed, j - 1)
                    need(dve, staged1, j + 1)
                    relu(dve, j, p, 1).then_inc(relu_d, 1)
                    if not (begin and p == 0):
                        keep(j - 1, 1 - p)

            stage(0, 0)
            rounds(dve, NJ // 2, body)
            keep(NJ - 1, 1)

        @block.sync
        def _(sp):
            view = env.sorted_out.rearrange("(j p) c -> p j c", p=P)
            GROUPS = 4
            for g in range(GROUPS):
                js = slice(NJ * g // GROUPS, NJ * (g + 1) // GROUPS)
                sp.wait_ge(kept, js.stop)
                sp.dma_start(view[:, js, :], YS[:, js, :]).then_inc(stored, 16)
            sp.wait_ge(stored, 16 * GROUPS)


def collect(nc, env, tag, YS, slot, alpha, NJ):
    NT, NC_ = env.NT, env.NC
    with ExitStack() as ctx:
        sb, ps, sem = scope(nc, ctx, tag + "c")
        own = YS
        gathered = [sem(f"gathered{n}") for n in range(NC_)]
        back = Back(nc, env, sb, ps, sem, y=True)
        block = ctx.enter_context(nc.Block())

        @block.gpsimd
        def _(pool):
            for t in range(NT):
                nc.gpsimd.indirect_dma_start(own[:, t, :], None, env.sorted_out[:, :],
                                             bass.IndirectOffsetOnAxis(slot[:, t:t + 1], 0)
                                             ).then_inc(gathered[t // TPC], 16)

        @block.vector
        def _(dve):
            for n in range(NC_):
                dve.wait_ge(gathered[n], 16 * TPC)
                back.dve(dve, n, own[:, n * TPC:(n + 1) * TPC, :], gain=alpha)


def products(nc, env, tag, items):
    with ExitStack() as ctx:
        _, ps, sem = scope(nc, ctx, tag)
        out = ps("out", [P, 4, 512])
        made, kept = sem("made"), sem("kept")
        block = ctx.enter_context(nc.Block())

        @block.tensor
        def _(pe):
            for j, (w, x, dst, scale) in enumerate(items):
                if j >= 4:
                    pe.wait_ge(kept, j - 3)
                f = dst.shape[1]
                nc.tensor.matmul(out[:, j % 4, 0:f], w, x, start=True, stop=True).then_inc(made, 1)

        @block.vector
        def _(dve):
            for j, (w, x, dst, scale) in enumerate(items):
                dve.wait_ge(made, j + 1)
                nc.vector.tensor_scalar(dst, out[:, j % 4, 0:dst.shape[1]], scale, None, ALU.mult).then_inc(kept, 1)
            dve.wait_ge(kept, len(items))


def attention(nc, env, a, tag):
    NT, T = env.NT, env.NT * P
    HD, D = 8, 128
    with ExitStack() as outer:
        sb, ps, sem = scope(nc, outer, tag)
        M, N = sb("M", [P, HD, P]), sb("N", [P, HD, P])
        g = sb("g", [P, 1])
        ZT = sb("ZT", [P, T])
        with ExitStack() as prep:
            psb, _, _ = scope(nc, prep, tag + "p")
            w = psb("w", [P, 3, HD, P])
            wo, woT = psb("wo", [P, HD * D]), psb("woT", [P, HD, P])
            row_scales(nc, env, tag + "sc", (float(D), 0.0, 1e-12, float(D) ** 0.5),
                       [(w[:, :, :, :], a["w_qkv"].rearrange("(j h p) c -> p j h c", p=P, h=HD)),
                                  (wo[:, :], a["w_out"]),
                                  (g[:, :], a["gamma"].rearrange("(p o) -> p o", o=1))])
            turn_weights(nc, tag + "t", env.ident, [(wo[:, h * P:(h + 1) * P], woT[:, h, :]) for h in range(HD)])
            products(nc, env, tag + "w",
                     [(w[:, 0, h, :], w[:, 1, h, :], M[:, h, :], float(D) ** -0.5) for h in range(HD)]
                     + [(w[:, 2, h, :], woT[:, h, :], N[:, h, :], g[:, 0:1]) for h in range(HD)])
        front_pass(nc, env, tag + "f", True, ZT[:, :], scale=g[:, 0:1])
        with ExitStack() as ctx:
            sb, ps, sem = scope(nc, ctx, tag + "a")
            vz = sb("vz", [P, 2, 2, P])
            qT = sb("qT", [P, 2, SEQ])
            R = 4
            pr = sb("pr", [P, R, 3, P])
            pT = sb("pT", [P, 2, 3, P])
            nm, den, inv = sb("nm", [P, R, 2]), sb("den", [P, R, 2]), sb("inv", [P, R, 2])
            yT = sb("yT", [P, 2, HD, SEQ])
            pq, psc, pp = ps("pq", [P, 2, 512]), ps("psc", [P, 2, 512]), ps("pp", [P, 2, 512])
            py, pout = ps("py", [P, 512]), ps("pout", [P, 512])
            valued, asked, q_in, scored, maxed, expd, inverted, scaled, turned, t_in, mixed, y_in, made, added = (
                sem(x) for x in ("valued", "asked", "qin", "scored", "maxed", "expd", "inverted", "scaled", "turned",
                                 "tin", "mixed", "yin", "made", "added"))
            back = Back(nc, env, sb, ps, sem, tiles=2)
            block = ctx.enter_context(nc.Block())
            NB = NT // 2
            U = 2 * HD
            TAIL = 7

            def pipeline(eng, step):
                def run(it, first, last, us):
                    for u in us:
                        def at(lag):
                            v = u - lag
                            if v < 0:
                                return None if first else (it - 1, v + U)
                            if v >= U:
                                return None if last else (it + 1, v - U)
                            return it, v
                        step(at)

                rounds(eng, NB // 2, lambda it, first, last: run(it, first, last, range(U)))
                run(NB // 2 - 1, NB == 2, True, range(U, U + TAIL))

            @block.tensor
            def _(pe):
                def ask(it, u):
                    m = it * U + u
                    hold(pe, q_in, m - 1)
                    nc.tensor.matmul(pq[:, u % 2, 0:SEQ], M[:, u % HD, :], ZT[:, bass.ds((it * 2 + u // HD) * SEQ, SEQ)],
                                     start=True, stop=True).then_inc(asked, 1)

                def score(it, u):
                    m = it * U + u
                    need(pe, q_in, m + 1)
                    need(pe, expd, m - 1)
                    base = (it * 2 + u // HD) * SEQ
                    S = psc[:, u % 2, :]
                    nc.tensor.matmul(S[:, 0:P], env.identb[:, :], env.causal[:, :], start=True, stop=False)
                    nc.tensor.matmul(S[:, 0:P], qT[:, u % 2, 0:P], ZT[:, bass.ds(base, P)], start=False, stop=True)
                    nc.tensor.matmul(S[:, 2 * P:3 * P], env.identb[:, :], env.causal[:, :], start=True, stop=True)
                    nc.tensor.matmul(S[:, P:3 * P], qT[:, u % 2, P:2 * P], ZT[:, bass.ds(base, SEQ)], start=False,
                                     stop=True, skip_group_check=True).then_inc(scored, 1)

                def turn(it, u):
                    m = it * U + u
                    need(pe, scaled, m + 1)
                    need(pe, t_in, m - 1)
                    for k in range(3):
                        ins = nc.tensor.transpose(pp[:, u % 2, k * P:(k + 1) * P], pr[:, u % R, k, :], env.ident[:, :])
                    ins.then_inc(turned, 1)

                def mix(it, u):
                    m = it * U + u
                    if u % HD == 0:
                        need(pe, valued, it * 2 + u // HD + 1)
                    need(pe, t_in, m + 1)
                    need(pe, y_in, m)
                    b = u // HD
                    nc.tensor.matmul(py[:, P:SEQ], vz[:, b, 1, :], pT[:, u % 2, 2, :], start=True, stop=True)
                    nc.tensor.matmul(py[:, 0:SEQ], vz[:, b, 0, :], pT[:, u % 2, 0:2, :], start=False,
                                     stop=True, skip_group_check=True).then_inc(mixed, 1)

                def project(it, u):
                    b = u // HD
                    q = it * 2 + b
                    need(pe, y_in, (q + 1) * HD)
                    need(pe, added, q)
                    for k in range(2):
                        for h in range(HD):
                            ins = nc.tensor.matmul(pout[:, k * P:(k + 1) * P], yT[:, b, h, k * P:(k + 1) * P],
                                                   N[:, h, :], start=(h == 0), stop=(h == HD - 1))
                    ins.then_inc(made, 1)

                def step(at):
                    if at(-1):
                        ask(*at(-1))
                    if at(0):
                        score(*at(0))
                    if at(2):
                        turn(*at(2))
                    if at(3):
                        mix(*at(3))
                    if at(5) and at(5)[1] % HD == HD - 1:
                        project(*at(5))

                ask(0, 0)
                pipeline(pe, step)

            @block.scalar
            def _(act):
                def q_copy(it, u):
                    m = it * U + u
                    need(act, asked, m + 1)
                    need(act, scored, m - 1)
                    nc.scalar.copy(qT[:, u % 2, :], pq[:, u % 2, 0:SEQ]).then_inc(q_in, 1)

                def exponentials(it, u):
                    m = it * U + u
                    need(act, maxed, m + 1)
                    need(act, turned, m + 1 - R)
                    need(act, inverted, m + 1 - R)
                    S = psc[:, u % 2, :]
                    nc.scalar.activation(pr[:, u % R, 0, :], S[:, 0:P], ACT.Exp, bias=nm[:, u % R, 0:1],
                                         accum_out=den[:, u % R, 0:1])
                    nc.scalar.activation(pr[:, u % R, 1:3, :], S[:, P:3 * P].rearrange("p (k c) -> p k c", k=2),
                                         ACT.Exp, bias=nm[:, u % R, 1:2],
                                         accum_out=den[:, u % R, 1:2]).then_inc(expd, 1)

                def y_copy(it, u):
                    if u % HD == 0:
                        need(act, made, it * 2 + u // HD - 1)
                    need(act, mixed, it * U + u + 1)
                    nc.scalar.copy(yT[:, u // HD, u % HD, :], py[:, 0:SEQ]).then_inc(y_in, 1)

                def step(at):
                    if at(-1):
                        q_copy(*at(-1))
                    if at(4):
                        y_copy(*at(4))
                    if at(0):
                        exponentials(*at(0))

                q_copy(0, 0)
                pipeline(act, step)

            @block.vector
            def _(dve):
                def rows(it, u):
                    b = u // HD
                    q = it * 2 + b
                    hold(dve, mixed, (q - 1) * HD)
                    for k in range(2):
                        t = q * 2 + k
                        ins = nc.vector.tensor_scalar(vz[:, b, k, :], env.X[:, t, :], env.mean[:, bass.ds(t, 1)],
                                                      env.rnorm[:, bass.ds(t, 1)], ALU.subtract, ALU.mult)
                    ins.then_inc(valued, 1)

                def maxima(it, u):
                    m = it * U + u
                    S = psc[:, u % 2, :]
                    need(dve, scored, m + 1)
                    need(dve, expd, m + 1 - R)
                    nc.vector.tensor_reduce(nm[:, u % R, 0:1], S[:, 0:P], AX, ALU.max, negate=True)
                    nc.vector.tensor_reduce(nm[:, u % R, 1:2], S[:, P:3 * P], AX, ALU.max,
                                            negate=True).then_inc(maxed, 1)

                def scale(it, u):
                    m = it * U + u
                    need(dve, expd, m + 1)
                    need(dve, scaled, m + 1 - R)
                    nc.vector.reciprocal(inv[:, u % R, :], den[:, u % R, :]).then_inc(inverted, 1)
                    need(dve, inverted, m + 1)
                    nc.vector.tensor_scalar(pr[:, u % R, 0, :], pr[:, u % R, 0, :], inv[:, u % R, 0:1], None, ALU.mult)
                    nc.vector.tensor_scalar(pr[:, u % R, 1:3, :], pr[:, u % R, 1:3, :], inv[:, u % R, 1:2], None,
                                            ALU.mult).then_inc(scaled, 1)

                def enter(it, u):
                    m = it * U + u
                    need(dve, turned, m + 1)
                    need(dve, mixed, m - 1)
                    nc.vector.tensor_copy(pT[:, u % 2, :, :],
                                          pp[:, u % 2, 0:3 * P].rearrange("p (k c) -> p k c", k=3)).then_inc(t_in, 1)

                def residual(it, u):
                    q = it * 2 + u // HD
                    need(dve, made, q + 1)
                    back.dve(dve, q, pout[:, 0:2 * P].rearrange("p (k c) -> p k c", k=2))
                    dve.sem_inc(added, 1)

                def step(at):
                    if at(3):
                        enter(*at(3))
                    if at(0):
                        if at(0)[1] % HD == 0:
                            rows(*at(0))
                        maxima(*at(0))
                    if at(1):
                        scale(*at(1))
                    if at(6) and at(6)[1] % HD == HD - 1:
                        residual(*at(6))

                pipeline(dve, step)


def product_key_weights(nc, env, a, tag):
    HD, K, NE = 8, 32, 1024
    J = NE // P
    second = (1.0, 1e-6, 0.0, 1.0)
    if env.product_key_weights is not None:
        row_scales(nc, env, tag + "sc", second)
        return env.product_key_weights
    lasting, _, _ = scope(nc, env.ctx, tag + "g")
    G = lasting("G", [P, HD, 2, K])
    downT, up, g = lasting("downT", [P, NE]), lasting("up", [P, J, P]), lasting("g", [P, 1])
    env.product_key_weights = (G, downT, up, g)
    with ExitStack() as ctx:
        sb, _, _ = scope(nc, ctx, tag + "p")
        wq = sb("wq", [P, HD * 2, P])
        keys, keysT = sb("keys", [P, 2, 2, P]), sb("keysT", [P, 2, HD * K])
        down = sb("down", [P, J, P])
        rows = a["w_q"].rearrange("(j p) c -> p j c", p=P)
        loads = [(wq[:, j:j + 4, :], rows[:, j:j + 4, :]) for j in range(0, 2 * HD, 4)]
        loads += [(keys[:, :, :, :], a["keys"].rearrange("(u h) k s d -> (h k) u s d", u=2)),
                  (down[:, :, :], a["expert_down"].rearrange("(j p) c -> p j c", p=P)),
                  (up[:, :, :], a["expert_up"].rearrange("(j p) c -> p j c", p=P)),
                  (g[:, :], a["norm_w"].rearrange("(p o) -> p o", o=1))]
        row_scales(nc, env, tag + "sc", second, loads)
        turn_weights(nc, tag + "t", env.ident,
                     [(down[:, j, :], downT[:, j * P:(j + 1) * P]) for j in range(J)]
                     + [(keys[:, t, s, :], keysT[:, s, t * P:(t + 1) * P]) for t in range(2) for s in range(2)])
        products(nc, env, tag + "w", [(wq[:, 2 * h + s, :], keysT[:, s, h * K:(h + 1) * K], G[:, h, s, :], 1.0)
                                      for h in range(HD) for s in range(2)])
    return env.product_key_weights


def product_keys(nc, env, a, tag):
    NT, T = env.NT, env.NT * P
    HD, K, NE = 8, 32, 1024
    J = NE // P
    G, downT, up, g = product_key_weights(nc, env, a, tag)
    with ExitStack() as outer:
        sb, ps, sem = scope(nc, outer, tag)
        ZT = sb("ZT", [P, T])
        front_pass(nc, env, tag + "f", True, ZT[:, :], scale=g[:, 0:1])
        with ExitStack() as ctx:
            sb, ps, sem = scope(nc, ctx, tag + "a")
            zc = sb("zc", [P, 2, P])
            sims = sb("sims", [P, 2, HD, 2, K])
            top = sb("top", [P, HD, 2, 8])
            cand = sb("cand", [P, HD, 8, 8])
            best = sb("best", [P, HD, 8])
            thr = sb("thr", [P, 2, HD])
            PR, DR, WR = 7, 1, 4
            psums, dsums = sb("psums", [P, PR, K, K]), sb("dsums", [P, DR, K, K])
            w = sb("w", [P, WR, NE])
            gl = sb("gl", [P, 2, J, P])
            hid = sb("hid", [P, J, P])
            psim, phd, pw, pout = ps("psim", [P, 512]), ps("phd", [P, J, P]), ps("pw", [P, 2, J, P]), ps("pout", [P, 512])
            copied, scored, s_in, pooled, paired, vec, weighed, summed, hidden, gelud, mixed, made, added, measured = (
                sem(x) for x in ("copied", "scored", "sin", "pooled", "paired", "vec", "weighed", "summed", "hidden",
                                 "gelud", "mixed", "made", "added", "measured"))
            block = ctx.enter_context(nc.Block())
            DVE_SUMS = (4,)
            POOL_SUMS = tuple(h for h in range(HD) if h not in DVE_SUMS)
            NP, ND = len(POOL_SUMS), len(DVE_SUMS)
            UNITS = ((0,), (1,), (2, 3), (4,), (5,), (6,), (7,))
            NU = len(UNITS)
            unit_of = {h: u for u, hs in enumerate(UNITS) for h in hs}
            PAIRS = tuple(hs for hs in UNITS if len(hs) == 2)
            PRELIM, STEPS = 4, 4 + ND

            def sum_of(p, h):
                s1 = sims[:, p, h, 0, :].rearrange("p (i o) -> p i o", o=1).broadcast_to([P, K, K])
                s2 = sims[:, p, h, 1, :].rearrange("p (o j) -> p o j", o=1).broadcast_to([P, K, K])
                return s1, s2

            @block.gpsimd
            def _(pool):
                def form(t, p, k):
                    h = POOL_SUMS[k]
                    need(pool, s_in, t + 1)
                    back_t, back_k = (t, k - PR) if k >= PR else (t - 1, k - PR + NP)
                    need(pool, weighed, back_t * HD + POOL_SUMS[back_k] + 1)
                    s1, s2 = sum_of(p, h)
                    nc.gpsimd.tensor_tensor(psums[:, (NP * p + k) % PR, :, :], s1, s2, ALU.add).then_inc(pooled, 1)

                def pair(t, i):
                    h, g_ = PAIRS[i]
                    need(pool, weighed, t * HD + g_ + 1)
                    nc.gpsimd.tensor_tensor(w[:, h % WR, :], w[:, h % WR, :], w[:, g_ % WR, :], ALU.add).then_inc(paired, 1)

                AHEAD = 5
                for k in range(AHEAD):
                    form(0, 0, k)

                def body(it, first, last):
                    for p in range(2):
                        t = it * 2 + p
                        form(t, p, AHEAD)
                        pair(t, 0)
                        form(t, p, AHEAD + 1)
                        if not (last and p == 1):
                            for k in range(AHEAD):
                                form(t + 1, 1 - p, k)

                rounds(pool, NT // 2, body)

            @block.tensor
            def _(pe):
                def sim(t, p):
                    need(pe, copied, t + 1)
                    need(pe, s_in, t)
                    nc.tensor.matmul(psim[:, :], zc[:, p, :], G[:, :, :, :].rearrange("p h s k -> p (h s k)"),
                                     start=True, stop=True).then_inc(scored, 1)

                def hide(t):
                    hold(pe, gelud, t)
                    for j in range(J):
                        ins = nc.tensor.matmul(phd[:, j, :], downT[:, j * P:(j + 1) * P], ZT[:, bass.ds(t * P, P)],
                                               start=True, stop=True)
                    ins.then_inc(hidden, 1)

                def out(t):
                    need(pe, mixed, t + 1)
                    need(pe, added, t)
                    for j in range(J):
                        ins = nc.tensor.matmul(pout[:, 0:P], hid[:, j, :], up[:, j, :], start=(j == 0), stop=(j == J - 1))
                    ins.then_inc(made, 1)

                def body(it, first, last):
                    for p in range(2):
                        t = it * 2 + p
                        for u, hs in enumerate(UNITS):
                            if u == 0:
                                if not (last and p == 1):
                                    sim(t + 1, 1 - p)
                                need(pe, mixed, t - 1)
                            if len(hs) == 2:
                                need(pe, paired, t * len(PAIRS) + PAIRS.index(hs) + 1)
                            else:
                                need(pe, weighed, t * HD + hs[0] + 1)
                            for j in range(J):
                                ins = nc.tensor.matmul(pw[:, p, j, :], w[:, hs[0] % WR, j * P:(j + 1) * P], env.ident[:, :],
                                                       start=(u == 0 and j % 4 == 0), stop=(u == NU - 1 and j % 4 == 3),
                                                       skip_group_check=True)
                            ins.then_inc(summed, 1)
                            if u == 1 and not (first and p == 0):
                                out(t - 1)
                            if u == 1 and not (last and p == 1):
                                hide(t + 1)

                sim(0, 0)
                hide(0)
                rounds(pe, NT // 2, body)
                out(NT - 1)

            @block.scalar
            def _(act):
                def body(it, first, last):
                    for p in range(2):
                        t = it * 2 + p
                        hold(act, scored, t - 1)
                        nc.scalar.copy(zc[:, p, :], ZT[:, bass.ds(t * P, P)]).then_inc(copied, 1)
                        need(act, weighed, (t - 1) * HD)
                        need(act, scored, t + 1)
                        nc.scalar.copy(sims[:, p, :, :, :].rearrange("p h s k -> p (h s k)"), psim[:, :]).then_inc(s_in, 1)
                        need(act, mixed, t - 1)
                        need(act, hidden, t + 1)
                        for q in range(2):
                            ins = nc.scalar.activation(gl[:, p, 4 * q:4 * q + 4, :], phd[:, 4 * q:4 * q + 4, :], ACT.Gelu)
                        ins.then_inc(gelud, 1)

                rounds(act, NT // 2, body)

            @block.vector
            def _(dve):
                def prelim(t, p, step, count):
                    if step == 0:
                        hold(dve, s_in, t + 1)
                        for h in range(HD):
                            for s in range(2):
                                ins = nc.vector.max(top[:, h, s, :], sims[:, p, h, s, :])
                    if step == 1:
                        dve.wait_ge(vec, count)
                        t1 = top[:, :, 0, :].rearrange("p h (i o) -> p h i o", o=1).broadcast_to([P, HD, 8, 8])
                        t2 = top[:, :, 1, :].rearrange("p h (o i) -> p h o i", o=1).broadcast_to([P, HD, 8, 8])
                        ins = nc.vector.tensor_tensor(cand[:, :, :, :], t1, t2, ALU.add)
                    if step == 2:
                        hold(dve, vec, count)
                        for h in range(HD):
                            ins = nc.vector.max(best[:, h, :], cand[:, h, :, :].rearrange("p i j -> p (i j)"))
                    if step == 3:
                        dve.wait_ge(vec, count)
                        ins = nc.vector.tensor_scalar(thr[:, p, :], best[:, :, 7], 1.1754944e-38, None, ALU.max)
                    ins.then_inc(vec, 1)

                def form(t, p, k):
                    need(dve, weighed, (t - 1) * HD + DVE_SUMS[k] + 1)
                    s1, s2 = sum_of(p, DVE_SUMS[k])
                    nc.vector.tensor_tensor(dsums[:, k, :, :], s1, s2, ALU.add).then_inc(vec, 1)

                def weigh(t, p, h, count):
                    if h in DVE_SUMS:
                        src = dsums[:, DVE_SUMS.index(h), :, :]
                        dve.wait_ge(vec, count)
                    else:
                        k = POOL_SUMS.index(h)
                        src = psums[:, (NP * p + k) % PR, :, :]
                        need(dve, pooled, t * NP + k + 1)
                    back_t, back_h = (t, h - WR) if h >= WR else (t - 1, h + HD - WR)
                    need(dve, summed, back_t * NU + unit_of[back_h] + 1)
                    nc.vector.scalar_tensor_tensor(w[:, h % WR, :].rearrange("p (i j) -> p i j", i=K), src,
                                                   thr[:, p, h:h + 1], src, ALU.is_ge, ALU.mult).then_inc(weighed, 1)

                def finish(t, p):
                    need(dve, summed, (t + 1) * NU)
                    need(dve, gelud, t + 1)
                    need(dve, made, t)
                    for q in range(2):
                        ins = nc.vector.tensor_tensor(hid[:, 4 * q:4 * q + 4, :], gl[:, p, 4 * q:4 * q + 4, :],
                                                      pw[:, p, 4 * q:4 * q + 4, :], ALU.mult)
                    ins.then_inc(mixed, 1)

                def residual(t):
                    need(dve, made, t + 1)
                    nc.vector.tensor_tensor(env.X[:, t, :], env.X[:, t, :], pout[:, 0:P], ALU.add).then_inc(added, 1)

                def statistics(t):
                    hold(dve, added, t + 1)
                    nc.vector.bn_stats(env.stats[:, t, :], env.X[:, t, :]).then_inc(measured, 1)

                for step in range(PRELIM):
                    prelim(0, 0, step, step)

                def body(it, first, last):
                    for p in range(2):
                        t = it * 2 + p
                        done = PRELIM + STEPS * t
                        begun, final = first and p == 0, last and p == 1
                        dve.wait_ge(vec, done)
                        weigh(t, p, 0, done)
                        weigh(t, p, 1, done)
                        weigh(t, p, 2, done)
                        if not begun:
                            finish(t - 1, 1 - p)
                        if not final:
                            prelim(t + 1, 1 - p, 0, done)
                        weigh(t, p, 3, done)
                        form(t, p, 0)
                        if not final:
                            prelim(t + 1, 1 - p, 1, done + 1)
                        weigh(t, p, 4, done + (1 if final else 2))
                        if not final:
                            prelim(t + 1, 1 - p, 2, done + 3)
                        weigh(t, p, 5, done)
                        if not begun:
                            residual(t - 1)
                        if not final:
                            prelim(t + 1, 1 - p, 3, done + 4)
                        weigh(t, p, 6, done)
                        if not begun:
                            statistics(t - 1)
                        weigh(t, p, 7, done)

                rounds(dve, NT // 2, body)
                finish(NT - 1, 1)
                residual(NT - 1)
                statistics(NT - 1)
                dve.wait_ge(measured, NT)


def rotary(nc, env, a, tag):
    NT, NC_ = env.NT, env.NC
    HD, D, S = 16, 8, 8
    NB = NT // 2
    with ExitStack() as outer:
        sb, ps, sem = scope(nc, outer, tag)
        wT, pT = sb("wT", [P, 3 * P]), sb("pT", [P, P])
        three = sb("three", [P, HD, P], BF16)
        wkq, qw = sb("wkq", [P, D]), sb("qw", [P, D])
        KK, QQ = sb("KK", [P, NT, P]), sb("QQ", [P, NT, P])
        V = sb("V", [P, NT, HD, D])
        norm2 = sb("norm2", [P, 2, NT, HD])
        with ExitStack() as prep:
            psb, pps, psem = scope(nc, prep, tag + "p")
            w, pw = psb("w", [P, 3, P]), psb("pw", [P, P])
            zc = psb("zc", [P, 2, CH])
            rope = psb("rope", [P, 2, 2, P])
            row_scales(nc, env, tag + "sc", None, [(w[:, :, :], a["W_kqv"].rearrange("(j p) c -> p j c", p=P)),
                                  (pw[:, :], a["W_proj"]),
                                  (rope[:, :, :, :], a["rope"]), (three[:, :, :], a["three"]),
                                  (wkq[:, :], a["k_norm_w"].rearrange("(o d) -> o d", o=1).broadcast_to([P, D])),
                                  (qw[:, :], a["q_norm_w"].rearrange("(o d) -> o d", o=1).broadcast_to([P, D]))])
            turn_weights(nc, tag + "t", env.ident, [(w[:, j, :], wT[:, j * P:(j + 1) * P]) for j in range(3)]
                         + [(pw[:, :], pT[:, :])])
            t1, t2 = psb("t1", [P, 2, 2, 2 * P]), psb("t2", [P, 2, 2, 2 * P])
            sq = psb("sq", [P, 2, TPC, P])
            pk, pv = pps("pk", [P, 2, TPC, 2 * P]), pps("pv", [P, 2, TPC, P])
            front = Front(nc, env, psb, pps, psem, False, lambda p: zc[:, p, :], banks=2)
            made, vin, cosd, rotated, squared, reduced = (psem(x) for x in (
                "made", "vin", "cosd", "rotated", "squared", "reduced"))
            with nc.Block() as block:
                def chunks(eng, now, ahead=None, behind=None):
                    def body(it, first, last):
                        for p in range(2):
                            n = it * 2 + p
                            if ahead and not (last and p):
                                ahead(n + 1, 1 - p)
                            if now:
                                now(n, p)
                            if behind and not (first and p == 0):
                                behind(n - 1, 1 - p)

                    if ahead:
                        ahead(0, 0)
                    rounds(eng, NC_ // 2, body)
                    if behind:
                        behind(NC_ - 1, 1)

                @block.gpsimd
                def _(pool):
                    def add(n, p):
                        for q in range(2):
                            m = 2 * n + q
                            hold(pool, cosd, 3 * m + 3)
                            for z, dst in ((0, KK), (1, QQ)):
                                ins = nc.gpsimd.tensor_tensor(dst[:, bass.ds(2 * m, 2), :], t1[:, q, :, z * P:(z + 1) * P],
                                                              t2[:, q, :, z * P:(z + 1) * P], ALU.add)
                            ins.then_inc(rotated, 1)

                    chunks(pool, add)

                @block.tensor
                def _(pe):
                    def project(n, p):
                        front.wait(pe, n)
                        need(pe, cosd, 6 * (n - 1))
                        need(pe, vin, n - 1)
                        for k in range(TPC):
                            z = zc[:, p, k * P:(k + 1) * P]
                            nc.tensor.matmul(pk[:, p, k, :], z, wT[:, 0:2 * P], start=True, stop=True)
                            ins = nc.tensor.matmul(pv[:, p, k, :], z, wT[:, 2 * P:3 * P], start=True, stop=True)
                        ins.then_inc(made, 1)

                    front.credit(pe)
                    chunks(pe, project, ahead=lambda n, p: front.pe(pe, n, p))

                @block.vector
                def _(dve):
                    def part(v, f):
                        return v.rearrange("p t (h f d) -> p t h f d", f=2, d=D // 2)[:, :, :, f, :]

                    def rotate(n, p):
                        need(dve, made, n + 1)
                        for q in range(2):
                            m = 2 * n + q
                            need(dve, rotated, m - 1)
                            for z in range(2):
                                x = pk[:, p, 2 * q:2 * q + 2, z * P:(z + 1) * P]
                                ins = nc.vector.tensor_tensor(t1[:, q, :, z * P:(z + 1) * P], x, rope[:, :, 0, :], ALU.mult)
                            ins.then_inc(cosd, 1)
                            for half in range(2):
                                for z in range(2):
                                    x = part(pk[:, p, 2 * q:2 * q + 2, z * P:(z + 1) * P], 1 - half)
                                    ins = nc.vector.tensor_tensor(part(t2[:, q, :, z * P:(z + 1) * P], half), x,
                                                                  part(rope[:, :, 1, :], half), ALU.mult)
                                ins.then_inc(cosd, 1)

                    def sum_squares(n, p):
                        for z in range(2):
                            hold(dve, squared, 2 * n + z + 1)
                            nc.vector.tensor_reduce(norm2[:, z, bass.ds(n * TPC, TPC), :],
                                                    sq[:, z, :, :].rearrange("p t (h d) -> p t h d", d=D), AX,
                                                    ALU.add).then_inc(reduced, 1)

                    chunks(dve, rotate, ahead=lambda n, p: front.dve(dve, n, p), behind=sum_squares)

                @block.scalar
                def _(act):
                    def ahead(n, p):
                        need(act, made, n - 1)
                        front.act(act, n, p)

                    def values(n, p):
                        hold(act, made, n + 1)
                        for k in range(TPC):
                            ins = nc.scalar.copy(V[:, n * TPC + k, :, :], pv[:, p, k, :].rearrange(
                                "p (h d) -> p h d", d=D))
                        ins.then_inc(vin, 1)

                    def square(n, p):
                        need(act, rotated, 2 * n + 2)
                        hold(act, reduced, 2 * n)
                        for z, src in ((0, KK), (1, QQ)):
                            nc.scalar.activation(sq[:, z, :, :], src[:, bass.ds(n * TPC, TPC), :], ACT.Square
                                                 ).then_inc(squared, 1)

                    front.credit_act(act)
                    chunks(act, values, ahead=ahead, behind=square)
        KS, QS = sb("KS", [P, 2, 2 * HD * S * D], BF16), sb("QS", [P, 2, 2 * HD * S * D], BF16)
        nb = sb("nb", [P, 2, 2, 64], BF16)
        G8 = HD // 2
        W = 2 * P + 2 * D
        held = sb("held", [P, 2, G8 * W])
        with ExitStack() as ctx:
            sb, ps, sem = scope(nc, ctx, tag + "n")
            rms = sb("rms", [P, 2, NT, HD])
            rooted, vec, inverted, divided, zeroed = (sem(x) for x in ("rooted", "vec", "inverted", "divided", "zeroed"))
            block = ctx.enter_context(nc.Block())

            def divide(tensor_tensor, z, x):
                v = x[:, :, :].rearrange("p t (h d) -> p (t h) d", d=D)
                f = norm2[:, z, :, :].rearrange("p t (h o) -> p (t h) o", o=1).broadcast_to([P, NT * HD, D])
                return tensor_tensor(v, v, f, ALU.mult)

            @block.scalar
            def _(act):
                nc.scalar.activation(rms[:, :, :, :], norm2[:, :, :, :], ACT.Sqrt, scale=1.0 / D).then_inc(rooted, 1)

            @block.vector
            def _(dve):
                link = Link(dve, vec)
                link(nc.vector.tensor_tensor(wkq[:, :], wkq[:, :], qw[:, :], ALU.mult))
                dve.wait_ge(rooted, 1)
                link(nc.vector.tensor_scalar(rms[:, :, :, :], rms[:, :, :, :], 1e-6, None, ALU.add))
                for z in (1, 0):
                    nc.vector.reciprocal(norm2[:, z, :, :], rms[:, z, :, :]).then_inc(inverted, 1)
                dve.wait_ge(inverted, 2)
                link(divide(nc.vector.tensor_tensor, 0, KK))
                v = KK[:, :, :].rearrange("p t (h d) -> p (t h) d", d=D)
                f = wkq[:, :].rearrange("p (o d) -> p o d", o=1).broadcast_to([P, NT * HD, D])
                link(nc.vector.scalar_tensor_tensor(v, v, float(D) ** -0.5, f, ALU.mult, ALU.mult))

            @block.gpsimd
            def _(pool):
                nc.gpsimd.memset(held[:, :, :], 0.0).then_inc(zeroed, 1)
                pool.wait_ge(zeroed, 1)
                for g in range(2):
                    for t in range(2):
                        part = held[:, g, :].rearrange("p (k c) -> p k c", c=W)[:, :, t * P + D:t * P + 2 * D]
                        ins = nc.gpsimd.memset(part, 1.0)
                pool.wait_ge(inverted, 1)
                divide(nc.gpsimd.tensor_tensor, 1, QQ).then_inc(divided, 1)
                nc.gpsimd.memset(KS[:, :, :], 0.0)
                nc.gpsimd.memset(QS[:, :, :], 0.0)
                nc.gpsimd.memset(nb[:, :, :, :], 0.0).then_inc(zeroed, 1)
                pool.wait_ge(divided, 1)
                pool.wait_ge(zeroed, 2)
        with ExitStack() as ctx:
            sb, ps, sem = scope(nc, ctx, tag + "a")
            rk, rq = sb("rk", [P, 2, 2 * P]), sb("rq", [P, 2, 2 * P])
            KT, QT = sb("KT", [P, 2, HD // 2, SEQ], BF16), sb("QT", [P, 2, HD // 2, SEQ], BF16)
            nm = sb("nm", [P, 2, HD])
            nr = sb("nr", [P, 2, HD])
            nT = sb("nT", [P, 2, SEQ], BF16)
            R = 4
            pr = sb("pr", [P, R, 3 * P])
            inv = sb("inv", [P, 2, 2, HD // 2])
            yu = sb("yu", [P, 2, SEQ])
            yt, yT = sb("yt", [P, 2, HD, D]), sb("yT", [P, SEQ])
            ptr = ps("ptr", [P, 2, 1024], BF16)
            psc, pst = ps("psc", [P, 2, 512]), ps("pst", [P, 2, 512])
            py, pout = ps("py", [P, 2, SEQ]), ps("pout", [P, 512])
            (kcast, qcast, krest, qrest, placed, t_in, scored, maxed, nmaxed, n_placed, n_in, shifted, expd, mixed,
             y_norm, y_placed, y_in, made, added, ainv, valued, y_out, y_back) = (sem(x) for x in (
                "kcast", "qcast", "krest", "qrest", "placed", "tin", "scored", "maxed", "nmaxed",
                "nplaced", "nin", "shifted", "expd", "mixed", "ynorm", "yplaced", "yin", "made", "added", "ainv", "valued", "yout", "yback"))
            back = Back(nc, env, sb, ps, sem, tiles=2)
            block = ctx.enter_context(nc.Block())

            def first_head(u):
                g = 8 * (u // 3 % 2) + u // 6
                return g if u % 3 == 0 else g + 4 * (u % 3 - 1)

            def slots(buf, p):
                return buf[:, p, :].rearrange("p (g s d) -> p g s d", s=S, d=D)

            def spread(x, k):
                return x.rearrange("p (g o d) -> p g o d", o=1, d=D).broadcast_to([P, 2 * HD, k, D])

            def heads(x):
                return x.rearrange("p (g d) -> p g d", d=D)

            def pipeline(eng, step, tail):
                def run(it, first, last, us):
                    for u in us:
                        def seq(d, u=u):
                            v = u // HD + d
                            if (v < 0 and first) or (v >= 2 and last):
                                return None
                            return it * 2 + v, v % 2

                        def head(lag, u=u):
                            at = seq((u - lag) // HD - u // HD)
                            return at and (*at, (u - lag) % HD)
                        step(u % HD, seq, head)

                rounds(eng, NB // 2, lambda it, first, last: run(it, first, last, range(2 * HD)))
                run(NB // 2 - 1, NB == 2, True, range(2 * HD, 2 * HD + tail))

            @block.scalar
            def _(act):
                def cast(n, p, part):
                    k = KK[:, bass.ds(2 * n, 2), :].rearrange("p t c -> p (t c)")
                    ks = slots(KS, p)
                    if part == 0:
                        hold(act, placed, 4 * (n - 1))
                        nc.scalar.copy(ks[:, :, 0:3, :], spread(k, 3)).then_inc(kcast, 1)
                    if part == 1:
                        need(act, krest, 2 * n + 1)
                        nc.scalar.copy(ks[:, :, 3:5, :], spread(rk[:, 0, :], 2)).then_inc(kcast, 1)
                    if part == 2:
                        need(act, krest, 2 * n + 2)
                        nc.scalar.copy(ks[:, :, 5, :], heads(rk[:, 1, :])).then_inc(kcast, 1)

                def exponentials(n, p, h):
                    m = n * HD + h
                    need(act, shifted, m + 1)
                    need(act, mixed, m + 1 - R)
                    nc.scalar.activation(pr[:, h % R, :], pst[:, h % 2, 0:3 * P], ACT.Exp).then_inc(expd, 1)

                def evacuate(n, p):
                    need(act, mixed, (n + 1) * HD)
                    need(act, y_back, n)
                    nc.scalar.copy(yu[:, :, :], py[:, :, :]).then_inc(y_out, 1)

                def enter_y(n, p):
                    need(act, y_placed, n + 1)
                    nc.scalar.copy(yT[:, :], pout[:, 0:SEQ]).then_inc(y_in, 1)

                def step(h, seq, head):
                    if h == 2 and seq(-1):
                        evacuate(*seq(-1))
                    if head(0):
                        exponentials(*head(0))
                    if h == 8 and seq(-1):
                        enter_y(*seq(-1))
                    if h in (8, 10, 12) and seq(2):
                        cast(*seq(2), h // 2 - 4)

                for n in range(2):
                    for part in range(3):
                        cast(n, n, part)
                pipeline(act, step, 9)

            @block.gpsimd
            def _(pool):
                def values(n, p, g):
                    hold(pool, mixed, (n - 1) * HD + (g + 1) * G8)
                    for t in range(2):
                        dst = held[:, g, :].rearrange("p (k c) -> p k c", c=W)[:, :, t * P:t * P + D]
                        ins = nc.gpsimd.tensor_copy(dst, V[:, 2 * n + t, g * G8:(g + 1) * G8, :])
                    ins.then_inc(valued, 1)

                def rest(n, p):
                    ks, qs = slots(KS, p), slots(QS, p)
                    k = KK[:, bass.ds(2 * n, 2), :].rearrange("p t (h d) -> p (t h) d", d=D)
                    q = QQ[:, bass.ds(2 * n, 2), :].rearrange("p t (h d) -> p (t h) d", d=D)
                    pool.wait_ge(kcast, 3 * n + 1)
                    nc.gpsimd.tensor_tensor(heads(rk[:, 0, :]), k, ks[:, :, 0, :], ALU.subtract).then_inc(krest, 1)
                    pool.wait_ge(qcast, 5 * n + 2)
                    nc.gpsimd.tensor_tensor(heads(rq[:, 0, :]), q, qs[:, :, 0, :], ALU.subtract).then_inc(qrest, 1)
                    pool.wait_ge(kcast, 3 * n + 2)
                    pool.wait_ge(krest, 2 * n + 1)
                    nc.gpsimd.tensor_tensor(heads(rk[:, 1, :]), heads(rk[:, 0, :]), ks[:, :, 3, :], ALU.subtract).then_inc(krest, 1)
                    pool.wait_ge(qcast, 5 * n + 4)
                    pool.wait_ge(qrest, 2 * n + 1)
                    nc.gpsimd.tensor_tensor(heads(rq[:, 1, :]), heads(rq[:, 0, :]), qs[:, :, 1, :], ALU.subtract).then_inc(qrest, 1)

                def body(it, first, last):
                    for p in range(2):
                        n = it * 2 + p
                        values(n, p, 0)
                        values(n, p, 1)
                        if not last:
                            rest(n + 2, p)

                rest(0, 0)
                rest(1, 1)

                rounds(pool, NB // 2, body)

            @block.tensor
            def _(pe):
                def place(n, p, g):
                    m = 4 * n + g
                    if g == 0:
                        need(pe, kcast, 3 * n + 3)
                        need(pe, n_in, n)
                    if g == 2:
                        need(pe, qcast, 5 * n + 5)
                    need(pe, t_in, m - 1)
                    src = (KS if g < 2 else QS)[:, p, :].rearrange("p (t a c) -> p t a c", t=2, c=P)
                    for a_ in range(4):
                        for t in range(2):
                            ins = nc.tensor.transpose(ptr[:, g % 2, (a_ * 2 + t) * P:(a_ * 2 + t + 1) * P],
                                                      src[:, t, 4 * (g % 2) + a_, :], env.identb[:, :])
                    ins.then_inc(placed, 1)

                def rows_of(h):
                    return slice(64 * (h % 2), 64 * (h % 2) + 64)

                def score(n, p, u):
                    m = 12 * n + u
                    if u == 0:
                        need(pe, t_in, 4 * n + 4)
                    need(pe, maxed, m - 1)
                    B = psc[:, u % 2, :]
                    g = first_head(u)
                    if u % 3 == 0:
                        for k in range(4):
                            h = g + 2 * k
                            r_ = rows_of(h)
                            o = B[:, k * P:(k + 1) * P]
                            nc.tensor.matmul(o, env.identb[:, :], env.causal[:, :], start=True, stop=False)
                            ins = nc.tensor.matmul(o, QT[r_, p, h // 2, 0:P], KT[r_, p, h // 2, 0:P], start=False, stop=True)
                    else:
                        for k in range(2):
                            h = g + 2 * k
                            r_ = rows_of(h)
                            nc.tensor.matmul(B[:, k * SEQ + P:(k + 1) * SEQ], env.identb[:, :], env.causal[:, :],
                                             start=True, stop=True)
                            ins = nc.tensor.matmul(B[:, k * SEQ:(k + 1) * SEQ], QT[r_, p, h // 2, P:SEQ],
                                                   KT[r_, p, h // 2, :], start=False, stop=True, skip_group_check=True)
                    ins.then_inc(scored, 1)

                def turn_max(n, p):
                    need(pe, nmaxed, 5 * n + 5)
                    need(pe, t_in, 4 * n + 4)
                    for t in range(2):
                        ins = nc.tensor.transpose(ptr[:, 0, t * P:(t + 1) * P],
                                                  nb[:, t, :, :].rearrange("p s h -> p (s h)"), env.identb[:, :])
                    ins.then_inc(n_placed, 1)

                def shift(n, p, h):
                    m = n * HD + h
                    need(pe, expd, m - 1)
                    if h == 0:
                        need(pe, n_in, n + 1)
                    B = pst[:, h % 2, :]
                    r_ = rows_of(h)
                    one = three[r_, h, :]
                    for c0, c1, j0, i0 in ((0, SEQ, 0, 0), (SEQ, SEQ + P, P, P)):
                        nc.tensor.matmul(B[:, c0:c0 + P], env.identb[:, :], env.causalT[:, :], start=True, stop=True)
                        nc.tensor.matmul(B[:, c0:c1], one, nT[r_, p, i0:SEQ], start=False, stop=True, skip_group_check=True)
                        ins = nc.tensor.matmul(B[:, c0:c1], KT[r_, p, h // 2, j0:j0 + P], QT[r_, p, h // 2, i0:SEQ],
                                               start=False, stop=True, skip_group_check=True)
                    ins.then_inc(shifted, 1)

                def mix(n, p, h):
                    m = n * HD + h
                    need(pe, expd, m + 1)
                    if h == 0:
                        need(pe, y_out, n)
                    g, k = h // G8, h % G8
                    if k == 0:
                        need(pe, valued, 2 * n + g + 1)
                    e = pr[:, h % R, :]
                    own = held[:, g, k * 2 * P:(k + 1) * 2 * P]
                    nc.tensor.matmul(py[:, g, :], own[:, 0:P], e[:, 0:SEQ], start=(k == 0), stop=False,
                                     skip_group_check=True)
                    nc.tensor.matmul(py[:, g, P:SEQ], own[:, P:2 * P], e[:, SEQ:SEQ + P], start=False,
                                     stop=(k == G8 - 1), skip_group_check=True).then_inc(mixed, 1)

                def turn_back(n, p):
                    need(pe, y_out, n + 1)
                    need(pe, added, n)
                    for t in range(2):
                        for g in range(2):
                            ins = nc.tensor.transpose(pout[:, (t * 2 + g) * P:(t * 2 + g + 1) * P],
                                                      yu[:, g, t * P:(t + 1) * P], env.ident[:, :])
                    ins.then_inc(y_back, 1)

                def place_y(n, p):
                    need(pe, y_norm, n + 1)
                    for t in range(2):
                        ins = nc.tensor.transpose(pout[:, t * P:(t + 1) * P], yt[:, t, :, :].rearrange("p h d -> p (h d)"),
                                                  env.ident[:, :])
                    ins.then_inc(y_placed, 1)

                def project(n, p):
                    need(pe, y_in, n + 1)
                    for t in range(2):
                        ins = nc.tensor.matmul(pout[:, SEQ + t * P:SEQ + (t + 1) * P], yT[:, t * P:(t + 1) * P], pT[:, :],
                                               start=True, stop=True)
                    ins.then_inc(made, 1)

                def step(h, seq, head):
                    if head(0):
                        shift(*head(0))
                    if seq(1):
                        if h < 4:
                            place(*seq(1), h)
                        elif h < 10:
                            score(*seq(1), 2 * (h - 4))
                            score(*seq(1), 2 * (h - 4) + 1)
                        elif h == 12:
                            turn_max(*seq(1))
                    if head(2):
                        mix(*head(2))
                    if h == 4 and seq(-1):
                        turn_back(*seq(-1))
                    if h == 7 and seq(-1):
                        place_y(*seq(-1))
                    if h == 9 and seq(-1):
                        project(*seq(-1))

                for g in range(4):
                    place(0, 0, g)
                for u in range(12):
                    score(0, 0, u)
                turn_max(0, 0)
                pipeline(pe, step, 10)

            @block.vector
            def _(dve):
                def cast(n, p, part):
                    q = QQ[:, bass.ds(2 * n, 2), :].rearrange("p t (h d) -> p (t h) d", d=D)
                    qs = slots(QS, p)
                    q1 = QQ[:, bass.ds(2 * n, 2), :].rearrange("p t c -> p (t c)")
                    if part == 0:
                        hold(dve, placed, 4 * (n - 1))
                        nc.vector.tensor_copy(qs[:, :, 0, :], q).then_inc(qcast, 1)
                        nc.vector.tensor_copy(qs[:, :, 3:6:2, :], spread(q1, 2)).then_inc(qcast, 1)
                    if part == 1:
                        need(dve, qrest, 2 * n + 1)
                        nc.vector.tensor_copy(qs[:, :, 1, :], heads(rq[:, 0, :])).then_inc(qcast, 1)
                        nc.vector.tensor_copy(qs[:, :, 4, :], heads(rq[:, 0, :])).then_inc(qcast, 1)
                    if part == 2:
                        need(dve, qrest, 2 * n + 2)
                        nc.vector.tensor_copy(qs[:, :, 2, :], heads(rq[:, 1, :])).then_inc(qcast, 1)

                def enter(n, p, g):
                    need(dve, placed, 4 * n + g + 1)
                    need(dve, shifted, (n - 1) * HD)
                    dst = (KT if g < 2 else QT)[:, p, 4 * (g % 2):4 * (g % 2) + 4, :]
                    nc.vector.tensor_copy(dst, ptr[:, g % 2, :].rearrange("p (a c) -> p a c", a=4)).then_inc(t_in, 1)

                def maximum(n, p, u):
                    g = first_head(u)
                    need(dve, scored, 12 * n + u + 1)
                    if u % 3 == 0:
                        dst, src = nm[:, 0, g:g + 7:2], psc[:, u % 2, :].rearrange("p (k c) -> p k c", k=4)
                    else:
                        dst, src = nm[:, 1, g:g + 3:2], psc[:, u % 2, :].rearrange("p (k c) -> p k c", k=2)
                    nc.vector.tensor_reduce(dst, src, AX, ALU.max, negate=True).then_inc(maxed, 1)

                def split_max(n, p):
                    need(dve, maxed, 12 * n + 12)
                    need(dve, n_placed, n)
                    link = Link(dve, nmaxed, 5 * n)

                    def both(x):
                        return x.rearrange("p t (o h) -> p t o h", o=1).broadcast_to([P, 2, 2, HD])

                    link(nc.vector.tensor_copy(nb[:, :, :, 0:HD], both(nm[:, :, :])))
                    link(nc.vector.tensor_tensor(nr[:, :, :], nm[:, :, :], nb[:, :, 0, 0:HD], ALU.subtract))
                    link(nc.vector.tensor_copy(nb[:, :, :, HD:2 * HD], both(nr[:, :, :])))
                    link(nc.vector.tensor_tensor(nm[:, :, :], nr[:, :, :], nb[:, :, 0, HD:2 * HD], ALU.subtract))
                    link(nc.vector.tensor_copy(nb[:, :, :, 2 * HD:3 * HD], both(nm[:, :, :])))

                def enter_max(n, p):
                    need(dve, n_placed, n + 1)
                    nc.vector.tensor_copy(nT[:, p, :], ptr[:, 0, 0:SEQ]).then_inc(n_in, 1)

                def normalise(n, p):
                    need(dve, y_back, n + 1)
                    need(dve, y_placed, n)
                    both = pout[:, :].rearrange("p (t h z d) -> p t h z d", t=2, z=2, d=D)
                    nc.vector.reciprocal(inv[:, :, :, :].rearrange("p t g k -> p t (g k)"), both[:, :, :, 1, 0]
                                         ).then_inc(ainv, 1)
                    need(dve, ainv, n + 1)
                    for t in range(2):
                        f = inv[:, t, :, :].rearrange("p g (k o) -> p (g k) o", o=1).broadcast_to([P, HD, D])
                        ins = nc.vector.tensor_tensor(yt[:, t, :, :], both[:, t, :, 0, :], f, ALU.mult)
                    ins.then_inc(y_norm, 1)

                def residual(n, p):
                    need(dve, made, n + 1)
                    back.dve(dve, n, pout[:, SEQ:2 * SEQ].rearrange("p (k c) -> p k c", k=2))
                    dve.sem_inc(added, 1)

                def step(h, seq, head):
                    if h == 5 and seq(-1):
                        normalise(*seq(-1))
                    if seq(1):
                        if h < 4:
                            enter(*seq(1), h)
                        elif h < 10:
                            maximum(*seq(1), 2 * (h - 4))
                            maximum(*seq(1), 2 * (h - 4) + 1)
                        elif h == 10:
                            split_max(*seq(1))
                        elif h == 13:
                            enter_max(*seq(1))
                    if h == 11 and seq(-1):
                        residual(*seq(-1))
                    if h in (8, 10, 12) and seq(2):
                        cast(*seq(2), h // 2 - 4)

                for part in range(3):
                    cast(0, 0, part)
                for g in range(4):
                    enter(0, 0, g)
                for u in range(12):
                    maximum(0, 0, u)
                split_max(0, 0)
                for part in range(3):
                    cast(1, 1, part)
                enter_max(0, 0)
                pipeline(dve, step, 12)


def state_space(nc, env, a, tag):
    NT, NC_, T = env.NT, env.NC, env.NT * P
    DS, TAPS, EPS = 64, 4, 1e-4
    GH = NC_ // 2
    with ExitStack() as outer:
        sb, ps, sem = scope(nc, outer, tag)
        wT = sb("wT", [P, 3, DS])
        outT = sb("outT", [P, P])
        cw, cb = sb("cw", [P, TAPS]), sb("cb", [P, 1])
        bias = sb("bias", [P, 3])
        A, near, rA = sb("A", [P, 1]), sb("near", [P, 1]), sb("rA", [P, 1])
        ob, ones = sb("ob", [1, P]), sb("ones", [1, P])
        ZT, XC = sb("ZT", [P, T]), sb("XC", [P, T])
        with ExitStack() as prep:
            psb, _, psem = scope(nc, prep, tag + "p")
            wd = psb("wd", [DS, P])
            wbc = psb("wbc", [DS, 2, 2, P])
            wm = psb("wm", [DS, 2, P])
            ow = psb("ow", [P, 2, DS])
            bb = psb("bb", [P, 2, 2])
            t = psb("t", [P, 4])
            pw, pb = a["in_proj_w"], a["in_proj_b"]
            loads = [(wd[:, :], pw[0:DS, :]),
                     (wbc[:, :, :, :], pw[DS:5 * DS, :].rearrange("(z n g) c -> n z g c", z=2, g=2)),
                     (cw[:, :], a["conv_w"].rearrange("c o k -> c (o k)")),
                     (cb[:, :], a["conv_b"].rearrange("(p o) -> p o", o=1)),
                     (ob[:, :], a["out_proj_b"].rearrange("(o d) -> o d", o=1))]
            for half in range(2):
                r_ = slice(half * DS, (half + 1) * DS)
                loads += [(bias[r_, 0:1], pb[0:DS].rearrange("(p o) -> p o", o=1)),
                          (bb[r_, :, :], pb[DS:5 * DS].rearrange("(z n g) -> n z g", z=2, g=2)),
                          (A[r_, :], a["A_log"].rearrange("(p o) -> p o", o=1)),
                          (ow[:, half, :], a["out_proj_w"])]
            row_scales(nc, env, tag + "sc", None, loads)
            vec, ex = psem("vec"), psem("ex")
            with nc.Block() as block:
                @block.scalar
                def _(act):
                    nc.scalar.activation(t[:, 0:1], A[:, :], ACT.Exp).then_inc(ex, 1)

                @block.vector
                def _(dve):
                    link = Link(dve, vec)
                    link(nc.vector.memset(ones[:, :], 1.0))
                    for z in range(2):
                        link(nc.vector.tensor_tensor(wm[:, z, :], wbc[:, z, 0, :], wbc[:, z, 1, :], ALU.add))
                        link(nc.vector.tensor_scalar(wm[:, z, :], wm[:, z, :], 0.5, None, ALU.mult))
                        link(nc.vector.tensor_tensor(bias[:, 1 + z:2 + z], bb[:, z, 0:1], bb[:, z, 1:2], ALU.add))
                        link(nc.vector.tensor_scalar(bias[:, 1 + z:2 + z], bias[:, 1 + z:2 + z], 0.5, None, ALU.mult))
                    dve.wait_ge(ex, 1)
                    link(nc.vector.tensor_scalar(near[:, :], t[:, 0:1], EPS, None, ALU.is_lt))
                    link(nc.vector.tensor_scalar(A[:, :], t[:, 0:1], -1.0, None, ALU.mult))
                    link(nc.vector.tensor_tensor(t[:, 1:2], A[:, :], near[:, :], ALU.subtract))
                    link(nc.vector.reciprocal(t[:, 2:3], t[:, 1:2]))
                    link(nc.vector.tensor_scalar(t[:, 3:4], near[:, :], -1.0, 1.0, ALU.mult, ALU.add))
                    link(nc.vector.tensor_tensor(rA[:, :], t[:, 2:3], t[:, 3:4], ALU.mult))
            turn_weights(nc, tag + "t", env.ident, [(wd[:, :], wT[:, 0, :])]
                         + [(wm[:, z, :], wT[:, 1 + z, :]) for z in range(2)]
                         + [(ow[:, :, :].rearrange("p a n -> p (a n)"), outT[:, :])])
        front_pass(nc, env, tag + "f", False, ZT[:, :])
        with ExitStack() as ctx:
            sb, ps, sem = scope(nc, ctx, tag + "c")
            vec = sem("vec")
            block = ctx.enter_context(nc.Block())
            L = SEQ - 1

            @block.vector
            def _(dve):
                link = Link(dve, vec)
                z = ZT[:, :].rearrange("p (s t) -> p s t", t=SEQ)
                x = XC[:, :].rearrange("p (s t) -> p s t", t=SEQ)
                link(nc.vector.memset(x[:, :, L:SEQ], 0.0))
                link(nc.vector.tensor_scalar(x[:, :, 0:L], z[:, :, 0:L], cw[:, 1:2], cb[:, 0:1], ALU.mult, ALU.add))
                for k, lo, hi in ((0, 1, L), (2, 0, L), (3, 0, L - 1)):
                    link(nc.vector.scalar_tensor_tensor(x[:, :, lo:hi], z[:, :, lo + k - 1:hi + k - 1], cw[:, k:k + 1],
                                                        x[:, :, lo:hi], ALU.mult, ALU.add))
        with ExitStack() as ctx:
            sb, ps, sem = scope(nc, ctx, tag + "s")
            d_, l_, e_, ab_ = (sb(k, [P, 2, CH]) for k in ("d", "l", "e", "ab"))
            w, c, q, h_, y = (sb(k, [P, CH]) for k in ("w", "c", "q", "h", "y"))
            pp, po = ps("pp", [P, 2, 3, 512]), ps("po", [P, 2, 512])
            made, acts, vec, outs, added = sem("made"), sem("acts"), sem("vec"), sem("outs"), sem("added")
            back = Back(nc, env, sb, ps, sem)
            block = ctx.enter_context(nc.Block())
            ASTEPS, STEPS = 5, 14

            @block.tensor
            def _(pe):
                def project(g):
                    need(pe, vec, STEPS * (g - 1))
                    for z in range(3):
                        for half in range(2):
                            n = g + half * GH
                            ins = nc.tensor.matmul(pp[half * DS:(half + 1) * DS, g % 2, z, :], wT[:, z, :],
                                                   XC[:, n * CH:(n + 1) * CH], start=True, stop=True)
                    ins.then_inc(made, 1)

                project(0)
                for g in range(GH):
                    if g + 1 < GH:
                        project(g + 1)
                    need(pe, vec, STEPS * (g + 1))
                    need(pe, added, 2 * g)
                    for half in range(2):
                        r_ = slice(half * DS, (half + 1) * DS)
                        for k in range(TPC):
                            o = po[:, half, k * P:(k + 1) * P]
                            nc.tensor.matmul(o, ones[:, :], ob[:, :], start=True, stop=False)
                            ins = nc.tensor.matmul(o, y[r_, k * P:(k + 1) * P], outT[r_, :], start=False, stop=True)
                        ins.then_inc(outs, 1)

            @block.scalar
            def _(act):
                def logs(g):
                    d, l, e = d_[:, g % 2, :], l_[:, g % 2, :], e_[:, g % 2, :]
                    link = Link(act, acts, ASTEPS * g)
                    need(act, made, g + 1)
                    need(act, vec, STEPS * (g - 1))
                    link(nc.scalar.activation(d, pp[:, g % 2, 0, :], ACT.Identity, bias=bias[:, 0:1]))
                    link(nc.scalar.activation(l, d, ACT.Abs))
                    link(nc.scalar.activation(e, l, ACT.Exp, scale=-1.0))
                    link(nc.scalar.activation(l, e, ACT.Ln, bias=1.0))

                logs(0)
                for g in range(GH):
                    need(act, vec, STEPS * g + 4)
                    nc.scalar.activation(ab_[:, g % 2, :], d_[:, g % 2, :], ACT.Exp, scale=A[:, 0:1]).then_inc(acts, 1)
                    if g + 1 < GH:
                        logs(g + 1)

            @block.vector
            def _(dve):
                def recur(g):
                    d, l, e, ab = (x[:, g % 2, :] for x in (d_, l_, e_, ab_))
                    link = Link(dve, vec, STEPS * g)
                    need(dve, acts, ASTEPS * g + 3)
                    link(nc.vector.tensor_scalar(w[:, :], e, 1.0, -1.0, ALU.add, ALU.add))
                    link(nc.vector.tensor_tensor(c[:, :], e, w[:, :], ALU.subtract))
                    need(dve, acts, ASTEPS * g + 4)
                    link(nc.vector.scalar_tensor_tensor(l, d, 0.0, l, ALU.max, ALU.add))
                    link(nc.vector.tensor_tensor(d, l, c[:, :], ALU.add))
                    link(nc.vector.tensor_scalar(w[:, :], d, A[:, 0:1], None, ALU.mult))
                    link(nc.vector.tensor_scalar(q[:, :], w[:, :], 1.0 / 6.0, 0.5, ALU.mult, ALU.add))
                    link(nc.vector.tensor_tensor(c[:, :], q[:, :], w[:, :], ALU.mult))
                    link(nc.vector.tensor_scalar(q[:, :], c[:, :], 1.0, near[:, 0:1], ALU.add, ALU.mult))
                    need(dve, acts, ASTEPS * g + 5)
                    link(nc.vector.tensor_scalar(w[:, :], ab, 1.0, rA[:, 0:1], ALU.subtract, ALU.mult))
                    link(nc.vector.tensor_tensor(c[:, :], w[:, :], q[:, :], ALU.add))
                    link(nc.vector.scalar_tensor_tensor(q[:, :], pp[:, g % 2, 1, :], bias[:, 1:2], c[:, :], ALU.add, ALU.mult))
                    for s in range(SPC):
                        cols = slice(s * SEQ, (s + 1) * SEQ)
                        link(nc.vector.tensor_tensor_scan(h_[:, cols], ab[:, cols], q[:, cols], 0.0, ALU.mult, ALU.add))
                    need(dve, outs, 2 * g)
                    link(nc.vector.scalar_tensor_tensor(y[:, :], pp[:, g % 2, 2, :], bias[:, 2:3], h_[:, :], ALU.add, ALU.mult))

                def residual(g):
                    for half in range(2):
                        need(dve, outs, 2 * g + half + 1)
                        back.dve(dve, g + half * GH, po[:, half, :].rearrange("p (k c) -> p k c", k=TPC),
                                 turn=2 * g + half)
                        dve.sem_inc(added, 1)

                for g in range(GH):
                    recur(g)
                    if g >= 1:
                        residual(g - 1)
                residual(GH - 1)


def store(nc, env, out):
    with ExitStack() as ctx:
        stored = ctx.enter_context(nc.semaphore("stored"))
        block = ctx.enter_context(nc.Block())

        @block.sync
        def _(sp):
            sp.dma_start(out.rearrange("b (s p) c -> p (b s) c", p=P), env.X[:, :, :]).then_inc(stored, 16)
            sp.wait_ge(stored, 16)


STAGES = ("mamba", "experts", "attention", "experts", "rotary", "product_keys", "state_space", "product_keys")


def hybrid(nc, args, out, stages=STAGES):
    Lent.handles = []
    env = Env()
    env.product_key_weights = None
    nb = args["L0_attn_a_x"].shape[0]
    env.NT = nb * SEQ // P
    env.NC = env.NT // TPC
    with ExitStack() as ctx:
        env.ctx = ctx
        sb, _, _ = scope(nc, ctx, "g")
        env.X = sb("X", [P, env.NT, P])
        env.stats = sb("stats", [P, env.NT, 6])
        env.mean, env.rstd = sb("mean", [P, env.NT]), sb("rstd", [P, env.NT])
        env.keep, env.shift = sb("keep", [P, env.NT]), sb("shift", [P, env.NT])
        env.root, env.rnorm = sb("root", [P, env.NT]), sb("rnorm", [P, env.NT])
        env.ident = sb("ident", [P, P])
        env.sel = sb("sel", [96, 32, P], BF16)
        env.ranks = sb("ranks", [P, 2, P], BF16)
        env.steps = sb("steps", [P, 2, 40])
        env.sorted_rows = nc.dram_tensor("sorted_rows", ((env.NT + 8) * P, P), F32, kind="Internal").ap()
        env.sorted_out = nc.dram_tensor("sorted_out", ((env.NT + 8) * P, P), F32, kind="Internal").ap()
        env.sorted_rows_written = False
        env.firsts = sb("firsts", [P, 1, 8])
        env.identb = sb("identb", [P, P], BF16)
        env.causal = sb("causal", [P, P], BF16)
        env.causalT = sb("causalT", [P, P], BF16)
        launch(nc, env, args["L0_attn_a_x"], [
            (env.ident[:, :], args["c_ident"]), (env.identb[:, :], args["c_identb"]),
            (env.causal[:, :], args["c_causal"]), (env.causalT[:, :], args["c_causalT"]),
            (env.ranks[:, :, :], args["c_ranks"]), (env.steps[:, :, :], args["c_steps"]),
            (env.firsts[:, :, :], args["c_firsts"]), (env.sel[:, :, :], args["c_sel"])])

        def of(prefix):
            return {k[len(prefix):]: v for k, v in args.items() if k.startswith(prefix)}

        for i, s in enumerate(stages):
            if s == "attention":
                attention(nc, env, of("L0_attn_b_"), f"b{i}")
            if s == "rotary":
                rotary(nc, env, dict(of("L1_attn_a_"), rope=args["c_rope"], three=args["c_three"]), f"r{i}")
            if s == "state_space":
                state_space(nc, env, of("L1_attn_b_"), f"s{i}")
            if s == "product_keys":
                product_keys(nc, env, of("L1_ffn_"), f"k{i}")
            if s == "experts":
                experts(nc, env, of("L0_ffn_"), f"e{i}")
            if s == "mamba":
                mamba(nc, env, of("L0_attn_a_"))
            sweep(nc)
        store(nc, env, out)


def shape_constants():
    bf = mybir.dt.np(BF16)
    sel = np.zeros((96, 32, P), bf)
    for part in range(3):
        for s in range(32):
            sel[32 * part + s, s, :] = 1
    ranks = np.ones((P, 2, P), bf)
    ranks[:, 0, :] = np.triu(np.ones((P, P)), 1).astype(bf)
    steps = np.tile(np.stack([np.arange(40) * P, np.arange(40)]).astype(np.float32), (P, 1, 1))
    firsts = np.tile(np.arange(8, 0, -1, dtype=np.float32), (P, 1, 1))
    causal = np.where(np.arange(P)[None, :] > np.arange(P)[:, None], np.float32(-1e30), np.float32(0)).astype(bf)
    three = np.zeros((P, 16, P), bf)
    for half in range(2):
        for part in range(3):
            for h in range(16):
                three[64 * half + 16 * part + h, h, :] = 1
    inv = (np.float32(1.0) / np.power(np.float32(10000.0), np.arange(0, 8, 2, dtype=np.float32) / np.float32(8)))
    freqs = (np.arange(SEQ, dtype=np.float32)[:, None] * inv[None, :].astype(np.float32)).astype(np.float32)
    cos, sin = np.cos(freqs), np.sin(freqs)
    one = np.stack([np.concatenate([cos, cos], 1), np.concatenate([-sin, sin], 1)], 1)
    rope = np.tile(one, (1, 1, 16)).reshape(2, P, 2, P).transpose(1, 0, 2, 3)
    return {
        "c_three": three,
        "c_rope": np.ascontiguousarray(rope.astype(np.float32)),
        "c_causalT": np.ascontiguousarray(causal.T),
        "c_identb": np.eye(P, dtype=bf),
        "c_causal": causal,
        "c_ranks": ranks,
        "c_steps": steps,
        "c_firsts": firsts,
        "c_ident": np.eye(P, dtype=np.float32),
        "c_sel": sel,
    }


def hybrid_layers_kernel(nc, *operands):
    hybrid(nc, dict(zip(_INS + _TABLES, operands[:-1])), operands[-1])


_INS = ['L0_attn_a_x', 'L0_attn_a_norm_g', 'L0_attn_a_norm_b', 'L0_attn_a_in_w', 'L0_attn_a_conv_w',
        'L0_attn_a_conv_b', 'L0_attn_a_xproj_w', 'L0_attn_a_dt_w', 'L0_attn_a_dt_b', 'L0_attn_a_A_log',
        'L0_attn_a_D', 'L0_attn_a_out_w', 'L0_attn_b_gamma', 'L0_attn_b_w_qkv', 'L0_attn_b_w_out',
        'L0_ffn_centroids', 'L0_ffn_gamma', 'L0_ffn_beta', 'L0_ffn_W1', 'L0_ffn_b1', 'L0_ffn_W2',
        'L0_ffn_b2', 'L1_attn_a_W_kqv', 'L1_attn_a_W_proj', 'L1_attn_a_q_norm_w', 'L1_attn_a_k_norm_w',
        'L1_attn_b_conv_w', 'L1_attn_b_conv_b', 'L1_attn_b_in_proj_w', 'L1_attn_b_in_proj_b',
        'L1_attn_b_A_log', 'L1_attn_b_out_proj_w', 'L1_attn_b_out_proj_b', 'L1_ffn_w_q', 'L1_ffn_keys',
        'L1_ffn_expert_down', 'L1_ffn_expert_up', 'L1_ffn_norm_w']
_TABLES = ['c_ident', 'c_identb', 'c_sel', 'c_ranks', 'c_steps', 'c_three', 'c_firsts', 'c_causal', 'c_causalT', 'c_rope']
_OUTS = [((16, 256, 128), 'float32')]


def kernel(**inputs):
    import numpy as _np
    import concourse.bacc as _bacc
    from concourse import mybir as _mybir
    from concourse.bass_utils import run_bass_kernel_spmd as _run

    nc = _bacc.Bacc("TRN2", target_bir_lowering=False, num_devices=1)
    tables = shape_constants()
    arrays, args = {}, []
    for name in _INS + _TABLES:
        a = _np.ascontiguousarray(inputs[name] if name in inputs else tables[name])
        arrays[f"in_{name}_dram"] = a
        args.append(nc.dram_tensor(f"in_{name}_dram", a.shape, _mybir.dt.from_np(a.dtype), kind="ExternalInput").ap())
    for i, (shape, dtype) in enumerate(_OUTS):
        dt = _mybir.dt.from_np(_np.dtype(dtype))
        args.append(nc.dram_tensor(f"out_{i}_dram", shape, dt, kind="ExternalOutput").ap())
    hybrid_layers_kernel(nc, *args)
    r = _run(nc, [arrays], core_ids=[0])
    got = tuple(r.results[0][f"out_{i}_dram"] for i in range(len(_OUTS)))
    return got[0]
```
